# Optimizing a Trainium2 kernel written in Bass

```python
import numpy as np
import jax
import jax.numpy as jnp

def _softmax(x, axis=-1):
    return jax.nn.softmax(x, axis=axis)

def _gelu(x):
    return jax.nn.gelu(x, approximate=True)

def _silu(x):
    return jax.nn.silu(x)

def _sigmoid(x):
    return jax.nn.sigmoid(x)

def _layernorm(x, axis=-1, eps=1e-05):
    m = jnp.mean(x, axis=axis, keepdims=True)
    v = jnp.var(x, axis=axis, keepdims=True)
    return (x - m) / jnp.sqrt(v + eps)

def _scatter_add(tgt, idx, src, axis=0):
    return tgt.at[idx].add(src)

def _segment_sum(src, seg, n):
    return jax.ops.segment_sum(src, seg, n)
kernel_name = 'mk_adaln_d2_jaxref_r4_410e2c'

def setup_inputs(seed: int=0):
    np.random.seed(seed)
    _w = jnp.asarray

    def _L0_attn_setup():
        import jax, jax.numpy as jnp
        import numpy as np
        B, T, E, H, L = (8, 1024, 256, 16, 64)
        HD = E // H
        key = jax.random.key(seed)
        ks = jax.random.split(key, 5)
        s = 1.0 / np.sqrt(E).astype(np.float32)
        x = jax.random.normal(ks[0], (B, T, E), dtype=jnp.float32)
        W_qkv = jax.random.normal(ks[1], (3 * E, E), dtype=jnp.float32) * s
        b_qkv = jnp.zeros((3 * E,), dtype=jnp.float32)
        W_out = jax.random.normal(ks[2], (E, E), dtype=jnp.float32) * s
        b_out = jnp.zeros((E,), dtype=jnp.float32)
        return {'x': x, 'W_qkv': W_qkv, 'b_qkv': b_qkv, 'W_out': W_out, 'b_out': b_out}
    _L0_attn_in = _L0_attn_setup()

    def _L0_ffn_setup():
        import jax, jax.numpy as jnp
        import numpy as np
        B, S, DIM = (4, 1024, 256)
        BASE_COUPLING = 0.1
        NUM_CYCLES = 3

        def _gelu(x):
            return jax.nn.gelu(x, approximate=False)

        def _coupling_net(h, w1, b1, w2, b2, w3, b3, w4, b4):
            h = _gelu(h @ w1 + b1)
            h = _gelu(h @ w2 + b2)
            h = _gelu(h @ w3 + b3)
            return jax.nn.sigmoid(h @ w4 + b4)

        def _global_net(h, w1, b1, w2, b2, w3, b3):
            h = _gelu(h @ w1 + b1)
            h = _gelu(h @ w2 + b2)
            return jax.nn.sigmoid(h @ w3 + b3)

        def _twist(x):
            o_r, o_i, p_r, p_i = jnp.split(x, 4, axis=-1)
            return jnp.concatenate([p_r, -p_i, -o_r, o_i], axis=-1)
        key = jax.random.key(seed)
        ks = jax.random.split(key, 9)
        d = DIM

        def w(k, fan_in, fan_out):
            return jax.random.normal(k, (fan_in, fan_out), dtype=jnp.float32) / np.sqrt(fan_in).astype(np.float32)
        inp = {'x': jax.random.normal(ks[0], (B, S, d), dtype=jnp.float32)}
        cn_dims = [(d, d), (d, d // 2), (d // 2, d // 4), (d // 4, 1)]
        for i, (a, b) in enumerate(cn_dims):
            inp[f'cn_w{i + 1}'] = w(ks[1 + i], a, b)
            inp[f'cn_b{i + 1}'] = jnp.zeros((b,), dtype=jnp.float32)
        gc_dims = [(d, d // 2), (d // 2, d // 4), (d // 4, 1)]
        for i, (a, b) in enumerate(gc_dims):
            inp[f'gc_w{i + 1}'] = w(ks[5 + i], a, b)
            inp[f'gc_b{i + 1}'] = jnp.zeros((b,), dtype=jnp.float32)
        inp['adaptive_range'] = jnp.full((1,), 0.2, dtype=jnp.float32)
        return inp
    _L0_ffn_in = _L0_ffn_setup()
    _L0_c = _w((lambda *s: np.random.randn(*s).astype(np.float32) * 0.05)(8, 256))
    _L0_wmod = _w((lambda *s: np.random.randn(*s).astype(np.float32) * 0.05)(256, 6 * 256) * 256 ** (-0.5))

    def _L1_attn_setup():
        import jax, jax.numpy as jnp
        import numpy as np
        HEADS = 8
        DIM_HEAD = 64
        SCALE = DIM_HEAD ** (-0.5)
        key = jax.random.key(seed)
        k1, k2, k3 = jax.random.split(key, 3)
        B, N, D = (2, 512, 256)
        dim_inner = HEADS * DIM_HEAD
        x = jax.random.normal(k1, (B, N, D), dtype=jnp.float32)
        W_qkv = jax.random.normal(k2, (6 * dim_inner, D), dtype=jnp.float32) * 0.02
        W_out = jax.random.normal(k3, (D, dim_inner), dtype=jnp.float32) * 0.02
        return {'x': x, 'W_qkv': W_qkv, 'W_out': W_out}
    _L1_attn_in = _L1_attn_setup()

    def _L1_ffn_setup():
        import jax, jax.numpy as jnp
        import numpy as np
        NUM_EXPERTS = 8
        EXPERT_CAPACITY = 2.0
        DIM = 256
        HIDDEN_DIM = 1024
        key = jax.random.key(seed)
        k_x, k_g, k_w1, k_w2 = jax.random.split(key, 4)
        n, t, d, f, e = (8, 256, DIM, HIDDEN_DIM, NUM_EXPERTS)
        x = jax.random.normal(k_x, (n, t, d), dtype=jnp.float32)
        gate_w = jax.random.normal(k_g, (e, d), dtype=jnp.float32) * 0.02
        w1 = jax.random.normal(k_w1, (e, d, f), dtype=jnp.float32) * 0.02
        w2 = jax.random.normal(k_w2, (e, f, d), dtype=jnp.float32) * 0.02
        return {'x': x, 'gate_w': gate_w, 'w1': w1, 'w2': w2}
    _L1_ffn_in = _L1_ffn_setup()
    _L1_c = _w((lambda *s: np.random.randn(*s).astype(np.float32) * 0.05)(8, 256))
    _L1_wmod = _w((lambda *s: np.random.randn(*s).astype(np.float32) * 0.05)(256, 6 * 256) * 256 ** (-0.5))
    _d = {'L0_attn_x': _L0_attn_in['x'], 'L0_attn_W_qkv': _L0_attn_in['W_qkv'], 'L0_attn_b_qkv': _L0_attn_in['b_qkv'], 'L0_attn_W_out': _L0_attn_in['W_out'], 'L0_attn_b_out': _L0_attn_in['b_out'], 'L0_ffn_cn_w1': _L0_ffn_in['cn_w1'], 'L0_ffn_cn_b1': _L0_ffn_in['cn_b1'], 'L0_ffn_cn_w2': _L0_ffn_in['cn_w2'], 'L0_ffn_cn_b2': _L0_ffn_in['cn_b2'], 'L0_ffn_cn_w3': _L0_ffn_in['cn_w3'], 'L0_ffn_cn_b3': _L0_ffn_in['cn_b3'], 'L0_ffn_cn_w4': _L0_ffn_in['cn_w4'], 'L0_ffn_cn_b4': _L0_ffn_in['cn_b4'], 'L0_ffn_gc_w1': _L0_ffn_in['gc_w1'], 'L0_ffn_gc_b1': _L0_ffn_in['gc_b1'], 'L0_ffn_gc_w2': _L0_ffn_in['gc_w2'], 'L0_ffn_gc_b2': _L0_ffn_in['gc_b2'], 'L0_ffn_gc_w3': _L0_ffn_in['gc_w3'], 'L0_ffn_gc_b3': _L0_ffn_in['gc_b3'], 'L0_ffn_adaptive_range': _L0_ffn_in['adaptive_range'], 'L0_c': _L0_c, 'L0_wmod': _L0_wmod, 'L1_attn_W_qkv': _L1_attn_in['W_qkv'], 'L1_attn_W_out': _L1_attn_in['W_out'], 'L1_ffn_gate_w': _L1_ffn_in['gate_w'], 'L1_ffn_w1': _L1_ffn_in['w1'], 'L1_ffn_w2': _L1_ffn_in['w2'], 'L1_c': _L1_c, 'L1_wmod': _L1_wmod}
    _x0 = _d['L0_attn_x']
    _d['L0_attn_x'] = jax.random.normal(jax.random.fold_in(jax.random.key(seed), 1), (8, 512, 256), dtype=_x0.dtype)
    del _x0
    return _d

def reference(L0_attn_x, L0_attn_W_qkv, L0_attn_b_qkv, L0_attn_W_out, L0_attn_b_out, L0_ffn_cn_w1, L0_ffn_cn_b1, L0_ffn_cn_w2, L0_ffn_cn_b2, L0_ffn_cn_w3, L0_ffn_cn_b3, L0_ffn_cn_w4, L0_ffn_cn_b4, L0_ffn_gc_w1, L0_ffn_gc_b1, L0_ffn_gc_w2, L0_ffn_gc_b2, L0_ffn_gc_w3, L0_ffn_gc_b3, L0_ffn_adaptive_range, L0_c, L0_wmod, L1_attn_W_qkv, L1_attn_W_out, L1_ffn_gate_w, L1_ffn_w1, L1_ffn_w2, L1_c, L1_wmod):

    def _L0_attn_ref(x, W_qkv, b_qkv, W_out, b_out):
        import jax, jax.numpy as jnp
        import numpy as np
        B, T, E, H, L = (8, 1024, 256, 16, 64)
        HD = E // H
        b, t, e = x.shape
        scaling = HD ** (-0.5)
        qkv = x @ W_qkv.T + b_qkv
        q, k, v = jnp.split(qkv, 3, axis=-1)
        q = q * scaling

        def to_blocks(a):
            return a.reshape(b, t, H, HD).transpose(0, 2, 1, 3).reshape(b, H, t // L, L, HD)
        qb, kb, vb = (to_blocks(q), to_blocks(k), to_blocks(v))
        attn = jax.nn.softmax(jnp.einsum('bhnld,bhnmd->bhnlm', qb, kb), axis=-1)
        out = jnp.einsum('bhnlm,bhnmd->bhnld', attn, vb)
        out = out.reshape(b, H, t, HD).transpose(0, 2, 1, 3).reshape(b, t, e)
        return out @ W_out.T + b_out

    def _L0_ffn_ref(x, cn_w1, cn_b1, cn_w2, cn_b2, cn_w3, cn_b3, cn_w4, cn_b4, gc_w1, gc_b1, gc_w2, gc_b2, gc_w3, gc_b3, adaptive_range):
        import jax, jax.numpy as jnp
        import numpy as np
        B, S, DIM = (4, 1024, 256)
        BASE_COUPLING = 0.1
        NUM_CYCLES = 3

        def _gelu(x):
            return jax.nn.gelu(x, approximate=False)

        def _coupling_net(h, w1, b1, w2, b2, w3, b3, w4, b4):
            h = _gelu(h @ w1 + b1)
            h = _gelu(h @ w2 + b2)
            h = _gelu(h @ w3 + b3)
            return jax.nn.sigmoid(h @ w4 + b4)

        def _global_net(h, w1, b1, w2, b2, w3, b3):
            h = _gelu(h @ w1 + b1)
            h = _gelu(h @ w2 + b2)
            return jax.nn.sigmoid(h @ w3 + b3)

        def _twist(x):
            o_r, o_i, p_r, p_i = jnp.split(x, 4, axis=-1)
            return jnp.concatenate([p_r, -p_i, -o_r, o_i], axis=-1)
        global_context = x.mean(axis=1, keepdims=True)
        gf = _global_net(global_context, gc_w1, gc_b1, gc_w2, gc_b2, gc_w3, gc_b3)
        out = x
        for _ in range(NUM_CYCLES):
            tf = _coupling_net(out, cn_w1, cn_b1, cn_w2, cn_b2, cn_w3, cn_b3, cn_w4, cn_b4)
            combined = 0.7 * gf + 0.3 * tf
            coupling = BASE_COUPLING + adaptive_range * (combined - 0.5) * 2.0
            out = out + coupling * _twist(out)
        return out

    def _L1_attn_ref(x, W_qkv, W_out):
        import jax, jax.numpy as jnp
        import numpy as np
        HEADS = 8
        DIM_HEAD = 64
        SCALE = DIM_HEAD ** (-0.5)
        B, N, D = x.shape
        h, d = (HEADS, DIM_HEAD)
        qkvs = x @ W_qkv.T
        qkvs = qkvs.reshape(B, N, 6, h, d)
        qkvs = jnp.transpose(qkvs, (2, 0, 3, 1, 4))
        qu, ku, vu, qc, kc, vc = qkvs
        qu_s = qu * SCALE
        qc_s = qc * SCALE
        neg = -jnp.finfo(x.dtype).max
        causal_mask = jnp.triu(jnp.ones((N, N), dtype=bool), 1)
        term1 = jnp.einsum('bhid,bhjd->bhij', qc_s, vu)
        term1 = jnp.where(causal_mask, 0.0, term1)
        lookahead = jax.nn.sigmoid(jnp.einsum('bhid,bhjd->bhij', qu_s, ku))
        lookahead = jnp.where(causal_mask, lookahead, 0.0)
        Su = jnp.einsum('bhij,bhkj->bhik', term1, lookahead)
        Sc = jnp.einsum('bhid,bhjd->bhij', qc_s, kc)
        scores = Sc - jax.nn.silu(Su)
        scores = jnp.where(causal_mask, neg, scores)
        attn = jax.nn.softmax(scores, axis=-1)
        out = jnp.einsum('bhij,bhjd->bhid', attn, vc)
        out = jnp.transpose(out, (0, 2, 1, 3)).reshape(B, N, h * d)
        return out @ W_out.T

    def _L1_ffn_ref(x, gate_w, w1, w2):
        import jax, jax.numpy as jnp
        import numpy as np
        NUM_EXPERTS = 8
        EXPERT_CAPACITY = 2.0
        DIM = 256
        HIDDEN_DIM = 1024
        n, t, d = x.shape
        e = gate_w.shape[0]
        k = int(EXPERT_CAPACITY * t / e)
        scores = jnp.einsum('ntd,ed->nte', x, gate_w)
        probs = jax.nn.softmax(scores, axis=-1)
        g, m = jax.lax.top_k(probs.transpose(0, 2, 1), k)
        batch_idx = jnp.arange(n)[:, None, None]
        xin = x[batch_idx, m]
        h = jnp.einsum('nekd,edf->nekf', xin, w1)
        h = jax.nn.gelu(h, approximate=False)
        h = jnp.einsum('nekf,efd->nekd', h, w2)
        out_tok = g[..., None] * h
        out = jnp.zeros((n, t, d), dtype=x.dtype).at[batch_idx, m].add(out_tok)
        return out
    x = L0_attn_x
    mod = (_silu(L0_c) @ L0_wmod).reshape(L0_c.shape[0], 6, 1, -1)
    sa, ca, ga, sb, cb, gb = (mod[:, 0], mod[:, 1], mod[:, 2], mod[:, 3], mod[:, 4], mod[:, 5])
    ga = (2 * (ga >= 0) - 1) * jnp.maximum(jnp.abs(ga), 0.25)
    gb = (2 * (gb >= 0) - 1) * jnp.maximum(jnp.abs(gb), 0.25)
    h = _layernorm(x, axis=-1) * (1 + ca) + sa
    x = x + ga * _L0_attn_ref(h, L0_attn_W_qkv, L0_attn_b_qkv, L0_attn_W_out, L0_attn_b_out)
    h = _layernorm(x, axis=-1) * (1 + cb) + sb
    x = x + gb * _L0_ffn_ref(h, L0_ffn_cn_w1, L0_ffn_cn_b1, L0_ffn_cn_w2, L0_ffn_cn_b2, L0_ffn_cn_w3, L0_ffn_cn_b3, L0_ffn_cn_w4, L0_ffn_cn_b4, L0_ffn_gc_w1, L0_ffn_gc_b1, L0_ffn_gc_w2, L0_ffn_gc_b2, L0_ffn_gc_w3, L0_ffn_gc_b3, L0_ffn_adaptive_range)
    mod = (_silu(L1_c) @ L1_wmod).reshape(L1_c.shape[0], 6, 1, -1)
    sa, ca, ga, sb, cb, gb = (mod[:, 0], mod[:, 1], mod[:, 2], mod[:, 3], mod[:, 4], mod[:, 5])
    ga = (2 * (ga >= 0) - 1) * jnp.maximum(jnp.abs(ga), 0.25)
    gb = (2 * (gb >= 0) - 1) * jnp.maximum(jnp.abs(gb), 0.25)
    h = _layernorm(x, axis=-1) * (1 + ca) + sa
    x = x + ga * _L1_attn_ref(h, L1_attn_W_qkv, L1_attn_W_out)
    h = _layernorm(x, axis=-1) * (1 + cb) + sb
    x = x + gb * _L1_ffn_ref(h, L1_ffn_gate_w, L1_ffn_w1, L1_ffn_w2)
    return x

_drawn_inputs = setup_inputs


def setup_inputs(seed=0):
    import zlib

    import numpy as np

    out = dict(_drawn_inputs(seed))
    spreads = {'L0_attn_b_qkv': (0.0, 0.324),
     'L0_attn_b_out': (0.0, 0.34),
     'L0_ffn_cn_b1': (0.0, 0.8),
     'L0_ffn_cn_b2': (0.0, 0.8),
     'L0_ffn_cn_b3': (0.0, 0.8),
     'L0_ffn_gc_b1': (0.0, 0.8),
     'L0_ffn_gc_b2': (0.0, 0.8)}
    factors = {'L0_ffn_cn_w1': 8.0,
     'L0_ffn_cn_w2': 8.0,
     'L0_ffn_cn_w3': 8.0,
     'L0_ffn_cn_w4': 8.0,
     'L0_ffn_gc_w1': 8.0,
     'L0_ffn_gc_w2': 8.0,
     'L0_ffn_gc_w3': 8.0,
     'L1_attn_W_qkv': 8.0,
     'L1_attn_W_out': 8.0,
     'L1_ffn_gate_w': 8.0,
     'L1_ffn_w1': 8.0,
     'L1_ffn_w2': 8.0,
     'L1_c': 6.952,
     'L1_wmod': 6.941}
    for name, (base, spread) in spreads.items():
        noise = np.random.default_rng([zlib.crc32(name.encode()), seed]).standard_normal(out[name].shape)
        drawn = base * np.exp(spread * noise) if base else spread * noise
        out[name] = jnp.asarray(drawn.astype(out[name].dtype))
    for name, factor in factors.items():
        out[name] = (out[name] * factor).astype(out[name].dtype)
    return out
```

```python
from contextlib import ExitStack

import concourse.bass as bass
from concourse import mybir

F32 = mybir.dt.float32
BF16 = mybir.dt.bfloat16
I32 = mybir.dt.int32
ALU = mybir.AluOpType
ACT = mybir.ActivationFunctionType
AX = mybir.AxisListType

P = 128
B, T, D = 8, 512, 256
NT = T // P
KC = D // P
EPS = 1e-5
H0, HD0, LB = 16, 16, 64
NBLK = T // LB
NR = P // 32
H1, HD1 = 8, 64
NHP = H1 // 2
CH1 = H1 * HD1
E, F = 8, 1024
FC = F // P
CAP = 2 * T // E
NEG = -1e30
CYCLES = 3
SA, CA, GA, SB, CB, GB = (KC * i for i in range(6))
NMOD = 6 * KC


class Line:

    def __init__(self, prog, eng, name):
        self.prog, self.eng, self.name = prog, eng, name
        self.sem = prog.nc.alloc_semaphore(name + "_done")
        self.restart()

    def restart(self):
        self.n, self.seen = 0, {}

    def wait(self, *marks):
        for m in marks:
            if m is None or m[2] != self.prog.epoch:
                continue
            sem, value, _ = m
            if self.seen.get(sem.name, 0) < value:
                self.eng.wait_ge(sem, value)
                self.seen[sem.name] = value

    def mark(self, instruction):
        self.n += 1
        instruction.then_inc(self.sem, 1)
        return (self.sem, self.n, self.prog.epoch)


class DmaSem:

    def __init__(self, prog, name):
        self.prog, self.n = prog, 0
        self.sem = prog.nc.alloc_semaphore(name)
        prog.dma_sems.append(self)

    def mark(self, instruction):
        self.n += 16
        instruction.then_inc(self.sem, 16)
        return (self.sem, self.n, self.prog.epoch)

    def last(self):
        return (self.sem, self.n, self.prog.epoch) if self.n else None


class Program:
    def __init__(self, nc):
        self.nc, self.epoch, self.dma_sems = nc, 0, []
        self.pe = Line(self, nc.tensor, "pe")
        self.act = Line(self, nc.scalar, "act")
        self.dve = Line(self, nc.vector, "dve")
        self.pool = Line(self, nc.gpsimd, "pool")
        self.sp = Line(self, nc.sync, "sp")
        self.lines = [self.pe, self.act, self.dve, self.pool]

    def meet(self):
        for d in self.dma_sems:
            self.sp.wait(d.last())
        self.nc.all_engine_barrier()
        for x in self.lines + self.dma_sems:
            self.nc.sync.sem_clear(x.sem)
        self.nc.all_engine_barrier()
        for x in self.lines:
            x.restart()
        for d in self.dma_sems:
            d.n = 0
        self.sp.restart()
        self.epoch += 1


class Bank:

    def __init__(self, nc, name):
        self.t = nc.alloc_psum_tensor(name, [P, 512], F32)
        self.free = []

    def __getitem__(self, key):
        return self.t[key]


class Ring:
    def __init__(self, banks):
        self.banks, self.n = banks, -1

    def take(self, pe):
        self.n += 1
        b = self.banks[self.n % len(self.banks)]
        pe.wait(*b.free)
        b.free = []
        return b


def interleave(*threads):
    live = [[g, n, 0] for g, n in threads]
    while live:
        x = min(live, key=lambda x: x[2] / x[1])
        x[2] += 1
        try:
            next(x[0])
        except StopIteration:
            live.remove(x)



class Norm:

    def __init__(self, prog, sb, name, power):
        self.p, self.power = prog, power
        self.stats = sb(name + "_stats", [P, NT, 6])
        self.mv = sb(name + "_mv", [P, NT, 2])
        self.rstd = sb(name + "_rstd", [P, NT])
        self.xn = sb(name + "_xn", [P, NT, D])

    def tokens(self, x, ready, xn_free):
        dve = self.p.dve
        v = dve.eng
        dve.wait(*ready)
        for t in range(NT):
            m = dve.mark(v.bn_stats(self.stats[:, t, :], x[:, t, :]))
        dve.wait(m)
        for t in range(NT):
            m = dve.mark(v.bn_aggr(self.mv[:, t, :], self.stats[:, t, :]))
        pool = self.p.pool
        pool.wait(m)
        m = pool.mark(pool.eng.tensor_scalar(self.rstd[:, :], self.mv[:, :, 1], EPS, None, ALU.add))
        pool.wait(m)
        m = pool.mark(pool.eng.tensor_tensor(self.rstd[:, :], self.rstd[:, :], self.power[:, :], ALU.pow))
        dve.wait(m, *xn_free)
        return [dve.mark(v.tensor_scalar(self.xn[:, t, :], x[:, t, :], self.mv[:, t, 0:1], self.rstd[:, t:t + 1],
                                         ALU.subtract, ALU.mult)) for t in range(NT)]

    def features(self, ring, ident, xn_done, hT, hT_free, mod, shift, scale, accum=None):
        pe, act = self.p.pe, self.p.act
        marks = []
        for c in range(KC):
            bank = ring.take(pe)
            for t in range(NT):
                pe.wait(xn_done[t])
                mm = pe.eng.transpose(bank[:, t * P:(t + 1) * P], self.xn[:, t, c * P:(c + 1) * P], ident[:, :])
            done = pe.mark(mm)
            act.wait(done, *hT_free)
            extra = {} if accum is None else {"accum_out": accum[:, c:c + 1]}
            m = act.mark(act.eng.activation(hT[:, c, :], bank[:, :], ACT.Identity, bias=mod[:, shift + c:shift + c + 1],
                                            scale=mod[:, scale + c:scale + c + 1], **extra))
            bank.free = [m]
            marks.append(m)
        return marks



class Constants:
    def __init__(self, prog, sb):
        nc, pool, dve = prog.nc, prog.pool, prog.dve
        g = pool.eng
        self.ident = sb("ident", [P, P])
        self.identb = sb("identb", [P, P], BF16)
        self.negL = sb("negL", [P, P], BF16)
        self.negS = sb("negS", [P, P], BF16)
        self.fold = sb("fold", [P, LB])
        self.iota_i = sb("iota_i", [P, P], I32)
        self.iota = sb("iota", [P, P])
        self.parity = sb("parity", [P, 2])
        self.group = sb("group", [P, P // HD0])
        self.sign = sb("sign", [P, 1])
        self.ones = sb("ones", [1, P])
        self.power = sb("power", [P, NT])

        def select(out, compare, fill, base, step, n, mult, after):
            pool.wait(after)
            return pool.mark(g.affine_select(out=out, in_=out, compare_op=compare, fill=fill, base=base,
                                             pattern=[[step, n]], channel_multiplier=mult))

        done = []
        m = pool.mark(g.memset(self.ident[:, :], 0.0))
        i1 = select(self.ident[:, :], ALU.not_equal, 1.0, 0, -1, P, 1, m)
        m = pool.mark(g.memset(self.negL[:, :], 0.0))
        done.append(select(self.negL[:, :], ALU.is_gt, NEG, 0, -1, P, 1, m))
        m = pool.mark(g.memset(self.negS[:, :], 0.0))
        done.append(select(self.negS[:, :], ALU.is_ge, NEG, 0, -1, P, 1, m))
        m = pool.mark(g.memset(self.fold[:, :], 0.0))
        m = select(self.fold[:, :], ALU.not_equal, 1.0, 0, -1, LB, 1, m)
        done.append(select(self.fold[:, :], ALU.not_equal, 1.0, -LB, -1, LB, 1, m))
        m = pool.mark(g.iota(self.iota_i[:, :], pattern=[[1, P]], base=0, channel_multiplier=0))
        m0 = pool.mark(g.memset(self.group[:, :], float(HD0) ** -0.5))
        m0 = select(self.group[:, :], ALU.is_ge, 0.0, 0, -HD0, P // HD0, 1, m0)
        m0 = select(self.group[:, :], ALU.is_ge, 0.0, HD0 - 1, HD0, P // HD0, -1, m0)
        m1 = pool.mark(g.memset(self.sign[:, :], 1.0))
        done.append(select(self.sign[:, :], ALU.is_ge, -1.0, P // 2 - 1, 0, 1, -1, m1))
        done.append(pool.mark(g.memset(self.ones[:, :], 1.0)))
        done.append(pool.mark(g.memset(self.power[:, :], -0.5)))
        v = dve.eng
        dve.wait(i1, m, m0)
        v.tensor_copy(self.identb[:, :], self.ident[:, :])
        v.tensor_copy(self.iota[:, :], self.iota_i[:, :])
        m2 = dve.mark(v.tensor_reduce(self.parity[:, :], self.group[:, :].rearrange("p (g a) -> p a g", a=2), AX.X,
                                      ALU.add))
        self.ready = done + [i1, m2]


def modulation(prog, ring, sb, layer, cT_d, wmod_d, mod_d, rows_d, row_kinds):
    pe, act, dve, sp = prog.pe, prog.act, prog.dve, prog.sp
    v = dve.eng
    n = f"m{layer}"
    cT = sb(n + "cT", [P, KC, B])
    th = sb(n + "th", [P, KC, B])
    sil = sb(n + "sil", [P, KC, B])
    w = sb(n + "w", [P, KC, 6 * D])
    cols = sb(n + "cols", [P, B, NMOD])
    size = sb(n + "size", [P, B, NMOD])
    rows = sb(n + "rows", [B, len(row_kinds) * D])
    rsize = sb(n + "rsize", [B, len(row_kinds) * D])
    dc, dw = DmaSem(prog, n + "_c_in"), DmaSem(prog, n + "_w_in")
    dm, dr = DmaSem(prog, n + "_cols_out"), DmaSem(prog, n + "_rows_out")
    c_in = dc.mark(sp.eng.dma_start(cT[:, :, :], cT_d.rearrange("(k p) b -> p k b", p=P)))
    w_in = dw.mark(sp.eng.dma_start(w[:, :, :], wmod_d.rearrange("(k p) n -> p k n", p=P)))
    act.wait(c_in)
    m = act.mark(act.eng.activation(th[:, :, :], cT[:, :, :], ACT.Tanh, scale=0.5))
    dve.wait(m, c_in)
    m = dve.mark(v.scalar_tensor_tensor(out=th[:, :, :], in0=th[:, :, :], scalar=1.0, in1=cT[:, :, :], op0=ALU.add,
                                        op1=ALU.mult))
    dve.wait(m)
    sil_done = dve.mark(v.tensor_scalar(sil[:, :, :], th[:, :, :], 0.5, None, ALU.mult))
    pe.wait(sil_done, w_in)
    bank = ring.take(pe)
    for j in range(NMOD):
        for k in range(KC):
            mm = pe.eng.matmul(bank[:, j * B:(j + 1) * B], w[:, k, j * P:(j + 1) * P], sil[:, k, :], start=(k == 0),
                               stop=(k == KC - 1))
    m = pe.mark(mm)
    dve.wait(m)
    m = dve.mark(v.tensor_copy(cols[:, :, :], bank[:, 0:NMOD * B].rearrange("p (j b) -> p b j", b=B)))
    bank.free = [m]
    dve.wait(m)
    for j in (CA, CB):
        m = dve.mark(v.tensor_scalar(cols[:, :, j:j + KC], cols[:, :, j:j + KC], 1.0, None, ALU.add))

    def gate(g, size):
        m = dve.mark(v.scalar_tensor_tensor(out=size, in0=g, scalar=-1.0, in1=g, op0=ALU.mult, op1=ALU.max))
        dve.wait(m)
        v.tensor_scalar(size, size, 0.25, None, ALU.max)
        m = dve.mark(v.tensor_scalar(g, g, 0.0, 2.0, ALU.is_ge, ALU.mult))
        dve.wait(m)
        return dve.mark(v.scalar_tensor_tensor(out=g, in0=g, scalar=-1.0, in1=size, op0=ALU.add, op1=ALU.mult))

    for j in (GA, GB):
        m = gate(cols[:, :, j:j + KC], size[:, :, j:j + KC])
    sp.wait(m)
    dm.mark(sp.eng.dma_start(mod_d.rearrange("b p n -> p b n"), cols[:, :, :]))
    for i, j in enumerate(row_kinds):
        bank = ring.take(pe)
        for k in range(KC):
            mm = pe.eng.matmul(bank[0:B, 0:D], sil[:, k, :], w[:, k, j * P:j * P + D], start=(k == 0),
                               stop=(k == KC - 1))
        m = pe.mark(mm)
        dve.wait(m)
        m = dve.mark(v.tensor_copy(rows[:, i * D:(i + 1) * D], bank[0:B, 0:D]))
        bank.free = [m]
    dve.wait(m)
    m = gate(rows[:, :], rsize[:, :])
    sp.wait(m)
    dr.mark(sp.eng.dma_start(rows_d, rows[:, :]))



class Block0:
    def __init__(self, prog, sb, const, ring, d):
        self.p, self.const, self.ring, self.d = prog, const, ring, d
        self.wqkv = sb("wqkv0", [P, KC, 3 * D])
        self.wout = sb("wout0", [P, KC, D])
        self.bq = sb("bq", [P, KC])
        self.bqp = sb("bqp", [P, KC, 2])
        self.bk = sb("bk", [P, KC])
        self.bv = sb("bv", [P, KC])
        self.bout = sb("bout", [1, D])
        self.w1 = sb("cw1", [P, KC, D])
        self.w2 = sb("cw2", [P, KC, P])
        self.w3 = sb("cw3", [P, 64])
        self.w4c = sb("cw4c", [64, 1])
        self.w4 = sb("cw4", [64, P])
        self.b1 = sb("cb1", [P, KC])
        self.b2 = sb("cb2", [P, 1])
        self.b3 = sb("cb3", [64, 1])
        self.b4 = sb("cb4", [P, 1])
        self.g1 = sb("gw1", [P, KC, P])
        self.g2 = sb("gw2", [P, 64])
        self.g3c = sb("gw3c", [64, 1])
        self.g3 = sb("gw3", [64, P])
        self.gb1 = sb("gb1", [P, 1])
        self.gb2 = sb("gb2", [64, 1])
        self.gb3 = sb("gb3", [P, 1])
        self.ar = sb("ar", [P, 1])
        self.sar = sb("sar", [P, 3])
        self.x = sb("x0", [P, NT, D])
        self.mod = sb("mod0", [P, NMOD])
        self.ga = sb("ga0", [P, D])
        self.norm = Norm(prog, sb, "n0", const.power)
        self.hT = sb("hT0", [P, KC, T])
        self.q = sb("q0", [P, KC, NBLK, 2, LB])
        self.k = sb("k0", [P, KC, NBLK, NR, LB])
        self.v = sb("v0", [P, NBLK, NR, 66])
        self.mx = [sb(f"mx0{i}", [P, NR * KC]) for i in range(2)]
        self.s = [sb(f"s0{i}", [P, NR, KC, LB]) for i in range(2)]
        self.pT = [sb(f"pT0{i}", [P, NR, P]) for i in range(2)]
        self.ri = [sb(f"ri0{i}", [P, NR, KC]) for i in range(2)]
        self.o = [sb(f"o0{i}", [P, KC, NR, 2, HD0]) for i in range(2)]
        self.tmp = sb("tmp0", [P, 2, D])
        self.sum = sb("sum0", [P, KC])
        self.gf = sb("gf", [P, 4])
        self.a1 = sb("a1", [P, KC, T])
        self.aT = self.a1
        self.a2 = sb("a2", [P, T])
        self.a3 = sb("a3", [64, T])
        self.tf = sb("tf", [P, T])
        names = ["x", "mod", "ga", "xout"]
        self.dma = {n: DmaSem(prog, f"b0_{n}") for n in names}
        self.dw = [DmaSem(prog, f"b0_w{i}") for i in range(2)]

    def setup(self):
        p, d = self.p, self.d
        nc, sp, dve, act = p.nc, p.sp, p.dve, p.act
        v = dve.eng
        e, dw = (act.eng, self.dw[0])

        def load(dst, src):
            return dw.mark(e.dma_start(dst, src))

        load(self.wqkv[:, :, :], d["w_qkv0"].rearrange("(k p) n -> p k n", p=P))
        bq = d["L0_attn_b_qkv"].rearrange("(a k p) -> a p k", p=P, k=KC)
        with nc.allow_non_contiguous_dma(reason="bias columns"):
            load(self.bq[:, :], bq[0])
            load(self.bk[:, :], bq[1])
            load(self.bv[:, :], bq[2])
            load(self.b1[:, :], d["L0_ffn_cn_b1"].rearrange("(k p) -> p k", p=P))
            load(self.b2[:, :], d["L0_ffn_cn_b2"].rearrange("(p a) -> p a", a=1))
            load(self.b3[:, :], d["L0_ffn_cn_b3"].rearrange("(p a) -> p a", a=1))
            load(self.gb1[:, :], d["L0_ffn_gc_b1"].rearrange("(p a) -> p a", a=1))
            load(self.gb2[:, :], d["L0_ffn_gc_b2"].rearrange("(p a) -> p a", a=1))
            load(self.b4[:, :], d["L0_ffn_cn_b4"].partition_broadcast(P))
            load(self.gb3[:, :], d["L0_ffn_gc_b3"].partition_broadcast(P))
            load(self.ar[:, :], d["L0_ffn_adaptive_range"].partition_broadcast(P))
            load(self.w4c[:, :], d["L0_ffn_cn_w4"])
            load(self.g3c[:, :], d["L0_ffn_gc_w3"])
        load(self.wout[:, :, :], d["w_out0"].rearrange("(k p) n -> p k n", p=P))
        load(self.bout[:, :], d["L0_attn_b_out"].rearrange("(a n) -> a n", a=1))
        load(self.w1[:, :, :], d["L0_ffn_cn_w1"].rearrange("(k p) n -> p k n", p=P))
        load(self.w2[:, :, :], d["L0_ffn_cn_w2"].rearrange("(k p) n -> p k n", p=P))
        load(self.w3[:, :], d["L0_ffn_cn_w3"])
        load(self.g1[:, :, :], d["L0_ffn_gc_w1"].rearrange("(k p) n -> p k n", p=P))
        loaded = load(self.g2[:, :], d["L0_ffn_gc_w2"])
        pool = p.pool
        g = pool.eng
        m = pool.mark(g.memset(self.v[:, :, :, :], 0.0))
        g.memset(self.k[:, :, :, :, :], 0.0)
        for o in self.o:
            g.memset(o[:, :, :, :, :], 0.0)
        dve.wait(m)
        for c in range(KC):
            v.memset(self.v[64 * c:64 * c + 64, :, :, 64 + c:65 + c], 1.0)
        dve.wait(loaded, *self.const.ready)
        v.tensor_copy(self.w4[:, :], self.w4c[:, 0:1].to_broadcast([64, P]))
        v.tensor_copy(self.g3[:, :], self.g3c[:, 0:1].to_broadcast([64, P]))
        for c in range(KC):
            v.tensor_scalar(self.bqp[:, c, :], self.const.parity[:, :], self.bq[:, c:c + 1], None, ALU.mult)
        v.tensor_scalar(self.b4[:, :], self.b4[:, :], 0.5, None, ALU.mult)
        v.tensor_scalar(self.gb3[:, :], self.gb3[:, :], 0.5, None, ALU.mult)
        m = dve.mark(v.tensor_tensor(self.ar[:, :], self.ar[:, :], self.const.sign[:, :], ALU.mult))
        dve.wait(m)
        v.tensor_scalar(self.sar[:, 0:1], self.ar[:, :], 0.3, None, ALU.mult)
        v.tensor_scalar(self.sar[:, 1:2], self.ar[:, :], 0.7, None, ALU.mult)
        dve.mark(v.tensor_scalar(self.sar[:, 2:3], self.const.sign[:, :], 0.1, None, ALU.mult))

    def batch(self, b):
        p, ring, const, d = self.p, self.ring, self.const, self.d
        pe, act, dve, sp = p.pe, p.act, p.dve, p.sp
        v, a, te = dve.eng, act.eng, pe.eng
        one = bass.ds(b, 1)
        x, hT = self.x, self.hT
        x_in = self.dma["x"].mark(sp.eng.dma_start(
            x[:, :, :], d["L0_attn_x"][one, :, :].rearrange("b (t p) n -> p (b t) n", p=P)))
        mod_in = self.dma["mod"].mark(sp.eng.dma_start(
            self.mod[:, :], d["mod0"][one, :, :].rearrange("b p n -> p (b n)")))
        ga_in = self.dma["ga"].mark(sp.eng.dma_start(
            self.ga[:, :], d["rows0"][one, :].rearrange("b n -> (b n)").partition_broadcast(P)))
        yield
        xn = self.norm.tokens(x, [x_in], [])
        yield
        act.wait(mod_in)
        h = self.norm.features(ring, const.ident, xn, hT, [], self.mod, SA, CA)
        yield
        kdone, qdone, vdone = [], [], []
        for c in range(KC):
            bank = ring.take(pe)
            pe.wait(*h)
            for k in range(KC):
                mm = te.matmul(bank[:, :], self.wqkv[:, k, D + c * P:D + (c + 1) * P], hT[:, k, :], start=(k == 0),
                               stop=(k == KC - 1))
            m = pe.mark(mm)
            act.wait(m)
            for r in range(NR):
                rows = slice(32 * r, 32 * r + 32)
                m = act.mark(a.activation(self.k[rows, c, :, r, :], bank[rows, :].rearrange("p (n m) -> p n m", m=LB),
                                          ACT.Identity, bias=self.bk[rows, c:c + 1]))
            bank.free = [m]
            kdone = [m]
            bank = ring.take(pe)
            for k in range(KC):
                mm = te.matmul(bank[:, :], self.wqkv[:, k, c * P:(c + 1) * P], hT[:, k, :], start=(k == 0),
                               stop=(k == KC - 1))
            m = pe.mark(mm)
            dve.wait(m)
            for par in range(2):
                m = dve.mark(v.tensor_scalar(self.q[:, c, :, par, :], bank[:, :].rearrange("p (n l) -> p n l", l=LB),
                                             const.parity[:, par:par + 1], self.bqp[:, c, par:par + 1], ALU.mult,
                                             ALU.add))
            bank.free = [m]
            qdone = [m]
            yield
        for half in range(2):
            bank = ring.take(pe)
            for n in range(4):
                blk = 4 * half + n
                for c in range(KC):
                    for k in range(KC):
                        mm = te.matmul(bank[64 * c:64 * c + 64, n * P:(n + 1) * P], hT[:, k, blk * LB:(blk + 1) * LB],
                                       self.wqkv[:, k, 2 * D + c * P:2 * D + (c + 1) * P], start=(k == 0),
                                       stop=(k == KC - 1))
            m = pe.mark(mm)
            for c in range(KC):
                rows = slice(64 * c, 64 * c + 64)
                line, copy = (act, a.copy) if c else (dve, v.tensor_copy)
                line.wait(m)
                vdone.append(line.mark(copy(self.v[rows, 4 * half:4 * half + 4, :, 32 * c:32 * c + 32],
                                            bank[rows, :].rearrange("p (n r e) -> p n r e", n=4, r=NR))))
            bank.free = vdone[-2:]
            yield
        sdone, exped, tdone, odone, adone = {}, {}, {}, {}, {}
        ptr_free, o_free, s_free = {}, {}, {}

        def scores(n):
            bank = ring.take(pe)
            pe.wait(*kdone, *qdone)
            for c in range(KC):
                mm = te.matmul(bank[:, c * 256:(c + 1) * 256], self.q[:, c, n, :, :].rearrange("p a l -> p (a l)"),
                               self.k[:, c, n, :, :].rearrange("p r m -> p (r m)"), start=True, stop=True)
            m = pe.mark(mm)
            view = bank[:, :].rearrange("p (c r m) -> p c r m", c=KC, r=NR)
            s, mx = self.s[n % 2], self.mx[n % 2]
            dve.wait(m)
            m = dve.mark(v.tensor_reduce(mx[:, :], bank[:, :].rearrange("p (g m) -> p g m", m=LB), AX.X, ALU.max))
            dve.wait(m, s_free.get(n - 2))
            m = dve.mark(v.tensor_tensor(s[:, :, :, :].rearrange("p r c m -> p c r m"), view,
                                         mx[:, :].rearrange("p (c r) -> p c r", c=KC).unsqueeze(3)
                                         .to_broadcast([P, KC, NR, LB]), ALU.subtract))
            bank.free = [m]
            act.wait(m)
            exped[n] = act.mark(a.activation(s[:, :, :, :], s[:, :, :, :], ACT.Exp))

        def turn(n):
            bank = ring.take(pe)
            pe.wait(exped[n])
            for r in range(NR):
                mm = te.transpose(bank[:, r * P:(r + 1) * P],
                                  self.s[n % 2][:, r, :, :].rearrange("p c m -> p (c m)"), const.ident[:, :])
            m = pe.mark(mm)
            s_free[n] = m
            act.wait(m, ptr_free.get(n - 2))
            tdone[n] = act.mark(a.copy(self.pT[n % 2][:, :, :], bank[:, :].rearrange("p (r l) -> p r l", r=NR)))
            bank.free = [tdone[n]]

        def values(n):
            bank = ring.take(pe)
            pe.wait(tdone[n], *vdone)
            for r in range(NR):
                mm = te.matmul(bank[:, r * 66:(r + 1) * 66], self.pT[n % 2][:, r, :], self.v[:, n, r, :], start=True,
                               stop=True)
            m = pe.mark(mm)
            ptr_free[n] = m
            view = bank[:, 0:NR * 66].rearrange("p (r e) -> p r e", r=NR)
            ri, o = self.ri[n % 2], self.o[n % 2]
            dve.wait(m)
            m = dve.mark(v.reciprocal(ri[:, :, :], view[:, :, 64:66]))
            dve.wait(m, o_free.get(n - 2))
            for par in range(2):
                rows = slice(64 * par, 64 * par + 64)
                for c in range(KC):
                    m = dve.mark(v.tensor_tensor(
                        o[rows, c, :, par, :], view[rows, :, 32 * c + 16 * par:32 * c + 16 * par + 16],
                        ri[rows, :, c:c + 1].to_broadcast([64, NR, HD0]), ALU.mult))
            bank.free = [m]
            odone[n] = m

        def gather(n):
            bank = ring.take(pe)
            pe.wait(odone[n])
            for c in range(KC):
                mm = te.matmul(bank[:, c * LB:(c + 1) * LB], self.o[n % 2][:, c, :, :, :].rearrange("p r a e -> p (r a e)"),
                               const.fold[:, :], start=True, stop=True)
            m = pe.mark(mm)
            o_free[n] = m
            act.wait(m)
            for c in range(KC):
                m = act.mark(a.activation(self.aT[:, c, n * LB:(n + 1) * LB], bank[:, c * LB:(c + 1) * LB],
                                          ACT.Identity, bias=self.bv[:, c:c + 1]))
            bank.free = [m]
            adone[n] = m

        for n in range(NBLK + 3):
            if n < NBLK:
                scores(n)
                yield
            if 0 <= n - 1 < NBLK:
                turn(n - 1)
                yield
            if 0 <= n - 2 < NBLK:
                values(n - 2)
                yield
            if 0 <= n - 3 < NBLK:
                gather(n - 3)
                yield
        xdone = []
        dve.wait(ga_in)
        for pair in range(NT // 2):
            bank = ring.take(pe)
            pe.wait(adone[NBLK - 1])
            for i in range(2):
                t = 2 * pair + i
                out = bank[:, i * D:(i + 1) * D]
                for k in range(KC):
                    te.matmul(out, self.aT[:, k, t * P:(t + 1) * P], self.wout[:, k, :], start=(k == 0), stop=False)
                mm = te.matmul(out, const.ones[:, :], self.bout[:, :], start=False, stop=True)
            m = pe.mark(mm)
            dve.wait(m, *xdone)
            m = dve.mark(v.tensor_tensor(self.tmp[:, :, :], bank[:, :].rearrange("p (i n) -> p i n", i=2),
                                         self.ga[:, :].unsqueeze(1).to_broadcast([P, 2, D]), ALU.mult))
            bank.free = [m]
            dve.wait(m)
            xt = x[:, 2 * pair:2 * pair + 2, :]
            xdone = [dve.mark(v.tensor_tensor(xt, xt, self.tmp[:, :, :], ALU.add))]
            yield
        xn = self.norm.tokens(x, xdone, h)
        yield
        out = self.norm.features(ring, const.ident, xn, hT, [], self.mod, SB, CB, accum=self.sum)
        yield
        bank = ring.take(pe)
        pe.wait(*out)
        for k in range(KC):
            mm = te.matmul(bank[:, 0:1], self.g1[:, k, :], self.sum[:, k:k + 1], start=(k == 0), stop=(k == KC - 1))
        m = pe.mark(mm)
        act.wait(m)
        m = act.mark(a.activation(self.gf[:, 0:1], bank[:, 0:1], ACT.Gelu, bias=self.gb1[:, :], scale=1.0 / T))
        bank.free = [m]
        yield
        bank = ring.take(pe)
        pe.wait(m)
        m = pe.mark(te.matmul(bank[0:64, 0:1], self.g2[:, :], self.gf[:, 0:1], start=True, stop=True))
        act.wait(m)
        m = act.mark(a.activation(self.gf[0:64, 1:2], bank[0:64, 0:1], ACT.Gelu, bias=self.gb2[:, :]))
        bank.free = [m]
        yield
        bank = ring.take(pe)
        pe.wait(m)
        m = pe.mark(te.matmul(bank[:, 0:1], self.g3[:, :], self.gf[0:64, 1:2], start=True, stop=True))
        act.wait(m)
        m = act.mark(a.activation(self.gf[:, 2:3], bank[:, 0:1], ACT.Tanh, bias=self.gb3[:, :], scale=0.5))
        bank.free = [m]
        dve.wait(m)
        base = dve.mark(v.tensor_scalar(self.gf[:, 3:4], self.gf[:, 2:3], self.sar[:, 1:2], self.sar[:, 2:3], ALU.mult,
                                        ALU.add))
        yield
        tdone2, csdone = [], []
        for cycle in range(CYCLES):
            l1 = []
            for c in range(KC):
                bank = ring.take(pe)
                pe.wait(*out)
                for k in range(KC):
                    mm = te.matmul(bank[:, :], self.w1[:, k, c * P:(c + 1) * P], hT[:, k, :], start=(k == 0),
                                   stop=(k == KC - 1))
                m = pe.mark(mm)
                act.wait(m)
                m = act.mark(a.activation(self.a1[:, c, :], bank[:, :], ACT.Gelu, bias=self.b1[:, c:c + 1]))
                bank.free = [m]
                l1.append(m)
                yield
            bank = ring.take(pe)
            pe.wait(*l1)
            for k in range(KC):
                mm = te.matmul(bank[:, :], self.w2[:, k, :], self.a1[:, k, :], start=(k == 0), stop=(k == KC - 1))
            m = pe.mark(mm)
            act.wait(m)
            m = act.mark(a.activation(self.a2[:, :], bank[:, :], ACT.Gelu, bias=self.b2[:, :]))
            bank.free = [m]
            yield
            bank = ring.take(pe)
            pe.wait(m)
            m = pe.mark(te.matmul(bank[0:64, :], self.w3[:, :], self.a2[:, :], start=True, stop=True))
            act.wait(m)
            m = act.mark(a.activation(self.a3[:, :], bank[0:64, :], ACT.Gelu, bias=self.b3[:, :]))
            bank.free = [m]
            yield
            bank = ring.take(pe)
            pe.wait(m)
            m = pe.mark(te.matmul(bank[:, :], self.w4[:, :], self.a3[:, :], start=True, stop=True))
            act.wait(m, *csdone)
            m = act.mark(a.activation(self.tf[:, :], bank[:, :], ACT.Tanh, bias=self.b4[:, :], scale=0.5))
            bank.free = [m]
            dve.wait(m, base)
            m = dve.mark(v.tensor_scalar(self.tf[:, :], self.tf[:, :], self.sar[:, 0:1], self.gf[:, 3:4], ALU.mult,
                                         ALU.add))
            dve.wait(m)
            dve.mark(v.tensor_tensor(self.a1[:, 0, :], self.tf[:, :], hT[:, 1, :], ALU.mult))
            m = dve.mark(v.tensor_tensor(self.a1[:, 1, :], self.tf[:, :], hT[:, 0, :], ALU.mult))
            csdone = [m]
            dve.wait(m)
            dve.mark(v.tensor_tensor(hT[:, 0, :], hT[:, 0, :], self.a1[:, 0, :], ALU.add))
            out = [dve.mark(v.tensor_tensor(hT[:, 1, :], hT[:, 1, :], self.a1[:, 1, :], ALU.subtract))]
            yield
        dve.wait(*out)
        for c in range(KC):
            m = dve.mark(v.tensor_scalar(hT[:, c, :], hT[:, c, :], self.mod[:, GB + c:GB + c + 1], None, ALU.mult))
        for pair in range(NT // 2):
            bank = ring.take(pe)
            pe.wait(m)
            for i in range(2):
                t = 2 * pair + i
                for c in range(KC):
                    mm = te.transpose(bank[:, i * D + c * P:i * D + (c + 1) * P], hT[:, c, t * P:(t + 1) * P],
                                      const.ident[:, :])
            md = pe.mark(mm)
            dve.wait(md)
            xt = x[:, 2 * pair:2 * pair + 2, :]
            md = dve.mark(v.tensor_tensor(xt, xt, bank[:, :].rearrange("p (i n) -> p i n", i=2), ALU.add))
            bank.free = [md]
        sp.wait(md)
        self.dma["xout"].mark(sp.eng.dma_start(d["x1"][one, :, :].rearrange("b (t p) n -> p (b t) n", p=P), x[:, :, :]))
        yield



class Block1:
    def __init__(self, prog, sb, const, ring, d):
        self.p, self.const, self.ring, self.d = prog, const, ring, d
        self.wqkv = sb("wqkv1", [P, KC, 6 * CH1])
        self.wout = sb("wout1", [P, NHP, D])
        self.wgate = sb("wgate", [P, KC, E])
        self.x = sb("x1s", [P, NT, D])
        self.mod = sb("mod1", [P, NMOD])
        self.ga = sb("ga1", [P, D])
        self.norm = Norm(prog, sb, "n1", const.power)
        self.hT = sb("hT1", [P, KC, T])
        self.vc = sb("vc1", [P, NT, CH1])
        self.f = [[sb(f"f1{i}{j}", [P, T]) for j in range(5)] for i in range(2)]
        w = P * NT * (NT + 1) // 2
        self.look = [sb(f"look{i}", [P, w]) for i in range(2)]
        self.term = [sb(f"term{i}", [P, w]) for i in range(2)]
        self.th = [sb(f"th1{i}", [P, T]) for i in range(2)]
        self.s = [sb(f"s1{i}", [P, T]) for i in range(2)]
        self.pT = [sb(f"pT1{i}", [P, T]) for i in range(2)]
        self.mx = [sb(f"mx1{i}", [P, 4]) for i in range(2)]
        self.o = [sb(f"o1{i}", [P, NT, P]) for i in range(2)]
        self.oT = sb("oT1", [P, NHP, T])
        self.tmp = sb("tmp1", [P, 2, D])
        self.pr = sb("pr1", [P, NT, E])
        self.pm = sb("pm1", [P, NT, 3])
        self.prT = sb("prT1", [E, T])
        self.dma = {n: DmaSem(prog, f"b1_{n}") for n in ["x", "mod", "ga", "w", "xout", "xn", "pr", "prT"]}

    def setup(self):
        e, d, dw = self.p.act.eng, self.d, self.dma["w"]
        dw.mark(e.dma_start(self.wqkv[:, :, :], d["w_qkv1"].rearrange("(k p) n -> p k n", p=P)))
        dw.mark(e.dma_start(self.wout[:, :, :], d["w_out1"].rearrange("(k p) n -> p k n", p=P)))
        dw.mark(e.dma_start(self.wgate[:, :, :], d["w_gate"].rearrange("(k p) n -> p k n", p=P)))

    def batch(self, b):
        p, ring, const, d = self.p, self.ring, self.const, self.d
        pe, act, dve, sp, pool = p.pe, p.act, p.dve, p.sp, p.pool
        v, a, te = dve.eng, act.eng, pe.eng
        one = bass.ds(b, 1)
        x, hT = self.x, self.hT
        x_in = self.dma["x"].mark(sp.eng.dma_start(
            x[:, :, :], d["x1"][one, :, :].rearrange("b (t p) n -> p (b t) n", p=P)))
        mod_in = self.dma["mod"].mark(sp.eng.dma_start(
            self.mod[:, :], d["mod1"][one, :, :].rearrange("b p n -> p (b n)")))
        ga_in = self.dma["ga"].mark(sp.eng.dma_start(
            self.ga[:, :], d["rows1"][one, 0:D].rearrange("b n -> (b n)").partition_broadcast(P)))
        yield
        xn = self.norm.tokens(x, [x_in], [])
        yield
        act.wait(mod_in)
        h = self.norm.features(ring, const.ident, xn, hT, [], self.mod, SA, CA)
        yield
        vcdone = []
        for t in range(NT):
            bank = ring.take(pe)
            pe.wait(*h)
            for k in range(KC):
                mm = te.matmul(bank[:, :], hT[:, k, t * P:(t + 1) * P], self.wqkv[:, k, 5 * CH1:6 * CH1],
                               start=(k == 0), stop=(k == KC - 1))
            m = pe.mark(mm)
            act.wait(m)
            m = act.mark(a.copy(self.vc[:, t, :], bank[:, :]))
            bank.free = [m]
            vcdone = [m]
            yield
        SCALES = [HD1 ** -0.5, 1.0, 1.0, HD1 ** -0.5, 2.0]
        fdone, lookdone, lt_free = {}, {}, {}
        projections_free = {}

        def project(hp, j):
            bank = ring.take(pe)
            for k in range(KC):
                mm = te.matmul(bank[:, :], self.wqkv[:, k, j * CH1 + hp * P:j * CH1 + (hp + 1) * P], hT[:, k, :],
                               start=(k == 0), stop=(k == KC - 1))
            m = pe.mark(mm)
            act.wait(m, projections_free.get(hp - 2))
            m = act.mark(a.mul(self.f[hp % 2][j][:, :], bank[:, :], SCALES[j]))
            bank.free = [m]
            fdone[hp] = m

        def off(j):
            return P * j * (j + 1) // 2

        def toff(j):
            return P * (j * NT - j * (j - 1) // 2)

        def lookahead(hd, j):
            rows = slice(64 * (hd % 2), 64 * (hd % 2) + 64)
            qu, ku, vu, qc, _ = self.f[hd // 2 % 2]
            look, term = self.look[hd % 2], self.term[hd % 2]
            w = (j + 1) * P
            bank = ring.take(pe)
            pe.wait(fdone[hd // 2])
            te.matmul(bank[:, 0:w], ku[rows, j * P:(j + 1) * P], qu[rows, 0:w], start=True, stop=False)
            m = pe.mark(te.matmul(bank[:, j * P:w], const.identb[:, :], const.negL[:, :], start=False, stop=True))
            act.wait(m, lt_free.get(hd - 2))
            dst = look[:, off(j):off(j) + w]
            m = act.mark(a.activation(dst, bank[:, 0:w], ACT.Tanh, scale=0.5))
            bank.free = [m]
            pool.wait(m)
            pool.mark(pool.eng.tensor_scalar(dst, dst, 0.5, 0.5, ALU.mult, ALU.add))
            bank = ring.take(pe)
            w = T - j * P
            m = pe.mark(te.matmul(bank[:, 0:w], vu[rows, j * P:(j + 1) * P], qc[rows, j * P:T], start=True, stop=True))
            dve.wait(m, lt_free.get(hd - 2))
            m = dve.mark(v.tensor_copy(term[:, toff(j):toff(j) + w], bank[:, 0:w]))
            bank.free = [m]
            pool.wait(m)
            diagonal = term[:, toff(j):toff(j) + P]
            lookdone[hd] = pool.mark(pool.eng.affine_select(
                out=diagonal, in_=diagonal, compare_op=ALU.is_ge, fill=0.0, base=0, pattern=[[1, P]],
                channel_multiplier=-1))

        expdone, pTdone, ridone, th_free, pT_free = {}, {}, {}, {}, {}

        def scores(u):
            hd, i = u // NT, u % NT
            rows = slice(64 * (hd % 2), 64 * (hd % 2) + 64)
            _, _, _, qc, kc = self.f[hd // 2 % 2]
            look, term = self.look[hd % 2], self.term[hd % 2]
            w = (i + 1) * P
            su = ring.take(pe)
            pe.wait(lookdone[hd])
            for j in range(i, -1, -1):
                mm = te.matmul(su[:, 0:(j + 1) * P], term[:, toff(j) + (i - j) * P:toff(j) + (i - j + 1) * P],
                               look[:, off(j):off(j) + (j + 1) * P], start=(j == i), stop=(j == 0))
            su_done = pe.mark(mm)
            if i == NT - 1:
                lt_free[hd] = su_done
            sc = ring.take(pe)
            te.matmul(sc[:, 0:w], qc[rows, i * P:(i + 1) * P], kc[rows, 0:w], start=True, stop=False)
            sc_done = pe.mark(te.matmul(sc[:, i * P:w], const.identb[:, :], const.negS[:, :], start=False, stop=True))
            if hd % 2 and i == NT - 1:
                projections_free[hd // 2] = sc_done
            th, s, mx = self.th[u % 2], self.s[u % 2], self.mx[u % 2]
            act.wait(su_done, th_free.get(u - 2))
            m = act.mark(a.activation(th[:, 0:w], su[:, 0:w], ACT.Tanh, scale=0.5))
            dve.wait(m, su_done)
            m = dve.mark(v.scalar_tensor_tensor(out=th[:, 0:w], in0=th[:, 0:w], scalar=1.0, in1=su[:, 0:w],
                                                op0=ALU.add, op1=ALU.mult))
            su.free = [m]
            dve.wait(m, sc_done, pT_free.get(u - 2))
            m = dve.mark(v.tensor_tensor_reduce(s[:, 0:w], sc[:, 0:w], th[:, 0:w], 1.0, -3e38, ALU.subtract, ALU.max,
                                                mx[:, 0:1]))
            sc.free = [m]
            th_free[u] = m
            dve.wait(m)
            m = dve.mark(v.tensor_scalar(mx[:, 1:2], mx[:, 0:1], -0.5, None, ALU.mult))
            act.wait(m)
            expdone[u] = act.mark(a.activation(s[:, 0:w], s[:, 0:w], ACT.Exp, bias=mx[:, 1:2], scale=0.5,
                                               accum_out=mx[:, 2:3]))

        def turn(u):
            i = u % NT
            w = (i + 1) * P
            bank = ring.take(pe)
            pe.wait(expdone[u])
            for k in range(i + 1):
                mm = te.transpose(bank[:, k * P:(k + 1) * P], self.s[u % 2][:, k * P:(k + 1) * P], const.ident[:, :])
            m = pe.mark(mm)
            pT_free[u] = m
            dve.wait(m, ridone.get(u - 2), expdone[u])
            pTdone[u] = dve.mark(v.tensor_copy(self.pT[u % 2][:, 0:w], bank[:, 0:w]))
            bank.free = [pTdone[u]]
            dve.mark(v.reciprocal(self.mx[u % 2][:, 3:4], self.mx[u % 2][:, 2:3]))

        def attend(u):
            hd, i = u // NT, u % NT
            bank = ring.take(pe)
            pe.wait(pTdone[u], *vcdone)
            for k in range(i + 1):
                mm = te.matmul(bank[:, 0:HD1], self.pT[u % 2][:, k * P:(k + 1) * P],
                               self.vc[:, k, hd * HD1:(hd + 1) * HD1], start=(k == 0), stop=(k == i))
            m = pe.mark(mm)
            dve.wait(m, (dve.sem, pTdone[u][1] + 1, p.epoch), o_free.get(hd // 2 - 2))
            ridone[u] = dve.mark(v.tensor_scalar(self.o[hd // 2 % 2][:, i, hd % 2 * HD1:(hd % 2 + 1) * HD1], bank[:, 0:HD1],
                                                 self.mx[u % 2][:, 3:4], None, ALU.mult))
            bank.free = [ridone[u]]

        oTdone, o_free = [], {}

        def turn_out(hp, last):
            bank = ring.take(pe)
            pe.wait(last)
            for t in range(NT):
                mm = te.transpose(bank[:, t * P:(t + 1) * P], self.o[hp % 2][:, t, :], const.ident[:, :])
            m = pe.mark(mm)
            o_free[hp] = m
            act.wait(m)
            oTdone.append(act.mark(a.copy(self.oT[:, hp, :], bank[:, :])))
            bank.free = [oTdone[-1]]

        for j in range(5):
            project(0, j)
            yield
        for j in range(NT):
            lookahead(0, j)
            yield
        nu = H1 * NT
        for u in range(nu + 2):
            hd, i = u // NT, u % NT
            if u < nu:
                scores(u)
                yield
                if hd % 2 == 0 and hd // 2 + 1 < NHP:
                    for j in [[0, 1], [2], [3], [4]][i]:
                        project(hd // 2 + 1, j)
                        yield
                if hd + 1 < H1:
                    lookahead(hd + 1, i)
                    yield
            if 0 <= u - 1 < nu:
                turn(u - 1)
                yield
            if 0 <= u - 2 < nu:
                attend(u - 2)
                if (u - 2) % (2 * NT) == 2 * NT - 1:
                    turn_out((u - 2) // (2 * NT), ridone[u - 2])
                yield
        xdone = []
        dve.wait(ga_in)
        for pair in range(NT // 2):
            bank = ring.take(pe)
            pe.wait(*oTdone)
            for i in range(2):
                t = 2 * pair + i
                for k in range(NHP):
                    mm = te.matmul(bank[:, i * D:(i + 1) * D], self.oT[:, k, t * P:(t + 1) * P], self.wout[:, k, :],
                                   start=(k == 0), stop=(k == NHP - 1))
            m = pe.mark(mm)
            dve.wait(m, *xdone)
            m = dve.mark(v.tensor_tensor(self.tmp[:, :, :], bank[:, :].rearrange("p (i n) -> p i n", i=2),
                                         self.ga[:, :].unsqueeze(1).to_broadcast([P, 2, D]), ALU.mult))
            bank.free = [m]
            dve.wait(m)
            xt = x[:, 2 * pair:2 * pair + 2, :]
            xdone = [dve.mark(v.tensor_tensor(xt, xt, self.tmp[:, :, :], ALU.add))]
            yield
        sp.wait(*xdone)
        self.dma["xout"].mark(sp.eng.dma_start(d["x2"][one, :, :].rearrange("b (t p) n -> p (b t) n", p=P), x[:, :, :]))
        xn = self.norm.tokens(x, xdone, h)
        sp.wait(*xn)
        self.dma["xn"].mark(sp.eng.dma_start(d["xn"][one, :, :].rearrange("b (t p) n -> p (b t) n", p=P),
                                             self.norm.xn[:, :, :]))
        yield
        h = self.norm.features(ring, const.ident, xn, hT, [], self.mod, SB, CB)
        yield
        bank = ring.take(pe)
        pe.wait(*h)
        for t in range(NT):
            for k in range(KC):
                mm = te.matmul(bank[:, t * E:(t + 1) * E], hT[:, k, t * P:(t + 1) * P], self.wgate[:, k, :],
                               start=(k == 0), stop=(k == KC - 1))
        m = pe.mark(mm)
        pr, pm = self.pr, self.pm
        view = bank[:, 0:NT * E].rearrange("p (t e) -> p t e", e=E)
        dve.wait(m)
        m = dve.mark(v.tensor_reduce(pm[:, :, 0], view, AX.X, ALU.max))
        dve.wait(m)
        m = dve.mark(v.tensor_tensor(pr[:, :, :], view, pm[:, :, 0:1].to_broadcast([P, NT, E]), ALU.subtract))
        bank.free = [m]
        act.wait(m)
        m = act.mark(a.activation(pr[:, :, :], pr[:, :, :], ACT.Exp))
        yield
        dve.wait(m)
        m = dve.mark(v.tensor_reduce(pm[:, :, 1], pr[:, :, :], AX.X, ALU.add))
        dve.wait(m)
        m = dve.mark(v.reciprocal(pm[:, :, 2], pm[:, :, 1]))
        dve.wait(m)
        m = dve.mark(v.tensor_tensor(pr[:, :, :], pr[:, :, :], pm[:, :, 2:3].to_broadcast([P, NT, E]), ALU.mult))
        sp.wait(m)
        self.dma["pr"].mark(sp.eng.dma_start(d["pr"][one, :, :].rearrange("b p n -> p (b n)"),
                                             pr[:, :, :].rearrange("p t e -> p (t e)")))
        bank = ring.take(pe)
        pe.wait(m)
        for t in range(NT):
            mm = te.transpose(bank[0:E, t * P:(t + 1) * P], pr[:, t, :], const.ident[:, :])
        m = pe.mark(mm)
        dve.wait(m)
        m = dve.mark(v.tensor_copy(self.prT[:, :], bank[0:E, :]))
        bank.free = [m]
        sp.wait(m)
        self.dma["prT"].mark(sp.eng.dma_start(d["prT"][one, :, :].rearrange("b e t -> (b e) t"), self.prT[:, :]))
        yield



class Experts:
    def __init__(self, prog, sb, const, banks, d):
        self.p, self.const, self.banks, self.d = prog, const, banks, d
        self.w1 = [sb(f"ew1{e}", [P, KC, F]) for e in range(E)]
        self.w2 = [sb(f"ew2{e}", [P, FC, D]) for e in range(E)]
        self.wsem = [prog.nc.alloc_semaphore(f"expert{e}_in") for e in range(E)]
        self.pr = sb("prall", [B * E, T])
        self.left = sb("prleft", [B * E, T])
        self.top = sb("top8", [B * E, 8])
        self.pos = sb("pos", [B * E, T])
        self.posT = sb("posT", [P, B, NT, E])
        self.dma = {n: DmaSem(prog, f"e_{n}") for n in ["pr", "pos"]}
        self.x = sb("xe", [P, NT, D])
        self.xn = sb("xne", [P, NT, D])
        self.mod = sb("mode", [P, NMOD])
        self.gb = sb("gbe", [P, D])
        self.prb = sb("prb", [P, NT, E])
        self.posb = sb("posb", [P, NT, E])
        self.pick = [sb(f"pick{i}", [P, NT, P]) for i in range(2)]
        self.wpick = [sb(f"wpick{i}", [P, NT, P]) for i in range(2)]
        self.spread = [sb(f"spread{i}", [P, T]) for i in range(2)]
        self.xin = [sb(f"xin{i}", [P, KC, P]) for i in range(2)]
        self.h1 = [sb(f"h1{i}", [P, FC, P]) for i in range(2)]
        self.h2 = [sb(f"h2{i}", [P, D]) for i in range(2)]
        self.bdma = {n: DmaSem(prog, f"eb_{n}") for n in ["x", "xn", "mod", "gb", "pr", "pos", "out"]}

    def load_weights(self):
        for e in range(E):
            eng = self.p.act.eng if e % 2 else self.p.sp.eng
            eng.dma_start(self.w1[e][:, :, :], self.d["L1_ffn_w1"][e].rearrange("(k p) n -> p k n", p=P)
                          ).then_inc(self.wsem[e], 16)
            eng.dma_start(self.w2[e][:, :, :], self.d["L1_ffn_w2"][e].rearrange("(k p) n -> p k n", p=P)
                          ).then_inc(self.wsem[e], 16)

    def choose(self):
        p = self.p
        pe, dve, sp = p.pe, p.dve, p.sp
        v = dve.eng
        m = self.dma["pr"].mark(sp.eng.dma_start(self.pr[:, :], self.d["prT"].rearrange("b e t -> (b e) t")))
        dve.wait(m)
        src = self.pr
        for n in range(CAP // 8):
            m = dve.mark(v.max(self.top[:, :], src[:, :]))
            dve.wait(m)
            m = dve.mark(v.match_replace(self.left[:, :], self.top[:, :], src[:, :], -1.0))
            dve.wait(m)
            src = self.left
        m = dve.mark(v.tensor_scalar(self.left[:, :], self.left[:, :], 0.0, None, ALU.is_lt))
        dve.wait(m)
        m = dve.mark(v.memset(self.pr[:, :], 0.0))
        dve.wait(m)
        m = dve.mark(v.tensor_tensor_scan(self.pos[:, :], self.left[:, :], self.pr[:, :], 0.0, ALU.add, ALU.add))
        dve.wait(m)
        m = dve.mark(v.tensor_tensor(self.pos[:, :], self.pos[:, :], self.left[:, :], ALU.mult))
        dve.wait(m)
        m = dve.mark(v.tensor_scalar(self.pos[:, :], self.pos[:, :], -1.0, None, ALU.add))
        bank = self.banks[0]
        pe.wait(m, *bank.free)
        n = B * E
        for t in range(NT):
            mm = pe.eng.transpose(bank[:, t * n:(t + 1) * n], self.pos[:, t * P:(t + 1) * P], self.const.ident[0:n, 0:n])
        m = pe.mark(mm)
        dve.wait(m)
        m = dve.mark(v.tensor_copy(self.posT[:, :, :, :], bank[:, 0:NT * n].rearrange("p (t b e) -> p b t e", t=NT, b=B)))
        bank.free = [m]
        sp.wait(m)
        self.dma["pos"].mark(sp.eng.dma_start(self.d["pos"].rearrange("b p n -> p b n"),
                                              self.posT[:, :, :, :].rearrange("p b t e -> p b (t e)")))

    def batch(self, b):
        p, const, d = self.p, self.const, self.d
        pe, act, dve, sp, pool = p.pe, p.act, p.dve, p.sp, p.pool
        v, a, te, g = dve.eng, act.eng, pe.eng, pool.eng
        one = bass.ds(b, 1)
        acc = self.banks[0:2]
        ring = Ring(self.banks[2:])

        def load(name, dst, src):
            return self.bdma[name].mark(sp.eng.dma_start(dst, src))

        pos_in = load("pos", self.posb[:, :, :].rearrange("p t e -> p (t e)"),
                      d["pos"][one, :, :].rearrange("b p n -> p (b n)"))
        pr_in = load("pr", self.prb[:, :, :].rearrange("p t e -> p (t e)"),
                     d["pr"][one, :, :].rearrange("b p n -> p (b n)"))
        mod_in = load("mod", self.mod[:, :], d["mod1"][one, :, :].rearrange("b p n -> p (b n)"))
        xn_in = load("xn", self.xn[:, :, :], d["xn"][one, :, :].rearrange("b (t p) n -> p (b t) n", p=P))
        x_in = load("x", self.x[:, :, :], d["x2"][one, :, :].rearrange("b (t p) n -> p (b t) n", p=P))
        gb_in = load("gb", self.gb[:, :], d["rows1"][one, D:2 * D].rearrange("b n -> (b n)").partition_broadcast(P))
        picked, wpicked, gathered, turned, xindone, spreaddone = {}, {}, {}, {}, {}, {}
        h1done, h2done, ffn1, ffn2, scattered = {}, {}, {}, {}, {}

        def pick(e):
            dve.wait(pos_in, gathered.get(e - 2))
            for t in range(NT):
                picked[e] = dve.mark(v.tensor_scalar(self.pick[e % 2][:, t, :], const.iota[:, :],
                                                     self.posb[:, t, e:e + 1], None, ALU.is_equal))
            pool.wait(pos_in, pr_in, turned.get(e - 2))
            for t in range(NT):
                wpicked[e] = pool.mark(g.tensor_scalar(self.wpick[e % 2][:, t, :], const.iota[:, :],
                                                       self.posb[:, t, e:e + 1], self.prb[:, t, e:e + 1],
                                                       ALU.is_equal, ALU.mult))

        def gather(e):
            bank = ring.take(pe)
            pe.wait(picked[e], xn_in)
            for c in range(KC):
                for t in range(NT):
                    mm = te.matmul(bank[:, c * P:(c + 1) * P], self.xn[:, t, c * P:(c + 1) * P],
                                   self.pick[e % 2][:, t, :], start=(t == 0), stop=(t == NT - 1))
            m = gathered[e] = pe.mark(mm)
            dve.wait(m, mod_in, ffn1.get(e - 2))
            for c in range(KC):
                m = dve.mark(v.tensor_scalar(self.xin[e % 2][:, c, :], bank[:, c * P:(c + 1) * P],
                                             self.mod[:, CB + c:CB + c + 1], self.mod[:, SB + c:SB + c + 1], ALU.mult,
                                             ALU.add))
            bank.free = [m]
            xindone[e] = m

        def turn(e):
            bank = ring.take(pe)
            pe.wait(wpicked[e])
            for t in range(NT):
                mm = te.transpose(bank[:, t * P:(t + 1) * P], self.wpick[e % 2][:, t, :], const.ident[:, :])
            m = turned[e] = pe.mark(mm)
            dve.wait(m, scattered.get(e - 2))
            spreaddone[e] = dve.mark(v.tensor_copy(self.spread[e % 2][:, :], bank[:, :]))
            bank.free = [spreaddone[e]]

        def hidden(e):
            pe.eng.wait_ge(self.wsem[e], 32)
            for half in range(2):
                bank = ring.take(pe)
                pe.wait(xindone[e])
                for i in range(FC // 2):
                    f = half * (FC // 2) + i
                    for k in range(KC):
                        mm = te.matmul(bank[:, i * P:(i + 1) * P], self.w1[e][:, k, f * P:(f + 1) * P],
                                       self.xin[e % 2][:, k, :], start=(k == 0), stop=(k == KC - 1))
                m = ffn1[e] = pe.mark(mm)
                act.wait(m, ffn2.get(e - 2))
                h1done[e] = act.mark(a.activation(
                    self.h1[e % 2][:, half * (FC // 2):(half + 1) * (FC // 2), :],
                    bank[:, :].rearrange("p (f s) -> p f s", s=P), ACT.Gelu))
                bank.free = [h1done[e]]

        def output(e):
            bank = ring.take(pe)
            pe.wait(h1done[e])
            for f in range(FC):
                mm = te.matmul(bank[:, 0:D], self.h1[e % 2][:, f, :], self.w2[e][:, f, :], start=(f == 0),
                               stop=(f == FC - 1))
            m = ffn2[e] = pe.mark(mm)
            act.wait(m, scattered.get(e - 2))
            h2done[e] = act.mark(a.copy(self.h2[e % 2][:, :], bank[:, 0:D]))
            bank.free = [h2done[e]]

        def scatter(e):
            pe.wait(h2done[e], spreaddone[e])
            for t in range(NT):
                mm = te.matmul(acc[t // 2][:, t % 2 * D:(t % 2 + 1) * D], self.spread[e % 2][:, t * P:(t + 1) * P],
                               self.h2[e % 2][:, :], start=(e == 0 and t % 2 == 0), stop=(e == E - 1 and t % 2 == 1),
                               skip_group_check=True)
            scattered[e] = pe.mark(mm)

        pick(0)
        gather(0)
        turn(0)
        pick(1)
        for e in range(E):
            hidden(e)
            if e + 1 < E:
                gather(e + 1)
            if e > 0:
                scatter(e - 1)
            if e + 1 < E:
                turn(e + 1)
            if e + 2 < E:
                pick(e + 2)
            output(e)
        scatter(E - 1)
        dve.wait(scattered[E - 1], gb_in, x_in)
        gb = self.gb[:, :].unsqueeze(1).to_broadcast([P, 2, D])
        for i in range(2):
            m = dve.mark(v.tensor_tensor(self.xn[:, 2 * i:2 * i + 2, :], acc[i][:, :].rearrange("p (i n) -> p i n", i=2),
                                         gb, ALU.mult))
        dve.wait(m)
        m = dve.mark(v.tensor_tensor(self.x[:, :, :], self.x[:, :, :], self.xn[:, :, :], ALU.add))
        sp.wait(m)
        self.bdma["out"].mark(sp.eng.dma_start(d["out"][one, :, :].rearrange("b (t p) n -> p (b t) n", p=P),
                                               self.x[:, :, :]))



def program(nc, d, stop=None):
    prog = Program(nc)
    for name, shape in [("mod0", [B, P, NMOD]), ("mod1", [B, P, NMOD]), ("rows0", [B, D]), ("rows1", [B, 2 * D]),
                        ("x1", [B, T, D]), ("x2", [B, T, D]), ("xn", [B, T, D]), ("pr", [B, P, NT * E]),
                        ("prT", [B, E, T]), ("pos", [B, P, NT * E])]:
        d[name] = nc.dram_tensor(name + "_scratch", shape, F32, kind="Internal").ap()

    def allocator(stack):
        return lambda name, shape, dtype=F32: stack.enter_context(nc.sbuf_tensor(name, shape, dtype))

    banks = [Bank(nc, f"bank{i}") for i in range(8)]
    with ExitStack() as whole:
        const = Constants(prog, allocator(whole))
        with ExitStack() as stack:
            sb = allocator(stack)
            modulation(prog, Ring(banks), sb, 0, d["cT0"], d["L0_wmod"], d["mod0"], d["rows0"], [GA])
            modulation(prog, Ring(banks), sb, 1, d["cT1"], d["L1_wmod"], d["mod1"], d["rows1"], [GA, GB])
            prog.meet()
        with ExitStack() as stack:
            sb = allocator(stack)
            b0 = Block0(prog, sb, const, Ring(banks[0:3]), d)
            b1 = Block1(prog, sb, const, Ring(banks[3:8]), d)
            b0.setup()
            b1.setup()
            prog.meet()
            for _ in b0.batch(0):
                pass
            prog.meet()
            with nc.Fori(0, B - 1) as i:
                interleave((b0.batch(i + 1), 75), (b1.batch(i), 185))
                prog.meet()
            for _ in b1.batch(B - 1):
                pass
            prog.meet()
        with ExitStack() as stack:
            ex = Experts(prog, allocator(stack), const, banks, d)
            ex.load_weights()
            ex.choose()
            prog.meet()
            with nc.Fori(0, B) as i:
                ex.batch(i)
                prog.meet()
            for s in ex.wsem:
                nc.sync.wait_ge(s, 32)


_DIRECT = ["L0_attn_x", "L0_attn_b_qkv", "L0_attn_b_out", "L0_ffn_cn_w1", "L0_ffn_cn_b1", "L0_ffn_cn_w2",
           "L0_ffn_cn_b2", "L0_ffn_cn_w3", "L0_ffn_cn_b3", "L0_ffn_cn_w4", "L0_ffn_cn_b4", "L0_ffn_gc_w1",
           "L0_ffn_gc_b1", "L0_ffn_gc_w2", "L0_ffn_gc_b2", "L0_ffn_gc_w3", "L0_ffn_gc_b3", "L0_ffn_adaptive_range",
           "L0_wmod", "L1_ffn_w1", "L1_ffn_w2", "L1_wmod"]
_TURNED = {"w_qkv0": "L0_attn_W_qkv", "w_out0": "L0_attn_W_out", "w_qkv1": "L1_attn_W_qkv", "w_out1": "L1_attn_W_out",
           "w_gate": "L1_ffn_gate_w", "cT0": "L0_c", "cT1": "L1_c"}


def kernel(**inputs):
    import numpy as np
    import concourse.bacc as bacc
    from concourse.bass_utils import run_bass_kernel_spmd

    nc = bacc.Bacc("TRN2", target_bir_lowering=False, num_devices=1)
    arrays = {n: np.ascontiguousarray(inputs[n]) for n in _DIRECT}
    arrays.update({n: np.ascontiguousarray(np.asarray(inputs[m]).T) for n, m in _TURNED.items()})
    d = {n: nc.dram_tensor(n, x.shape, F32, kind="ExternalInput").ap() for n, x in arrays.items()}
    d["out"] = nc.dram_tensor("out", (B, T, D), F32, kind="ExternalOutput").ap()
    program(nc, d)
    r = run_bass_kernel_spmd(nc, [arrays], core_ids=[0])
    return r.results[0]["out"]
```

```python
import concourse.bass as bass
from concourse import mybir

F32 = mybir.dt.float32
BF16 = mybir.dt.bfloat16
I32 = mybir.dt.int32
ALU = mybir.AluOpType
ACT = mybir.ActivationFunctionType
AX = mybir.AxisListType

P = 128
B, T, D = 8, 512, 256
NT = T // P
KC = D // P
EPS = 1e-5
H0, HD0, LB = 16, 16, 64
NBLK = T // LB
NR = P // 32
H1, HD1 = 8, 64
NHP = H1 // 2
CH1 = H1 * HD1
E, F = 8, 1024
FC = F // P
CAP = 2 * T // E
NEG = -1e30
CYCLES = 3
N0, N1, NTAIL = 64, 153, 20
SA, CA, GA, SB, CB, GB = (KC * i for i in range(6))
NMOD = 6 * KC


class Line:

    def __init__(self, prog, eng, name):
        self.prog, self.eng, self.name = prog, eng, name
        self.sem = prog.nc.alloc_semaphore(name + "_done")
        self.restart()

    def restart(self):
        self.n, self.seen = 0, {}

    def wait(self, *marks):
        for m in marks:
            if m is None or m[2] != self.prog.epoch:
                continue
            sem, value, _ = m
            if self.seen.get(sem.name, 0) < value:
                self.eng.wait_ge(sem, value)
                self.seen[sem.name] = value

    def mark(self, instruction):
        self.n += 1
        instruction.then_inc(self.sem, 1)
        return (self.sem, self.n, self.prog.epoch)


class DmaSem:

    def __init__(self, prog, name):
        self.prog, self.n = prog, 0
        self.sem = prog.nc.alloc_semaphore(name)
        prog.dma_sems.append(self)

    def mark(self, instruction):
        self.n += 16
        instruction.then_inc(self.sem, 16)
        return (self.sem, self.n, self.prog.epoch)

    def last(self):
        return (self.sem, self.n, self.prog.epoch) if self.n else None


class Program:
    def __init__(self, nc):
        self.nc, self.epoch, self.dma_sems = nc, 0, []
        self.pe = Line(self, nc.tensor, "pe")
        self.act = Line(self, nc.scalar, "act")
        self.dve = Line(self, nc.vector, "dve")
        self.pool = Line(self, nc.gpsimd, "pool")
        self.sp = Line(self, nc.sync, "sp")
        self.lines = [self.pe, self.act, self.dve, self.pool]

    def meet(self):
        for d in self.dma_sems:
            self.sp.wait(d.last())
        self.nc.all_engine_barrier()
        for x in self.lines + self.dma_sems:
            self.nc.sync.sem_clear(x.sem)
        self.nc.all_engine_barrier()
        for x in self.lines:
            x.restart()
        for d in self.dma_sems:
            d.n = 0
        self.sp.restart()
        self.epoch += 1


class Bank:

    def __init__(self, nc, name):
        self.t = nc.alloc_psum_tensor(name, [P, 512], F32)
        self.free = []

    def __getitem__(self, key):
        return self.t[key]


class Ring:
    def __init__(self, banks):
        self.banks, self.n = banks, -1

    def take(self, pe):
        self.n += 1
        b = self.banks[self.n % len(self.banks)]
        pe.wait(*b.free)
        b.free = []
        return b


def interleave(*threads):
    live = [[g, n, span, 0] for g, n, span in threads]
    while live:
        x = min(live, key=lambda x: x[3] / x[1] * x[2])
        x[3] += 1
        try:
            next(x[0])
        except StopIteration:
            live.remove(x)


class Arena:

    def __init__(self, nc, at, end):
        self.nc, self.at, self.end = nc, (at + 31) // 32 * 32, end

    def __call__(self, name, shape, dtype=F32):
        size = 2 if dtype == BF16 else 4
        for n in shape[1:]:
            size *= n
        t = self.nc.alloc_sbuf_tensor_at(name, shape, dtype, offset=self.at)
        self.at += (size + 31) // 32 * 32
        assert self.at <= self.end, (name, self.at, self.end)
        return t



class Norm:

    def __init__(self, prog, sb, name, power):
        self.p, self.power = prog, power
        self.stats = sb(name + "_stats", [P, NT, 6])
        self.mv = sb(name + "_mv", [P, NT, 2])
        self.rstd = sb(name + "_rstd", [P, NT])
        self.xn = sb(name + "_xn", [P, NT, D])

    def tokens(self, x, ready, xn_free):
        dve = self.p.dve
        v = dve.eng
        dve.wait(*ready)
        for t in range(NT):
            m = dve.mark(v.bn_stats(self.stats[:, t, :], x[:, t, :]))
        dve.wait(m)
        for t in range(NT):
            m = dve.mark(v.bn_aggr(self.mv[:, t, :], self.stats[:, t, :]))
        pool = self.p.pool
        pool.wait(m)
        m = pool.mark(pool.eng.tensor_scalar(self.rstd[:, :], self.mv[:, :, 1], EPS, None, ALU.add))
        pool.wait(m)
        m = pool.mark(pool.eng.tensor_tensor(self.rstd[:, :], self.rstd[:, :], self.power[:, :], ALU.pow))
        dve.wait(m, *xn_free)
        return [dve.mark(v.tensor_scalar(self.xn[:, t, :], x[:, t, :], self.mv[:, t, 0:1], self.rstd[:, t:t + 1],
                                         ALU.subtract, ALU.mult)) for t in range(NT)]

    def features(self, ring, ident, xn_done, hT, hT_free, mod, shift, scale, accum=None):
        pe, act = self.p.pe, self.p.act
        marks = []
        for c in range(KC):
            bank = ring.take(pe)
            for t in range(NT):
                pe.wait(xn_done[t])
                mm = pe.eng.transpose(bank[:, t * P:(t + 1) * P], self.xn[:, t, c * P:(c + 1) * P], ident[:, :])
            done = pe.mark(mm)
            act.wait(done, *hT_free)
            extra = {} if accum is None else {"accum_out": accum[:, c:c + 1]}
            m = act.mark(act.eng.activation(hT[:, c, :], bank[:, :], ACT.Identity, bias=mod[:, shift + c:shift + c + 1],
                                            scale=mod[:, scale + c:scale + c + 1], **extra))
            bank.free = [m]
            marks.append(m)
        return marks



class Constants:
    def __init__(self, prog, sb):
        nc, pool, dve = prog.nc, prog.pool, prog.dve
        g = pool.eng
        self.ident = sb("ident", [P, P])
        self.identb = sb("identb", [P, P], BF16)
        self.negL = sb("negL", [P, P], BF16)
        self.negS = sb("negS", [P, P], BF16)
        self.fold = sb("fold", [P, LB])
        self.iota_i = sb("iota_i", [P, P], I32)
        self.iota = sb("iota", [P, P])
        self.parity = sb("parity", [P, 2])
        self.group = sb("group", [P, P // HD0])
        self.sign = sb("sign", [P, 1])
        self.ones = sb("ones", [1, P])
        self.power = sb("power", [P, NT])

        def select(out, compare, fill, base, step, n, mult, after):
            pool.wait(after)
            return pool.mark(g.affine_select(out=out, in_=out, compare_op=compare, fill=fill, base=base,
                                             pattern=[[step, n]], channel_multiplier=mult))

        done = []
        m = pool.mark(g.memset(self.ident[:, :], 0.0))
        i1 = select(self.ident[:, :], ALU.not_equal, 1.0, 0, -1, P, 1, m)
        m = pool.mark(g.memset(self.negL[:, :], 0.0))
        done.append(select(self.negL[:, :], ALU.is_gt, NEG, 0, -1, P, 1, m))
        m = pool.mark(g.memset(self.negS[:, :], 0.0))
        done.append(select(self.negS[:, :], ALU.is_ge, NEG, 0, -1, P, 1, m))
        m = pool.mark(g.memset(self.fold[:, :], 0.0))
        m = select(self.fold[:, :], ALU.not_equal, 1.0, 0, -1, LB, 1, m)
        done.append(select(self.fold[:, :], ALU.not_equal, 1.0, -LB, -1, LB, 1, m))
        m = pool.mark(g.iota(self.iota_i[:, :], pattern=[[1, P]], base=0, channel_multiplier=0))
        m0 = pool.mark(g.memset(self.group[:, :], float(HD0) ** -0.5))
        m0 = select(self.group[:, :], ALU.is_ge, 0.0, 0, -HD0, P // HD0, 1, m0)
        m0 = select(self.group[:, :], ALU.is_ge, 0.0, HD0 - 1, HD0, P // HD0, -1, m0)
        m1 = pool.mark(g.memset(self.sign[:, :], 1.0))
        done.append(select(self.sign[:, :], ALU.is_ge, -1.0, P // 2 - 1, 0, 1, -1, m1))
        done.append(pool.mark(g.memset(self.ones[:, :], 1.0)))
        done.append(pool.mark(g.memset(self.power[:, :], -0.5)))
        v = dve.eng
        dve.wait(i1, m, m0)
        v.tensor_copy(self.identb[:, :], self.ident[:, :])
        v.tensor_copy(self.iota[:, :], self.iota_i[:, :])
        m2 = dve.mark(v.tensor_reduce(self.parity[:, :], self.group[:, :].rearrange("p (g a) -> p a g", a=2), AX.X,
                                      ALU.add))
        self.ready = done + [i1, m2]


def modulation(prog, ring, sb, layer, w, cT_d, wmod_d, mod_d, rows_d, row_kinds):
    pe, act, dve, sp = prog.pe, prog.act, prog.dve, prog.sp
    v = dve.eng
    n = f"m{layer}"
    cT = sb(n + "cT", [P, KC, B])
    th = sb(n + "th", [P, KC, B])
    sil = sb(n + "sil", [P, KC, B])
    cols = sb(n + "cols", [P, B, NMOD])
    size = sb(n + "size", [P, B, NMOD])
    rows = sb(n + "rows", [B, len(row_kinds) * D])
    rsize = sb(n + "rsize", [B, len(row_kinds) * D])
    dc, dw = DmaSem(prog, n + "_c_in"), DmaSem(prog, n + "_w_in")
    dm, dr = DmaSem(prog, n + "_cols_out"), DmaSem(prog, n + "_rows_out")
    c_in = dc.mark(sp.eng.dma_start(cT[:, :, :], cT_d.rearrange("(k p) b -> p k b", p=P)))
    w_in = dw.mark(sp.eng.dma_start(w, wmod_d.rearrange("(k p) n -> p k n", p=P)))
    act.wait(c_in)
    m = act.mark(act.eng.activation(th[:, :, :], cT[:, :, :], ACT.Tanh, scale=0.5))
    dve.wait(m, c_in)
    m = dve.mark(v.scalar_tensor_tensor(out=th[:, :, :], in0=th[:, :, :], scalar=1.0, in1=cT[:, :, :], op0=ALU.add,
                                        op1=ALU.mult))
    dve.wait(m)
    sil_done = dve.mark(v.tensor_scalar(sil[:, :, :], th[:, :, :], 0.5, None, ALU.mult))
    pe.wait(sil_done, w_in)
    bank = ring.take(pe)
    for j in range(NMOD):
        for k in range(KC):
            mm = pe.eng.matmul(bank[:, j * B:(j + 1) * B], w[:, k, j * P:(j + 1) * P], sil[:, k, :], start=(k == 0),
                               stop=(k == KC - 1))
    m = pe.mark(mm)
    dve.wait(m)
    m = dve.mark(v.tensor_copy(cols[:, :, :], bank[:, 0:NMOD * B].rearrange("p (j b) -> p b j", b=B)))
    bank.free = [m]
    dve.wait(m)
    for j in (CA, CB):
        m = dve.mark(v.tensor_scalar(cols[:, :, j:j + KC], cols[:, :, j:j + KC], 1.0, None, ALU.add))

    def gate(g, size):
        m = dve.mark(v.scalar_tensor_tensor(out=size, in0=g, scalar=-1.0, in1=g, op0=ALU.mult, op1=ALU.max))
        dve.wait(m)
        v.tensor_scalar(size, size, 0.25, None, ALU.max)
        m = dve.mark(v.tensor_scalar(g, g, 0.0, 2.0, ALU.is_ge, ALU.mult))
        dve.wait(m)
        return dve.mark(v.scalar_tensor_tensor(out=g, in0=g, scalar=-1.0, in1=size, op0=ALU.add, op1=ALU.mult))

    for j in (GA, GB):
        m = gate(cols[:, :, j:j + KC], size[:, :, j:j + KC])
    sp.wait(m)
    out = [dm.mark(sp.eng.dma_start(mod_d.rearrange("b p n -> p b n"), cols[:, :, :]))]
    for i, j in enumerate(row_kinds):
        bank = ring.take(pe)
        for k in range(KC):
            mm = pe.eng.matmul(bank[0:B, 0:D], sil[:, k, :], w[:, k, j * P:j * P + D], start=(k == 0),
                               stop=(k == KC - 1))
        m = rows_read = pe.mark(mm)
        dve.wait(m)
        m = dve.mark(v.tensor_copy(rows[:, i * D:(i + 1) * D], bank[0:B, 0:D]))
        bank.free = [m]
    dve.wait(m)
    m = gate(rows[:, :], rsize[:, :])
    sp.wait(m)
    out.append(dr.mark(sp.eng.dma_start(rows_d, rows[:, :])))
    return out, rows_read



class Block0:
    def __init__(self, prog, sb, const, ring, d):
        self.p, self.const, self.ring, self.d = prog, const, ring, d
        self.wqkv = sb("wqkv0", [P, KC, 3 * D])
        self.wout = sb("wout0", [P, KC, D])
        self.bq = sb("bq", [P, KC])
        self.bqp = sb("bqp", [P, KC, 2])
        self.bk = sb("bk", [P, KC])
        self.bv = sb("bv", [P, KC])
        self.bout = sb("bout", [1, D])
        self.w1 = sb("cw1", [P, KC, D])
        self.w2 = sb("cw2", [P, KC, P])
        self.w3 = sb("cw3", [P, 64])
        self.w4c = sb("cw4c", [64, 1])
        self.w4 = sb("cw4", [64, P])
        self.b1 = sb("cb1", [P, KC])
        self.b2 = sb("cb2", [P, 1])
        self.b3 = sb("cb3", [64, 1])
        self.b4 = sb("cb4", [P, 1])
        self.g1 = sb("gw1", [P, KC, P])
        self.g2 = sb("gw2", [P, 64])
        self.g3c = sb("gw3c", [64, 1])
        self.g3 = sb("gw3", [64, P])
        self.gb1 = sb("gb1", [P, 1])
        self.gb2 = sb("gb2", [64, 1])
        self.gb3 = sb("gb3", [P, 1])
        self.ar = sb("ar", [P, 1])
        self.sar = sb("sar", [P, 3])
        self.x = sb("x0", [P, NT, D])
        self.mod = sb("mod0", [P, NMOD])
        self.ga = sb("ga0", [P, D])
        self.mod_next = sb("mod0n", [P, NMOD])
        self.norm = Norm(prog, sb, "n0", const.power)
        self.tmp = self.norm.xn[:, 0:2, :]
        self.hT = sb("hT0", [P, KC, T])
        self.q = sb("q0", [P, KC, NBLK, 2, LB])
        self.k = sb("k0", [P, KC, NBLK, NR, LB])
        self.v = sb("v0", [P, NBLK, NR, 66])
        self.mx = [sb(f"mx0{i}", [P, NR * KC]) for i in range(2)]
        self.s = [sb(f"s0{i}", [P, NR, KC, LB]) for i in range(2)]
        self.pT = [sb(f"pT0{i}", [P, NR, P]) for i in range(2)]
        self.ri = [sb(f"ri0{i}", [P, NR, KC]) for i in range(2)]
        self.o = [sb(f"o0{i}", [P, KC, NR, 2, HD0]) for i in range(2)]
        self.sum = sb("sum0", [P, KC])
        self.gf = sb("gf", [P, 4])
        self.a1 = sb("a1", [P, KC, T])
        self.aT = self.a1
        self.a2 = sb("a2", [P, T])
        self.a3 = sb("a3", [64, T])
        self.tf = sb("tf", [P, T])
        names = ["x", "mod", "modn", "ga", "xout"]
        self.dma = {n: DmaSem(prog, f"b0_{n}") for n in names}
        self.dw = [DmaSem(prog, f"b0_w{i}") for i in range(2)]

    def setup(self):
        p, d = self.p, self.d
        nc, sp, dve, act = p.nc, p.sp, p.dve, p.act
        v = dve.eng
        e, dw = (act.eng, self.dw[0])

        def load(dst, src):
            return dw.mark(e.dma_start(dst, src))

        load(self.wqkv[:, :, :], d["w_qkv0"].rearrange("(k p) n -> p k n", p=P))
        bq = d["L0_attn_b_qkv"].rearrange("(a k p) -> a p k", p=P, k=KC)
        with nc.allow_non_contiguous_dma(reason="bias columns"):
            load(self.bq[:, :], bq[0])
            load(self.bk[:, :], bq[1])
            load(self.bv[:, :], bq[2])
            load(self.b1[:, :], d["L0_ffn_cn_b1"].rearrange("(k p) -> p k", p=P))
            load(self.b2[:, :], d["L0_ffn_cn_b2"].rearrange("(p a) -> p a", a=1))
            load(self.b3[:, :], d["L0_ffn_cn_b3"].rearrange("(p a) -> p a", a=1))
            load(self.gb1[:, :], d["L0_ffn_gc_b1"].rearrange("(p a) -> p a", a=1))
            load(self.gb2[:, :], d["L0_ffn_gc_b2"].rearrange("(p a) -> p a", a=1))
            load(self.b4[:, :], d["L0_ffn_cn_b4"].partition_broadcast(P))
            load(self.gb3[:, :], d["L0_ffn_gc_b3"].partition_broadcast(P))
            load(self.ar[:, :], d["L0_ffn_adaptive_range"].partition_broadcast(P))
            load(self.w4c[:, :], d["L0_ffn_cn_w4"])
            load(self.g3c[:, :], d["L0_ffn_gc_w3"])
        load(self.wout[:, :, :], d["w_out0"].rearrange("(k p) n -> p k n", p=P))
        load(self.bout[:, :], d["L0_attn_b_out"].rearrange("(a n) -> a n", a=1))
        load(self.w1[:, :, :], d["L0_ffn_cn_w1"].rearrange("(k p) n -> p k n", p=P))
        load(self.w2[:, :, :], d["L0_ffn_cn_w2"].rearrange("(k p) n -> p k n", p=P))
        load(self.w3[:, :], d["L0_ffn_cn_w3"])
        load(self.g1[:, :, :], d["L0_ffn_gc_w1"].rearrange("(k p) n -> p k n", p=P))
        loaded = load(self.g2[:, :], d["L0_ffn_gc_w2"])
        pool = p.pool
        g = pool.eng
        m = pool.mark(g.memset(self.v[:, :, :, :], 0.0))
        m0 = pool.mark(g.memset(self.k[:, :, :, :, :], 0.0))
        for o in self.o:
            m0 = pool.mark(g.memset(o[:, :, :, :, :], 0.0))
        dve.wait(m)
        for c in range(KC):
            v.memset(self.v[64 * c:64 * c + 64, :, :, 64 + c:65 + c], 1.0)
        dve.wait(loaded, *self.const.ready)
        v.tensor_copy(self.w4[:, :], self.w4c[:, 0:1].to_broadcast([64, P]))
        v.tensor_copy(self.g3[:, :], self.g3c[:, 0:1].to_broadcast([64, P]))
        for c in range(KC):
            v.tensor_scalar(self.bqp[:, c, :], self.const.parity[:, :], self.bq[:, c:c + 1], None, ALU.mult)
        v.tensor_scalar(self.b4[:, :], self.b4[:, :], 0.5, None, ALU.mult)
        v.tensor_scalar(self.gb3[:, :], self.gb3[:, :], 0.5, None, ALU.mult)
        m = dve.mark(v.tensor_tensor(self.ar[:, :], self.ar[:, :], self.const.sign[:, :], ALU.mult))
        dve.wait(m)
        v.tensor_scalar(self.sar[:, 0:1], self.ar[:, :], 0.3, None, ALU.mult)
        v.tensor_scalar(self.sar[:, 1:2], self.ar[:, :], 0.7, None, ALU.mult)
        return [loaded, m0,
                dve.mark(v.tensor_scalar(self.sar[:, 2:3], self.const.sign[:, :], 0.1, None, ALU.mult))]

    def batch(self, b, b1):
        p, ring, const, d = self.p, self.ring, self.const, self.d
        pe, act, dve, sp = p.pe, p.act, p.dve, p.sp
        v, a, te = dve.eng, act.eng, pe.eng
        one = bass.ds(b, 1)
        x, hT = self.x, self.hT
        x_in = self.dma["x"].mark(sp.eng.dma_start(
            x[:, :, :], d["L0_attn_x"][one, :, :].rearrange("b (t p) n -> p (b t) n", p=P)))
        mod_in = self.dma["mod"].mark(sp.eng.dma_start(
            self.mod[:, :], d["mod0"][one, :, :].rearrange("b p n -> p (b n)")))
        modn_in = self.dma["modn"].mark(sp.eng.dma_start(
            self.mod_next[:, :], d["mod1"][one, :, :].rearrange("b p n -> p (b n)")))
        ga_in = self.dma["ga"].mark(sp.eng.dma_start(
            self.ga[:, :], d["rows0"][one, :].rearrange("b n -> (b n)").partition_broadcast(P)))
        yield
        xn = self.norm.tokens(x, [x_in], [])
        yield
        act.wait(mod_in)
        h = self.norm.features(ring, const.ident, xn, hT, [], self.mod, SA, CA)
        yield
        kdone, qdone, vdone = [], [], []
        for c in range(KC):
            bank = ring.take(pe)
            pe.wait(*h)
            for k in range(KC):
                mm = te.matmul(bank[:, :], self.wqkv[:, k, D + c * P:D + (c + 1) * P], hT[:, k, :], start=(k == 0),
                               stop=(k == KC - 1))
            m = pe.mark(mm)
            act.wait(m)
            for r in range(NR):
                rows = slice(32 * r, 32 * r + 32)
                m = act.mark(a.activation(self.k[rows, c, :, r, :], bank[rows, :].rearrange("p (n m) -> p n m", m=LB),
                                          ACT.Identity, bias=self.bk[rows, c:c + 1]))
            bank.free = [m]
            kdone = [m]
            bank = ring.take(pe)
            for k in range(KC):
                mm = te.matmul(bank[:, :], self.wqkv[:, k, c * P:(c + 1) * P], hT[:, k, :], start=(k == 0),
                               stop=(k == KC - 1))
            m = pe.mark(mm)
            dve.wait(m)
            for par in range(2):
                m = dve.mark(v.tensor_scalar(self.q[:, c, :, par, :], bank[:, :].rearrange("p (n l) -> p n l", l=LB),
                                             const.parity[:, par:par + 1], self.bqp[:, c, par:par + 1], ALU.mult,
                                             ALU.add))
            bank.free = [m]
            qdone = [m]
            yield
        for half in range(2):
            bank = ring.take(pe)
            for n in range(4):
                blk = 4 * half + n
                for c in range(KC):
                    for k in range(KC):
                        mm = te.matmul(bank[64 * c:64 * c + 64, n * P:(n + 1) * P], hT[:, k, blk * LB:(blk + 1) * LB],
                                       self.wqkv[:, k, 2 * D + c * P:2 * D + (c + 1) * P], start=(k == 0),
                                       stop=(k == KC - 1))
            m = pe.mark(mm)
            for c in range(KC):
                rows = slice(64 * c, 64 * c + 64)
                line, copy = (act, a.copy) if c else (dve, v.tensor_copy)
                line.wait(m)
                vdone.append(line.mark(copy(self.v[rows, 4 * half:4 * half + 4, :, 32 * c:32 * c + 32],
                                            bank[rows, :].rearrange("p (n r e) -> p n r e", n=4, r=NR))))
            bank.free = vdone[-2:]
            yield
        sdone, exped, tdone, odone, adone = {}, {}, {}, {}, {}
        ptr_free, o_free, s_free = {}, {}, {}

        def scores(n):
            bank = ring.take(pe)
            pe.wait(*kdone, *qdone)
            for c in range(KC):
                mm = te.matmul(bank[:, c * 256:(c + 1) * 256], self.q[:, c, n, :, :].rearrange("p a l -> p (a l)"),
                               self.k[:, c, n, :, :].rearrange("p r m -> p (r m)"), start=True, stop=True)
            m = pe.mark(mm)
            view = bank[:, :].rearrange("p (c r m) -> p c r m", c=KC, r=NR)
            s, mx = self.s[n % 2], self.mx[n % 2]
            dve.wait(m)
            m = dve.mark(v.tensor_reduce(mx[:, :], bank[:, :].rearrange("p (g m) -> p g m", m=LB), AX.X, ALU.max))
            dve.wait(m, s_free.get(n - 2))
            m = dve.mark(v.tensor_tensor(s[:, :, :, :].rearrange("p r c m -> p c r m"), view,
                                         mx[:, :].rearrange("p (c r) -> p c r", c=KC).unsqueeze(3)
                                         .to_broadcast([P, KC, NR, LB]), ALU.subtract))
            bank.free = [m]
            act.wait(m)
            exped[n] = act.mark(a.activation(s[:, :, :, :], s[:, :, :, :], ACT.Exp))

        def turn(n):
            bank = ring.take(pe)
            pe.wait(exped[n])
            for r in range(NR):
                mm = te.transpose(bank[:, r * P:(r + 1) * P],
                                  self.s[n % 2][:, r, :, :].rearrange("p c m -> p (c m)"), const.ident[:, :])
            m = pe.mark(mm)
            s_free[n] = m
            act.wait(m, ptr_free.get(n - 2))
            tdone[n] = act.mark(a.copy(self.pT[n % 2][:, :, :], bank[:, :].rearrange("p (r l) -> p r l", r=NR)))
            bank.free = [tdone[n]]

        def values(n):
            bank = ring.take(pe)
            pe.wait(tdone[n], *vdone)
            for r in range(NR):
                mm = te.matmul(bank[:, r * 66:(r + 1) * 66], self.pT[n % 2][:, r, :], self.v[:, n, r, :], start=True,
                               stop=True)
            m = pe.mark(mm)
            ptr_free[n] = m
            view = bank[:, 0:NR * 66].rearrange("p (r e) -> p r e", r=NR)
            ri, o = self.ri[n % 2], self.o[n % 2]
            dve.wait(m)
            m = dve.mark(v.reciprocal(ri[:, :, :], view[:, :, 64:66]))
            dve.wait(m, o_free.get(n - 2))
            for par in range(2):
                rows = slice(64 * par, 64 * par + 64)
                for c in range(KC):
                    m = dve.mark(v.tensor_tensor(
                        o[rows, c, :, par, :], view[rows, :, 32 * c + 16 * par:32 * c + 16 * par + 16],
                        ri[rows, :, c:c + 1].to_broadcast([64, NR, HD0]), ALU.mult))
            bank.free = [m]
            odone[n] = m

        def gather(n):
            bank = ring.take(pe)
            pe.wait(odone[n])
            for c in range(KC):
                mm = te.matmul(bank[:, c * LB:(c + 1) * LB], self.o[n % 2][:, c, :, :, :].rearrange("p r a e -> p (r a e)"),
                               const.fold[:, :], start=True, stop=True)
            m = pe.mark(mm)
            o_free[n] = m
            act.wait(m)
            for c in range(KC):
                m = act.mark(a.activation(self.aT[:, c, n * LB:(n + 1) * LB], bank[:, c * LB:(c + 1) * LB],
                                          ACT.Identity, bias=self.bv[:, c:c + 1]))
            bank.free = [m]
            adone[n] = m

        for n in range(NBLK + 3):
            if n < NBLK:
                scores(n)
                yield
            if 0 <= n - 1 < NBLK:
                turn(n - 1)
                yield
            if 0 <= n - 2 < NBLK:
                values(n - 2)
                yield
            if 0 <= n - 3 < NBLK:
                gather(n - 3)
                yield
        xdone = []
        dve.wait(ga_in)
        for pair in range(NT // 2):
            bank = ring.take(pe)
            pe.wait(adone[NBLK - 1])
            for i in range(2):
                t = 2 * pair + i
                out = bank[:, i * D:(i + 1) * D]
                for k in range(KC):
                    te.matmul(out, self.aT[:, k, t * P:(t + 1) * P], self.wout[:, k, :], start=(k == 0), stop=False)
                mm = te.matmul(out, const.ones[:, :], self.bout[:, :], start=False, stop=True)
            m = pe.mark(mm)
            dve.wait(m, *xdone)
            m = dve.mark(v.tensor_tensor(self.tmp, bank[:, :].rearrange("p (i n) -> p i n", i=2),
                                         self.ga[:, :].unsqueeze(1).to_broadcast([P, 2, D]), ALU.mult))
            bank.free = [m]
            dve.wait(m)
            xt = x[:, 2 * pair:2 * pair + 2, :]
            xdone = [dve.mark(v.tensor_tensor(xt, xt, self.tmp, ALU.add))]
            yield
        xn = self.norm.tokens(x, xdone, h)
        yield
        out = self.norm.features(ring, const.ident, xn, hT, [], self.mod, SB, CB, accum=self.sum)
        yield
        bank = ring.take(pe)
        pe.wait(*out)
        for k in range(KC):
            mm = te.matmul(bank[:, 0:1], self.g1[:, k, :], self.sum[:, k:k + 1], start=(k == 0), stop=(k == KC - 1))
        m = pe.mark(mm)
        act.wait(m)
        m = act.mark(a.activation(self.gf[:, 0:1], bank[:, 0:1], ACT.Gelu, bias=self.gb1[:, :], scale=1.0 / T))
        bank.free = [m]
        yield
        bank = ring.take(pe)
        pe.wait(m)
        m = pe.mark(te.matmul(bank[0:64, 0:1], self.g2[:, :], self.gf[:, 0:1], start=True, stop=True))
        act.wait(m)
        m = act.mark(a.activation(self.gf[0:64, 1:2], bank[0:64, 0:1], ACT.Gelu, bias=self.gb2[:, :]))
        bank.free = [m]
        yield
        bank = ring.take(pe)
        pe.wait(m)
        m = pe.mark(te.matmul(bank[:, 0:1], self.g3[:, :], self.gf[0:64, 1:2], start=True, stop=True))
        act.wait(m)
        m = act.mark(a.activation(self.gf[:, 2:3], bank[:, 0:1], ACT.Tanh, bias=self.gb3[:, :], scale=0.5))
        bank.free = [m]
        dve.wait(m)
        base = dve.mark(v.tensor_scalar(self.gf[:, 3:4], self.gf[:, 2:3], self.sar[:, 1:2], self.sar[:, 2:3], ALU.mult,
                                        ALU.add))
        yield
        tdone2, csdone = [], []
        for cycle in range(CYCLES):
            l1 = []
            for c in range(KC):
                bank = ring.take(pe)
                pe.wait(*out)
                for k in range(KC):
                    mm = te.matmul(bank[:, :], self.w1[:, k, c * P:(c + 1) * P], hT[:, k, :], start=(k == 0),
                                   stop=(k == KC - 1))
                m = pe.mark(mm)
                act.wait(m)
                m = act.mark(a.activation(self.a1[:, c, :], bank[:, :], ACT.Gelu, bias=self.b1[:, c:c + 1]))
                bank.free = [m]
                l1.append(m)
                yield
            bank = ring.take(pe)
            pe.wait(*l1)
            for k in range(KC):
                mm = te.matmul(bank[:, :], self.w2[:, k, :], self.a1[:, k, :], start=(k == 0), stop=(k == KC - 1))
            m = pe.mark(mm)
            act.wait(m)
            m = act.mark(a.activation(self.a2[:, :], bank[:, :], ACT.Gelu, bias=self.b2[:, :]))
            bank.free = [m]
            yield
            bank = ring.take(pe)
            pe.wait(m)
            m = pe.mark(te.matmul(bank[0:64, :], self.w3[:, :], self.a2[:, :], start=True, stop=True))
            act.wait(m)
            m = act.mark(a.activation(self.a3[:, :], bank[0:64, :], ACT.Gelu, bias=self.b3[:, :]))
            bank.free = [m]
            yield
            bank = ring.take(pe)
            pe.wait(m)
            m = pe.mark(te.matmul(bank[:, :], self.w4[:, :], self.a3[:, :], start=True, stop=True))
            act.wait(m, *csdone)
            m = act.mark(a.activation(self.tf[:, :], bank[:, :], ACT.Tanh, bias=self.b4[:, :], scale=0.5))
            bank.free = [m]
            dve.wait(m, base)
            m = dve.mark(v.tensor_scalar(self.tf[:, :], self.tf[:, :], self.sar[:, 0:1], self.gf[:, 3:4], ALU.mult,
                                         ALU.add))
            dve.wait(m)
            dve.mark(v.tensor_tensor(self.a1[:, 0, :], self.tf[:, :], hT[:, 1, :], ALU.mult))
            m = dve.mark(v.tensor_tensor(self.a1[:, 1, :], self.tf[:, :], hT[:, 0, :], ALU.mult))
            csdone = [m]
            dve.wait(m)
            dve.mark(v.tensor_tensor(hT[:, 0, :], hT[:, 0, :], self.a1[:, 0, :], ALU.add))
            out = [dve.mark(v.tensor_tensor(hT[:, 1, :], hT[:, 1, :], self.a1[:, 1, :], ALU.subtract))]
            yield
        dve.wait(*out)
        for c in range(KC):
            m = dve.mark(v.tensor_scalar(hT[:, c, :], hT[:, c, :], self.mod[:, GB + c:GB + c + 1], None, ALU.mult))
        for pair in range(NT // 2):
            bank = ring.take(pe)
            pe.wait(m)
            for i in range(2):
                t = 2 * pair + i
                for c in range(KC):
                    mm = te.transpose(bank[:, i * D + c * P:i * D + (c + 1) * P], hT[:, c, t * P:(t + 1) * P],
                                      const.ident[:, :])
            md = pe.mark(mm)
            dve.wait(md)
            xt = x[:, 2 * pair:2 * pair + 2, :]
            md = dve.mark(v.tensor_tensor(xt, xt, bank[:, :].rearrange("p (i n) -> p i n", i=2), ALU.add))
            bank.free = [md]
        sp.wait(md)
        self.dma["xout"].mark(sp.eng.dma_start(d["x1"][one, :, :].rearrange("b (t p) n -> p (b t) n", p=P), x[:, :, :]))
        xn = self.norm.tokens(x, [md], [])
        yield
        act.wait(modn_in)
        self.norm.features(ring, const.ident, xn, b1.hT, [b1.last_projection], self.mod_next, SA, CA)
        yield



class Block1:
    def __init__(self, prog, sb, const, ring, d):
        self.p, self.const, self.ring, self.d = prog, const, ring, d
        self.wqkv = sb("wqkv1", [P, KC, 6 * CH1])
        self.wout = sb("wout1", [P, NHP, D])
        self.wgate = sb("wgate", [P, KC, E])
        self.x = sb("x1s", [P, NT, D])
        self.mod = sb("mod1", [P, NMOD])
        self.ga = sb("ga1", [P, D])
        self.norm = Norm(prog, sb, "n1", const.power)
        self.hT = sb("hT1", [P, KC, T])
        self.vc = sb("vc1", [P, NT, CH1])
        self.setup_at = sb.at
        self.f = [[sb(f"f1{i}{j}", [P, T]) for j in range(5)] for i in range(2)]
        w = P * NT * (NT + 1) // 2
        self.look = [sb(f"look{i}", [P, w]) for i in range(2)]
        self.term = [sb(f"term{i}", [P, w]) for i in range(2)]
        self.th = [sb(f"th1{i}", [P, T]) for i in range(2)]
        self.s = [sb(f"s1{i}", [P, T]) for i in range(2)]
        self.pT = [sb(f"pT1{i}", [P, T]) for i in range(2)]
        self.mx = [sb(f"mx1{i}", [P, 4]) for i in range(2)]
        self.o = [sb(f"o1{i}", [P, NT, P]) for i in range(2)]
        self.oT = sb("oT1", [P, NHP, T])
        self.tmp = self.norm.xn[:, 0:2, :]
        self.hTt = sb("hT1t", [P, KC, T])
        self.left = sb("left", [E, T])
        self.zero = sb("zero", [E, T])
        self.top = sb("top8", [E, 8])
        self.pos = sb("pos", [P, NT * E])
        self.last_projection = self.output_projection = None
        self.pr = sb("pr1", [P, NT, E])
        self.pm = sb("pm1", [P, NT, 3])
        self.prT = sb("prT1", [E, T])
        self.dma = {n: DmaSem(prog, f"b1_{n}") for n in ["x", "mod", "ga", "w", "xout", "xn", "pr", "pos"]}

    def setup(self, weights_read):
        e, d, dw = self.p.sp.eng, self.d, self.dma["w"]
        self.p.sp.wait(*weights_read)
        self.p.pool.mark(self.p.pool.eng.memset(self.zero[:, :], 0.0))
        dw.mark(e.dma_start(self.wqkv[:, :, :], d["w_qkv1"].rearrange("(k p) n -> p k n", p=P)))
        dw.mark(e.dma_start(self.wout[:, :, :], d["w_out1"].rearrange("(k p) n -> p k n", p=P)))
        dw.mark(e.dma_start(self.wgate[:, :, :], d["w_gate"].rearrange("(k p) n -> p k n", p=P)))

    def attention(self, b):
        p, ring, const = self.p, self.ring, self.const
        pe, act, dve, pool = p.pe, p.act, p.dve, p.pool
        v, a, te = dve.eng, act.eng, pe.eng
        hT = self.hT
        self.last_projection = None
        vcdone = []
        for t in range(NT):
            bank = ring.take(pe)
            for k in range(KC):
                mm = te.matmul(bank[:, :], hT[:, k, t * P:(t + 1) * P], self.wqkv[:, k, 5 * CH1:6 * CH1],
                               start=(k == 0), stop=(k == KC - 1))
            m = pe.mark(mm)
            act.wait(m)
            m = act.mark(a.copy(self.vc[:, t, :], bank[:, :]))
            bank.free = [m]
            vcdone = [m]
            yield
        SCALES = [HD1 ** -0.5, 1.0, 1.0, HD1 ** -0.5, 2.0]
        fdone, lookdone, lt_free = {}, {}, {}
        projections_free = {}

        def project(hp, j):
            bank = ring.take(pe)
            for k in range(KC):
                mm = te.matmul(bank[:, :], self.wqkv[:, k, j * CH1 + hp * P:j * CH1 + (hp + 1) * P], hT[:, k, :],
                               start=(k == 0), stop=(k == KC - 1))
            m = pe_done = pe.mark(mm)
            act.wait(m, projections_free.get(hp - 2))
            m = act.mark(a.mul(self.f[hp % 2][j][:, :], bank[:, :], SCALES[j]))
            bank.free = [m]
            fdone[hp] = m
            if (hp, j) == (NHP - 1, 4):
                self.last_projection = pe_done

        def off(j):
            return P * j * (j + 1) // 2

        def toff(j):
            return P * (j * NT - j * (j - 1) // 2)

        def lookahead(hd, j):
            rows = slice(64 * (hd % 2), 64 * (hd % 2) + 64)
            qu, ku, vu, qc, _ = self.f[hd // 2 % 2]
            look, term = self.look[hd % 2], self.term[hd % 2]
            w = (j + 1) * P
            bank = ring.take(pe)
            pe.wait(fdone[hd // 2])
            te.matmul(bank[:, 0:w], ku[rows, j * P:(j + 1) * P], qu[rows, 0:w], start=True, stop=False)
            m = pe.mark(te.matmul(bank[:, j * P:w], const.identb[:, :], const.negL[:, :], start=False, stop=True))
            act.wait(m, lt_free.get(hd - 2))
            dst = look[:, off(j):off(j) + w]
            m = act.mark(a.activation(dst, bank[:, 0:w], ACT.Tanh, scale=0.5))
            bank.free = [m]
            pool.wait(m)
            pool.mark(pool.eng.tensor_scalar(dst, dst, 0.5, 0.5, ALU.mult, ALU.add))
            bank = ring.take(pe)
            w = T - j * P
            m = pe.mark(te.matmul(bank[:, 0:w], vu[rows, j * P:(j + 1) * P], qc[rows, j * P:T], start=True, stop=True))
            dve.wait(m, lt_free.get(hd - 2))
            m = dve.mark(v.tensor_copy(term[:, toff(j):toff(j) + w], bank[:, 0:w]))
            bank.free = [m]
            pool.wait(m)
            diagonal = term[:, toff(j):toff(j) + P]
            lookdone[hd] = pool.mark(pool.eng.affine_select(
                out=diagonal, in_=diagonal, compare_op=ALU.is_ge, fill=0.0, base=0, pattern=[[1, P]],
                channel_multiplier=-1))

        expdone, pTdone, ridone, th_free, pT_free = {}, {}, {}, {}, {}

        def scores(u):
            hd, i = u // NT, u % NT
            rows = slice(64 * (hd % 2), 64 * (hd % 2) + 64)
            _, _, _, qc, kc = self.f[hd // 2 % 2]
            look, term = self.look[hd % 2], self.term[hd % 2]
            w = (i + 1) * P
            su = ring.take(pe)
            pe.wait(lookdone[hd])
            for j in range(i, -1, -1):
                mm = te.matmul(su[:, 0:(j + 1) * P], term[:, toff(j) + (i - j) * P:toff(j) + (i - j + 1) * P],
                               look[:, off(j):off(j) + (j + 1) * P], start=(j == i), stop=(j == 0))
            su_done = pe.mark(mm)
            if i == NT - 1:
                lt_free[hd] = su_done
            sc = ring.take(pe)
            te.matmul(sc[:, 0:w], qc[rows, i * P:(i + 1) * P], kc[rows, 0:w], start=True, stop=False)
            sc_done = pe.mark(te.matmul(sc[:, i * P:w], const.identb[:, :], const.negS[:, :], start=False, stop=True))
            if hd % 2 and i == NT - 1:
                projections_free[hd // 2] = sc_done
            th, s, mx = self.th[u % 2], self.s[u % 2], self.mx[u % 2]
            act.wait(su_done, th_free.get(u - 2))
            m = act.mark(a.activation(th[:, 0:w], su[:, 0:w], ACT.Tanh, scale=0.5))
            dve.wait(m, su_done)
            m = dve.mark(v.scalar_tensor_tensor(out=th[:, 0:w], in0=th[:, 0:w], scalar=1.0, in1=su[:, 0:w],
                                                op0=ALU.add, op1=ALU.mult))
            su.free = [m]
            dve.wait(m, sc_done, pT_free.get(u - 2))
            m = dve.mark(v.tensor_tensor_reduce(s[:, 0:w], sc[:, 0:w], th[:, 0:w], 1.0, -3e38, ALU.subtract, ALU.max,
                                                mx[:, 0:1]))
            sc.free = [m]
            th_free[u] = m
            dve.wait(m)
            m = dve.mark(v.tensor_scalar(mx[:, 1:2], mx[:, 0:1], -0.5, None, ALU.mult))
            act.wait(m)
            expdone[u] = act.mark(a.activation(s[:, 0:w], s[:, 0:w], ACT.Exp, bias=mx[:, 1:2], scale=0.5,
                                               accum_out=mx[:, 2:3]))

        def turn(u):
            i = u % NT
            w = (i + 1) * P
            bank = ring.take(pe)
            pe.wait(expdone[u])
            for k in range(i + 1):
                mm = te.transpose(bank[:, k * P:(k + 1) * P], self.s[u % 2][:, k * P:(k + 1) * P], const.ident[:, :])
            m = pe.mark(mm)
            pT_free[u] = m
            dve.wait(m, ridone.get(u - 2), expdone[u])
            pTdone[u] = dve.mark(v.tensor_copy(self.pT[u % 2][:, 0:w], bank[:, 0:w]))
            bank.free = [pTdone[u]]
            dve.mark(v.reciprocal(self.mx[u % 2][:, 3:4], self.mx[u % 2][:, 2:3]))

        def attend(u):
            hd, i = u // NT, u % NT
            bank = ring.take(pe)
            pe.wait(pTdone[u], *vcdone)
            for k in range(i + 1):
                mm = te.matmul(bank[:, 0:HD1], self.pT[u % 2][:, k * P:(k + 1) * P],
                               self.vc[:, k, hd * HD1:(hd + 1) * HD1], start=(k == 0), stop=(k == i))
            m = pe.mark(mm)
            dve.wait(m, (dve.sem, pTdone[u][1] + 1, p.epoch), o_free.get(hd // 2 - 2))
            ridone[u] = dve.mark(v.tensor_scalar(self.o[hd // 2 % 2][:, i, hd % 2 * HD1:(hd % 2 + 1) * HD1], bank[:, 0:HD1],
                                                 self.mx[u % 2][:, 3:4], None, ALU.mult))
            bank.free = [ridone[u]]

        oTdone, o_free = [], {}

        def turn_out(hp, last):
            bank = ring.take(pe)
            pe.wait(last)
            for t in range(NT):
                mm = te.transpose(bank[:, t * P:(t + 1) * P], self.o[hp % 2][:, t, :], const.ident[:, :])
            m = pe.mark(mm)
            o_free[hp] = m
            act.wait(m, self.output_projection)
            oTdone.append(act.mark(a.copy(self.oT[:, hp, :], bank[:, :])))
            bank.free = [oTdone[-1]]

        for j in range(5):
            project(0, j)
            yield
        for j in range(NT):
            lookahead(0, j)
            yield
        nu = H1 * NT
        for u in range(nu + 2):
            hd, i = u // NT, u % NT
            if u < nu:
                scores(u)
                yield
                if hd % 2 == 0 and hd // 2 + 1 < NHP:
                    for j in [[0, 1], [2], [3], [4]][i]:
                        project(hd // 2 + 1, j)
                        yield
                if hd + 1 < H1:
                    lookahead(hd + 1, i)
                    yield
            if 0 <= u - 1 < nu:
                turn(u - 1)
                yield
            if 0 <= u - 2 < nu:
                attend(u - 2)
                if (u - 2) % (2 * NT) == 2 * NT - 1:
                    turn_out((u - 2) // (2 * NT), ridone[u - 2])
                yield

    def tail(self, b):
        p, ring, const, d = self.p, self.ring, self.const, self.d
        pe, act, dve, sp = p.pe, p.act, p.dve, p.sp
        v, a, te = dve.eng, act.eng, pe.eng
        one = bass.ds(b, 1)
        x, hT = self.x, self.hTt
        x_in = self.dma["x"].mark(sp.eng.dma_start(
            x[:, :, :], d["x1"][one, :, :].rearrange("b (t p) n -> p (b t) n", p=P)))
        mod_in = self.dma["mod"].mark(sp.eng.dma_start(
            self.mod[:, :], d["mod1"][one, :, :].rearrange("b p n -> p (b n)")))
        ga_in = self.dma["ga"].mark(sp.eng.dma_start(
            self.ga[:, :], d["rows1"][one, 0:D].rearrange("b n -> (b n)").partition_broadcast(P)))
        xdone = []
        dve.wait(ga_in, x_in)
        for pair in range(NT // 2):
            bank = ring.take(pe)
            for i in range(2):
                t = 2 * pair + i
                for k in range(NHP):
                    mm = te.matmul(bank[:, i * D:(i + 1) * D], self.oT[:, k, t * P:(t + 1) * P], self.wout[:, k, :],
                                   start=(k == 0), stop=(k == NHP - 1))
            m = pe.mark(mm)
            self.output_projection = m
            dve.wait(m, *xdone)
            m = dve.mark(v.tensor_tensor(self.tmp, bank[:, :].rearrange("p (i n) -> p i n", i=2),
                                         self.ga[:, :].unsqueeze(1).to_broadcast([P, 2, D]), ALU.mult))
            bank.free = [m]
            dve.wait(m)
            xt = x[:, 2 * pair:2 * pair + 2, :]
            xdone = [dve.mark(v.tensor_tensor(xt, xt, self.tmp, ALU.add))]
            yield
        sp.wait(*xdone)
        self.dma["xout"].mark(sp.eng.dma_start(d["x2"][one, :, :].rearrange("b (t p) n -> p (b t) n", p=P), x[:, :, :]))
        xn = self.norm.tokens(x, xdone, [])
        sp.wait(*xn)
        self.dma["xn"].mark(sp.eng.dma_start(d["xn"][one, :, :].rearrange("b (t p) n -> p (b t) n", p=P),
                                             self.norm.xn[:, :, :]))
        yield
        act.wait(mod_in)
        h = self.norm.features(ring, const.ident, xn, hT, [], self.mod, SB, CB)
        yield
        bank = ring.take(pe)
        pe.wait(*h)
        for t in range(NT):
            for k in range(KC):
                mm = te.matmul(bank[:, t * E:(t + 1) * E], hT[:, k, t * P:(t + 1) * P], self.wgate[:, k, :],
                               start=(k == 0), stop=(k == KC - 1))
        m = pe.mark(mm)
        pr, pm = self.pr, self.pm
        view = bank[:, 0:NT * E].rearrange("p (t e) -> p t e", e=E)
        dve.wait(m)
        m = dve.mark(v.tensor_reduce(pm[:, :, 0], view, AX.X, ALU.max))
        dve.wait(m)
        m = dve.mark(v.tensor_tensor(pr[:, :, :], view, pm[:, :, 0:1].to_broadcast([P, NT, E]), ALU.subtract))
        bank.free = [m]
        act.wait(m)
        m = act.mark(a.activation(pr[:, :, :], pr[:, :, :], ACT.Exp))
        yield
        dve.wait(m)
        m = dve.mark(v.tensor_reduce(pm[:, :, 1], pr[:, :, :], AX.X, ALU.add))
        dve.wait(m)
        m = dve.mark(v.reciprocal(pm[:, :, 2], pm[:, :, 1]))
        dve.wait(m)
        m = dve.mark(v.tensor_tensor(pr[:, :, :], pr[:, :, :], pm[:, :, 2:3].to_broadcast([P, NT, E]), ALU.mult))
        sp.wait(m)
        self.dma["pr"].mark(sp.eng.dma_start(d["pr"][one, :, :].rearrange("b p n -> p (b n)"),
                                             pr[:, :, :].rearrange("p t e -> p (t e)")))
        bank = ring.take(pe)
        pe.wait(m)
        for t in range(NT):
            mm = te.transpose(bank[0:E, t * P:(t + 1) * P], pr[:, t, :], const.ident[:, :])
        m = pe.mark(mm)
        dve.wait(m)
        m = dve.mark(v.tensor_copy(self.prT[:, :], bank[0:E, :]))
        bank.free = [m]
        yield
        src = self.prT
        for n in range(CAP // 8):
            dve.wait(m)
            m = dve.mark(v.max(self.top[:, :], src[:, :]))
            dve.wait(m)
            m = dve.mark(v.match_replace(self.left[:, :], self.top[:, :], src[:, :], -1.0))
            src = self.left
            if n % 2:
                yield
        dve.wait(m)
        m = dve.mark(v.tensor_scalar(self.left[:, :], self.left[:, :], 0.0, None, ALU.is_lt))
        dve.wait(m)
        m = dve.mark(v.tensor_tensor_scan(self.prT[:, :], self.left[:, :], self.zero[:, :], 0.0, ALU.add, ALU.add))
        dve.wait(m)
        m = dve.mark(v.tensor_tensor(self.prT[:, :], self.prT[:, :], self.left[:, :], ALU.mult))
        dve.wait(m)
        m = dve.mark(v.tensor_scalar(self.prT[:, :], self.prT[:, :], -1.0, None, ALU.add))
        yield
        bank = ring.take(pe)
        pe.wait(m)
        for t in range(NT):
            mm = te.transpose(bank[:, t * E:(t + 1) * E], self.prT[:, t * P:(t + 1) * P], const.ident[0:E, 0:E])
        m = pe.mark(mm)
        dve.wait(m)
        m = dve.mark(v.tensor_copy(self.pos[:, :], bank[:, 0:NT * E]))
        bank.free = [m]
        sp.wait(m)
        self.dma["pos"].mark(sp.eng.dma_start(d["pos"][one, :, :].rearrange("b p n -> p (b n)"), self.pos[:, :]))
        yield



class Experts:
    def __init__(self, prog, const, banks, d, early, late):
        self.p, self.const, self.banks, self.d = prog, const, banks, d
        self.w1, self.w2 = [], []
        self.n_early = (early.end - early.at) // (4 * (KC * F + FC * D))
        for e in range(E):
            sb = early if e < self.n_early else late
            self.w1.append(sb(f"ew1{e}", [P, KC, F]))
            self.w2.append(sb(f"ew2{e}", [P, FC, D]))
        self.wsem = [prog.nc.alloc_semaphore(f"expert{e}_in") for e in range(E)]
        sb = late
        self.data = [{
            "x": sb(f"xe{i}", [P, NT, D]),
            "xn": sb(f"xne{i}", [P, NT, D]),
            "mod": sb(f"mode{i}", [P, NMOD]),
            "gb": sb(f"gbe{i}", [P, D]),
            "pr": sb(f"prb{i}", [P, NT, E]),
            "pos": sb(f"posb{i}", [P, NT, E]),
        } for i in range(2)]
        self.pick = [sb(f"pick{i}", [P, NT, P]) for i in range(2)]
        self.wpick = [sb(f"wpick{i}", [P, NT, P]) for i in range(2)]
        self.spread = [sb(f"spread{i}", [P, T]) for i in range(2)]
        self.xin = [sb(f"xin{i}", [P, KC, P]) for i in range(2)]
        self.h1 = [sb(f"h1{i}", [P, FC, P]) for i in range(2)]
        self.h2 = [sb(f"h2{i}", [P, D]) for i in range(2)]
        self.dma = [{n: DmaSem(prog, f"e{i}_{n}") for n in ["x", "xn", "mod", "gb", "pr", "pos", "out"]}
                    for i in range(2)]

    def load_weights(self, experts):
        for e in experts:
            for w, name in ((self.w1[e], "L1_ffn_w1"), (self.w2[e], "L1_ffn_w2")):
                self.p.sp.eng.dma_start(w[:, :, :], self.d[name][e].rearrange("(k p) n -> p k n", p=P)
                                        ).then_inc(self.wsem[e], 16)

    def two_batches(self, b0):
        p, const, d = self.p, self.const, self.d
        pe, act, dve, sp, pool = p.pe, p.act, p.dve, p.sp, p.pool
        v, a, te, g = dve.eng, act.eng, pe.eng, pool.eng
        accs = [self.banks[0:2], self.banks[2:4]]
        ring = Ring(self.banks[4:])
        loaded = []
        for i in range(2):
            one, t = bass.ds(b0 + i, 1), self.data[i]
            marks = {}
            for name, dst, src in [
                    ("pos", t["pos"][:, :, :].rearrange("p t e -> p (t e)"),
                     d["pos"][one, :, :].rearrange("b p n -> p (b n)")),
                    ("xn", t["xn"][:, :, :], d["xn"][one, :, :].rearrange("b (t p) n -> p (b t) n", p=P)),
                    ("pr", t["pr"][:, :, :].rearrange("p t e -> p (t e)"),
                     d["pr"][one, :, :].rearrange("b p n -> p (b n)")),
                    ("mod", t["mod"][:, :], d["mod1"][one, :, :].rearrange("b p n -> p (b n)")),
                    ("x", t["x"][:, :, :], d["x2"][one, :, :].rearrange("b (t p) n -> p (b t) n", p=P)),
                    ("gb", t["gb"][:, :], d["rows1"][one, D:2 * D].rearrange("b n -> (b n)").partition_broadcast(P))]:
                marks[name] = self.dma[i][name].mark(sp.eng.dma_start(dst, src))
            loaded.append(marks)
        picked, wpicked, gathered, turned, xindone, spreaddone = {}, {}, {}, {}, {}, {}
        h1done, h2done, ffn1, ffn2, scattered = {}, {}, {}, {}, {}

        def pick(u):
            i, e = u // E, u % E
            t_, marks = self.data[i], loaded[i]
            dve.wait(marks["pos"], gathered.get(u - 2))
            for t in range(NT):
                picked[u] = dve.mark(v.tensor_scalar(self.pick[u % 2][:, t, :], const.iota[:, :],
                                                     t_["pos"][:, t, e:e + 1], None, ALU.is_equal))
            pool.wait(marks["pos"], marks["pr"], turned.get(u - 2))
            for t in range(NT):
                wpicked[u] = pool.mark(g.tensor_scalar(self.wpick[u % 2][:, t, :], const.iota[:, :],
                                                       t_["pos"][:, t, e:e + 1], t_["pr"][:, t, e:e + 1],
                                                       ALU.is_equal, ALU.mult))

        def gather(u):
            t_, marks = self.data[u // E], loaded[u // E]
            bank = ring.take(pe)
            pe.wait(picked[u], marks["xn"])
            for c in range(KC):
                for t in range(NT):
                    mm = te.matmul(bank[:, c * P:(c + 1) * P], t_["xn"][:, t, c * P:(c + 1) * P],
                                   self.pick[u % 2][:, t, :], start=(t == 0), stop=(t == NT - 1))
            m = gathered[u] = pe.mark(mm)
            dve.wait(m, marks["mod"], ffn1.get(u - 2))
            for c in range(KC):
                m = dve.mark(v.tensor_scalar(self.xin[u % 2][:, c, :], bank[:, c * P:(c + 1) * P],
                                             t_["mod"][:, CB + c:CB + c + 1], t_["mod"][:, SB + c:SB + c + 1],
                                             ALU.mult, ALU.add))
            bank.free = [m]
            xindone[u] = m

        def turn(u):
            bank = ring.take(pe)
            pe.wait(wpicked[u])
            for t in range(NT):
                mm = te.transpose(bank[:, t * P:(t + 1) * P], self.wpick[u % 2][:, t, :], const.ident[:, :])
            m = turned[u] = pe.mark(mm)
            dve.wait(m, scattered.get(u - 2))
            spreaddone[u] = dve.mark(v.tensor_copy(self.spread[u % 2][:, :], bank[:, :]))
            bank.free = [spreaddone[u]]

        def hidden(u):
            e = u % E
            if u < E:
                te.wait_ge(self.wsem[e], 32)
            for half in range(2):
                bank = ring.take(pe)
                pe.wait(xindone[u])
                for i in range(FC // 2):
                    f = half * (FC // 2) + i
                    for k in range(KC):
                        mm = te.matmul(bank[:, i * P:(i + 1) * P], self.w1[e][:, k, f * P:(f + 1) * P],
                                       self.xin[u % 2][:, k, :], start=(k == 0), stop=(k == KC - 1))
                m = ffn1[u] = pe.mark(mm)
                act.wait(m, ffn2.get(u - 2))
                h1done[u, half] = act.mark(a.activation(
                    self.h1[u % 2][:, half * (FC // 2):(half + 1) * (FC // 2), :],
                    bank[:, :].rearrange("p (f s) -> p f s", s=P), ACT.Gelu))
                bank.free = [h1done[u, half]]

        def output(u):
            bank = ring.take(pe)
            for f in range(FC):
                pe.wait(h1done[u, f // (FC // 2)])
                mm = te.matmul(bank[:, 0:D], self.h1[u % 2][:, f, :], self.w2[u % E][:, f, :], start=(f == 0),
                               stop=(f == FC - 1))
            m = ffn2[u] = pe.mark(mm)
            act.wait(m, scattered.get(u - 2))
            h2done[u] = act.mark(a.copy(self.h2[u % 2][:, :], bank[:, 0:D]))
            bank.free = [h2done[u]]

        def scatter(u):
            i, e = u // E, u % E
            acc = accs[i]
            pe.wait(h2done[u], spreaddone[u])
            for t in range(NT):
                mm = te.matmul(acc[t // 2][:, t % 2 * D:(t % 2 + 1) * D], self.spread[u % 2][:, t * P:(t + 1) * P],
                               self.h2[u % 2][:, :], start=(e == 0 and t % 2 == 0), stop=(e == E - 1 and t % 2 == 1),
                               skip_group_check=True)
            scattered[u] = pe.mark(mm)
            if e < E - 1:
                return
            t_, marks = self.data[i], loaded[i]
            dve.wait(scattered[u], marks["gb"], marks["x"])
            gb = t_["gb"][:, :].unsqueeze(1).to_broadcast([P, 2, D])
            for j in range(2):
                m = dve.mark(v.tensor_tensor(t_["xn"][:, 2 * j:2 * j + 2, :],
                                             acc[j][:, :].rearrange("p (i n) -> p i n", i=2), gb, ALU.mult))
            dve.wait(m)
            m = dve.mark(v.tensor_tensor(t_["x"][:, :, :], t_["x"][:, :, :], t_["xn"][:, :, :], ALU.add))
            sp.wait(m)
            self.dma[i]["out"].mark(sp.eng.dma_start(
                d["out"][bass.ds(b0 + i, 1), :, :].rearrange("b (t p) n -> p (b t) n", p=P), t_["x"][:, :, :]))

        n = 2 * E
        pick(0)
        gather(0)
        turn(0)
        pick(1)
        for u in range(n):
            hidden(u)
            if u + 1 < n:
                gather(u + 1)
            if u > 0:
                scatter(u - 1)
            if u + 1 < n:
                turn(u + 1)
            if u + 2 < n:
                pick(u + 2)
            output(u)
        scatter(n - 1)



def program(nc, d):
    prog = Program(nc)
    for name, shape in [("mod0", [B, P, NMOD]), ("mod1", [B, P, NMOD]), ("rows0", [B, D]), ("rows1", [B, 2 * D]),
                        ("x1", [B, T, D]), ("x2", [B, T, D]), ("xn", [B, T, D]), ("pr", [B, P, NT * E]),
                        ("pos", [B, P, NT * E])]:
        d[name] = nc.dram_tensor(name + "_scratch", shape, F32, kind="Internal").ap()

    banks = [Bank(nc, f"bank{i}") for i in range(8)]
    end = nc.sbuf_usable_end
    low = Arena(nc, nc.sbuf_base, end)
    const = Constants(prog, low)
    shared = low.at
    b1 = Block1(prog, low, const, Ring(banks[3:8]), d)
    middle = low.at
    b0 = Block0(prog, low, const, Ring(banks[0:3]), d)
    setup_sb = Arena(nc, b1.setup_at, middle)
    half = b1.wqkv[:, :, 0:6 * D], b1.wqkv[:, :, 6 * D:12 * D]
    ring = Ring(banks)
    out0, read0 = modulation(prog, ring, setup_sb, 0, half[0], d["cT0"], d["L0_wmod"], d["mod0"], d["rows0"], [GA])
    out1, read1 = modulation(prog, ring, setup_sb, 1, half[1], d["cT1"], d["L1_wmod"], d["mod1"], d["rows1"], [GA, GB])
    ready = const.ready + b0.setup() + out0 + out1
    b1.setup([read0, read1])
    for line in prog.lines + [prog.sp]:
        line.wait(*ready)
    for _ in b0.batch(0, b1):
        pass
    prog.meet()
    interleave((b0.batch(1, b1), N0, 0.93), (b1.attention(0), N1, 1.0))
    prog.meet()
    with nc.Fori(1, B - 1) as i:
        interleave((b0.batch(i + 1, b1), N0, 0.93), (b1.attention(i), N1, 1.0), (b1.tail(i - 1), NTAIL, 0.5))
        prog.meet()
    ex = Experts(prog, const, banks, d, Arena(nc, middle, end), Arena(nc, shared, middle))
    ex.load_weights(range(ex.n_early))
    interleave((b1.attention(B - 1), N1, 1.0), (b1.tail(B - 2), NTAIL, 0.5))
    prog.meet()
    for _ in b1.tail(B - 1):
        pass
    prog.meet()
    ex.load_weights(range(ex.n_early, E))
    with nc.Fori(0, B // 2) as i:
        ex.two_batches(2 * i)
        prog.meet()
    for s in ex.wsem:
        nc.sync.wait_ge(s, 32)


_DIRECT = ["L0_attn_x", "L0_attn_b_qkv", "L0_attn_b_out", "L0_ffn_cn_w1", "L0_ffn_cn_b1", "L0_ffn_cn_w2",
           "L0_ffn_cn_b2", "L0_ffn_cn_w3", "L0_ffn_cn_b3", "L0_ffn_cn_w4", "L0_ffn_cn_b4", "L0_ffn_gc_w1",
           "L0_ffn_gc_b1", "L0_ffn_gc_w2", "L0_ffn_gc_b2", "L0_ffn_gc_w3", "L0_ffn_gc_b3", "L0_ffn_adaptive_range",
           "L0_wmod", "L1_ffn_w1", "L1_ffn_w2", "L1_wmod"]
_TURNED = {"w_qkv0": "L0_attn_W_qkv", "w_out0": "L0_attn_W_out", "w_qkv1": "L1_attn_W_qkv", "w_out1": "L1_attn_W_out",
           "w_gate": "L1_ffn_gate_w", "cT0": "L0_c", "cT1": "L1_c"}


def kernel(**inputs):
    import numpy as np
    import concourse.bacc as bacc
    from concourse.bass_utils import run_bass_kernel_spmd

    nc = bacc.Bacc("TRN2", target_bir_lowering=False, num_devices=1)
    arrays = {n: np.ascontiguousarray(inputs[n]) for n in _DIRECT}
    arrays.update({n: np.ascontiguousarray(np.asarray(inputs[m]).T) for n, m in _TURNED.items()})
    d = {n: nc.dram_tensor(n, x.shape, F32, kind="ExternalInput").ap() for n, x in arrays.items()}
    d["out"] = nc.dram_tensor("out", (B, T, D), F32, kind="ExternalOutput").ap()
    program(nc, d)
    r = run_bass_kernel_spmd(nc, [arrays], core_ids=[0])
    return r.results[0]["out"]
```

```python
import concourse.bass as bass
from concourse import mybir

F32 = mybir.dt.float32
BF16 = mybir.dt.bfloat16
I32 = mybir.dt.int32
ALU = mybir.AluOpType
ACT = mybir.ActivationFunctionType
AX = mybir.AxisListType

P = 128
B, T, D = 8, 512, 256
NT = T // P
KC = D // P
EPS = 1e-5
H0, HD0, LB = 16, 16, 64
NBLK = T // LB
NR = P // 32
H1, HD1 = 8, 64
NHP = H1 // 2
CH1 = H1 * HD1
E, F = 8, 1024
FC = F // P
CAP = 2 * T // E
NEG = -1e30
CYCLES = 3
N0, NTAIL, NCHOOSE, NMOE = 69, 10, 19, 66
SPREAD0, SPREAD_TAIL, SPREAD_CHOOSE, SPREAD_FIRST, SPREAD_LAST = 0.9, 0.43, 0.9, 0.2, 0.6
WEIGHT = {"V": 1.4, "P": 1.4}
BESIDE0, BESIDE_TAIL = "VPSA", "VLA"
NATT = 24 * WEIGHT["P"] + 128
EARLY = ["pos", "xn", "pr", "mod"]
SA, CA, GA, SB, CB, GB = (KC * i for i in range(6))
NMOD = 6 * KC


class Line:

    def __init__(self, prog, eng, name):
        self.prog, self.eng, self.name = prog, eng, name
        self.sem = prog.nc.alloc_semaphore(name + "_done")
        self.restart()

    def restart(self):
        self.n, self.seen = 0, {}

    def wait(self, *marks):
        for m in marks:
            if m is None or m[2] != self.prog.epoch:
                continue
            sem, value, _ = m
            if self.seen.get(sem.name, 0) < value:
                self.eng.wait_ge(sem, value)
                self.seen[sem.name] = value

    def mark(self, instruction):
        self.n += 1
        instruction.then_inc(self.sem, 1)
        return (self.sem, self.n, self.prog.epoch)


class DmaSem:

    def __init__(self, prog, name):
        self.prog, self.n = prog, 0
        self.sem = prog.nc.alloc_semaphore(name)
        prog.dma_sems.append(self)

    def mark(self, instruction):
        self.n += 16
        instruction.then_inc(self.sem, 16)
        return (self.sem, self.n, self.prog.epoch)

    def last(self):
        return (self.sem, self.n, self.prog.epoch) if self.n else None


class Program:
    def __init__(self, nc):
        self.nc, self.epoch, self.dma_sems = nc, 0, []
        self.pe = Line(self, nc.tensor, "pe")
        self.act = Line(self, nc.scalar, "act")
        self.dve = Line(self, nc.vector, "dve")
        self.pool = Line(self, nc.gpsimd, "pool")
        self.sp = Line(self, nc.sync, "sp")
        self.lines = [self.pe, self.act, self.dve, self.pool]

    def meet(self):
        for d in self.dma_sems:
            self.sp.wait(d.last())
        self.nc.all_engine_barrier()
        for x in self.lines + self.dma_sems:
            if x.n:
                self.nc.sync.sem_clear(x.sem)
        self.nc.all_engine_barrier()
        for x in self.lines:
            x.restart()
        for d in self.dma_sems:
            d.n = 0
        self.sp.restart()
        self.epoch += 1


class Bank:

    def __init__(self, nc, name):
        self.t = nc.alloc_psum_tensor(name, [P, 512], F32)
        self.free = []

    def __getitem__(self, key):
        return self.t[key]


class Ring:
    def __init__(self, banks):
        self.banks, self.n = banks, -1

    def take(self, pe):
        self.n += 1
        b = self.banks[self.n % len(self.banks)]
        pe.wait(*b.free)
        b.free = []
        return b


def interleave(main, total, *others):
    live = [[g, n, span, after, 0] for g, n, span, after in others]
    done = -0.8
    for kind in main:
        done += WEIGHT.get(kind, 1)
        for x in list(live):
            while x in live and kind in x[3] and x[4] / x[1] * x[2] * total < done:
                x[4] += 1
                if next(x[0], "end") == "end":
                    live.remove(x)
    while live:
        for x in list(live):
            if next(x[0], "end") == "end":
                live.remove(x)


class Arena:

    def __init__(self, nc, at, end):
        self.nc, self.at, self.end = nc, (at + 31) // 32 * 32, end

    def __call__(self, name, shape, dtype=F32):
        size = 2 if dtype == BF16 else 4
        for n in shape[1:]:
            size *= n
        t = self.nc.alloc_sbuf_tensor_at(name, shape, dtype, offset=self.at)
        self.at += (size + 31) // 32 * 32
        assert self.at <= self.end, (name, self.at, self.end)
        return t



class Norm:

    def __init__(self, prog, sb, name, power):
        self.p, self.power = prog, power
        self.stats = sb(name + "_stats", [P, NT, 6])
        self.mv = sb(name + "_mv", [P, NT, 2])
        self.rstd = sb(name + "_rstd", [P, NT])
        self.xn = sb(name + "_xn", [P, NT, D])

    def tokens(self, x, ready, xn_free):
        dve = self.p.dve
        v = dve.eng
        dve.wait(*ready)
        for t in range(NT):
            m = dve.mark(v.bn_stats(self.stats[:, t, :], x[:, t, :]))
        dve.wait(m)
        for t in range(NT):
            m = dve.mark(v.bn_aggr(self.mv[:, t, :], self.stats[:, t, :]))
        pool = self.p.pool
        pool.wait(m)
        m = pool.mark(pool.eng.tensor_scalar(self.rstd[:, :], self.mv[:, :, 1], EPS, None, ALU.add))
        pool.wait(m)
        m = pool.mark(pool.eng.tensor_tensor(self.rstd[:, :], self.rstd[:, :], self.power[:, :], ALU.pow))
        dve.wait(m, *xn_free)
        return [dve.mark(v.tensor_scalar(self.xn[:, t, :], x[:, t, :], self.mv[:, t, 0:1], self.rstd[:, t:t + 1],
                                         ALU.subtract, ALU.mult)) for t in range(NT)]

    def features(self, ring, ident, xn_done, hT, hT_free, mod, shift, scale, accum=None):
        pe, act = self.p.pe, self.p.act
        marks = []
        for c in range(KC):
            bank = ring.take(pe)
            for t in range(NT):
                pe.wait(xn_done[t])
                mm = pe.eng.transpose(bank[:, t * P:(t + 1) * P], self.xn[:, t, c * P:(c + 1) * P], ident[:, :])
            done = pe.mark(mm)
            act.wait(done, *hT_free)
            extra = {} if accum is None else {"accum_out": accum[:, c:c + 1]}
            m = act.mark(act.eng.activation(hT[:, c, :], bank[:, :], ACT.Identity, bias=mod[:, shift + c:shift + c + 1],
                                            scale=mod[:, scale + c:scale + c + 1], **extra))
            bank.free = [m]
            marks.append(m)
        return marks



class Constants:
    def __init__(self, prog, sb):
        nc, pool, dve = prog.nc, prog.pool, prog.dve
        g = pool.eng
        self.ident = sb("ident", [P, P])
        self.identb = sb("identb", [P, P], BF16)
        self.negL = sb("negL", [P, P], BF16)
        self.negS = sb("negS", [P, P], BF16)
        self.fold = sb("fold", [P, LB])
        self.iota_i = sb("iota_i", [P, P], I32)
        self.iota = sb("iota", [P, P])
        self.parity = sb("parity", [P, 2])
        self.group = sb("group", [P, P // HD0])
        self.sign = sb("sign", [P, 1])
        self.ones = sb("ones", [3, P], BF16)
        self.power = sb("power", [P, NT])

        def select(out, compare, fill, base, step, n, mult, after):
            pool.wait(after)
            return pool.mark(g.affine_select(out=out, in_=out, compare_op=compare, fill=fill, base=base,
                                             pattern=[[step, n]], channel_multiplier=mult))

        done = []
        m = pool.mark(g.memset(self.ident[:, :], 0.0))
        i1 = select(self.ident[:, :], ALU.not_equal, 1.0, 0, -1, P, 1, m)
        m = pool.mark(g.memset(self.negL[:, :], 0.0))
        done.append(select(self.negL[:, :], ALU.is_gt, NEG, 0, -1, P, 1, m))
        m = pool.mark(g.memset(self.negS[:, :], 0.0))
        done.append(select(self.negS[:, :], ALU.is_ge, NEG, 0, -1, P, 1, m))
        m = pool.mark(g.memset(self.fold[:, :], 0.0))
        m = select(self.fold[:, :], ALU.not_equal, 1.0, 0, -1, LB, 1, m)
        done.append(select(self.fold[:, :], ALU.not_equal, 1.0, -LB, -1, LB, 1, m))
        m = pool.mark(g.iota(self.iota_i[:, :], pattern=[[1, P]], base=0, channel_multiplier=0))
        m0 = pool.mark(g.memset(self.group[:, :], float(HD0) ** -0.5))
        m0 = select(self.group[:, :], ALU.is_ge, 0.0, 0, -HD0, P // HD0, 1, m0)
        m0 = select(self.group[:, :], ALU.is_ge, 0.0, HD0 - 1, HD0, P // HD0, -1, m0)
        m1 = pool.mark(g.memset(self.sign[:, :], 1.0))
        done.append(select(self.sign[:, :], ALU.is_ge, -1.0, P // 2 - 1, 0, 1, -1, m1))
        done.append(pool.mark(g.memset(self.ones[:, :], 1.0)))
        done.append(pool.mark(g.memset(self.power[:, :], -0.5)))
        v = dve.eng
        dve.wait(i1, m, m0)
        v.tensor_copy(self.identb[:, :], self.ident[:, :])
        v.tensor_copy(self.iota[:, :], self.iota_i[:, :])
        m2 = dve.mark(v.tensor_reduce(self.parity[:, :], self.group[:, :].rearrange("p (g a) -> p a g", a=2), AX.X,
                                      ALU.add))
        self.ready = done + [i1, m2]


def modulation(prog, ring, sb, layer, w, cT_d, wmod_d, mod_d, rows_d, row_kinds, result):
    pe, act, dve, sp = prog.pe, prog.act, prog.dve, prog.sp
    v = dve.eng
    n = f"m{layer}"
    cT = sb(n + "cT", [P, KC, B])
    th = sb(n + "th", [P, KC, B])
    sil = sb(n + "sil", [P, KC, B])
    cols = sb(n + "cols", [P, B, NMOD])
    size = sb(n + "size", [P, B, NMOD])
    rows = sb(n + "rows", [B, len(row_kinds) * D])
    rsize = sb(n + "rsize", [B, len(row_kinds) * D])
    dc, dw = DmaSem(prog, n + "_c_in"), DmaSem(prog, n + "_w_in")
    dm, dr = DmaSem(prog, n + "_cols_out"), DmaSem(prog, n + "_rows_out")
    c_in = dc.mark(sp.eng.dma_start(cT[:, :, :], cT_d.rearrange("(k p) b -> p k b", p=P)))
    w_in = dw.mark(sp.eng.dma_start(w, wmod_d.rearrange("(k p) n -> p k n", p=P)))
    yield
    act.wait(c_in)
    m = act.mark(act.eng.activation(th[:, :, :], cT[:, :, :], ACT.Tanh, scale=0.5))
    dve.wait(m, c_in)
    m = dve.mark(v.scalar_tensor_tensor(out=th[:, :, :], in0=th[:, :, :], scalar=1.0, in1=cT[:, :, :], op0=ALU.add,
                                        op1=ALU.mult))
    dve.wait(m)
    sil_done = dve.mark(v.tensor_scalar(sil[:, :, :], th[:, :, :], 0.5, None, ALU.mult))
    pe.wait(sil_done, w_in)
    bank = ring.take(pe)
    for j in range(NMOD):
        if j % 2 == 0:
            yield
        for k in range(KC):
            mm = pe.eng.matmul(bank[:, j * B:(j + 1) * B], w[:, k, j * P:(j + 1) * P], sil[:, k, :], start=(k == 0),
                               stop=(k == KC - 1))
    m = pe.mark(mm)
    dve.wait(m)
    m = dve.mark(v.tensor_copy(cols[:, :, :], bank[:, 0:NMOD * B].rearrange("p (j b) -> p b j", b=B)))
    bank.free = [m]
    dve.wait(m)
    for j in (CA, CB):
        m = dve.mark(v.tensor_scalar(cols[:, :, j:j + KC], cols[:, :, j:j + KC], 1.0, None, ALU.add))

    def gate(g, size):
        m = dve.mark(v.scalar_tensor_tensor(out=size, in0=g, scalar=-1.0, in1=g, op0=ALU.mult, op1=ALU.max))
        dve.wait(m)
        v.tensor_scalar(size, size, 0.25, None, ALU.max)
        m = dve.mark(v.tensor_scalar(g, g, 0.0, 2.0, ALU.is_ge, ALU.mult))
        dve.wait(m)
        return dve.mark(v.scalar_tensor_tensor(out=g, in0=g, scalar=-1.0, in1=size, op0=ALU.add, op1=ALU.mult))

    for j in (GA, GB):
        m = gate(cols[:, :, j:j + KC], size[:, :, j:j + KC])
    sp.wait(m)
    yield
    out = [dm.mark(sp.eng.dma_start(mod_d.rearrange("b p n -> p b n"), cols[:, :, :]))]
    yield
    for i, j in enumerate(row_kinds):
        bank = ring.take(pe)
        for k in range(KC):
            mm = pe.eng.matmul(bank[0:B, 0:D], sil[:, k, :], w[:, k, j * P:j * P + D], start=(k == 0),
                               stop=(k == KC - 1))
        m = rows_read = pe.mark(mm)
        dve.wait(m)
        m = dve.mark(v.tensor_copy(rows[:, i * D:(i + 1) * D], bank[0:B, 0:D]))
        bank.free = [m]
        yield
    dve.wait(m)
    m = gate(rows[:, :], rsize[:, :])
    sp.wait(m)
    out.append(dr.mark(sp.eng.dma_start(rows_d, rows[:, :])))
    result.update(out=out, read=rows_read, cols=cols[:, 0, :])
    yield



class Block0:
    def __init__(self, prog, sb, const, ring, d):
        self.p, self.const, self.ring, self.d = prog, const, ring, d
        self.wqkv = sb("wqkv0", [P, KC, 3 * D])
        self.wout = sb("wout0", [P, KC, D])
        self.bq = sb("bq", [P, KC])
        self.bqp = sb("bqp", [P, KC, 2])
        self.bk = sb("bk", [P, KC])
        self.bv = sb("bv", [P, KC])
        self.bout = sb("bout", [3, D])
        self.bout_parts = sb("bout_parts", [3, D], BF16)
        self.w1 = sb("cw1", [P, KC, D])
        self.w2 = sb("cw2", [P, KC, P])
        self.w3 = sb("cw3", [P, 64])
        self.w4c = sb("cw4c", [64, 1])
        self.w4 = sb("cw4", [64, P])
        self.b1 = sb("cb1", [P, KC])
        self.b2 = sb("cb2", [P, 1])
        self.b3 = sb("cb3", [64, 1])
        self.b4 = sb("cb4", [P, 1])
        self.g1 = sb("gw1", [P, KC, P])
        self.g2 = sb("gw2", [P, 64])
        self.g3c = sb("gw3c", [64, 1])
        self.g3 = sb("gw3", [64, P])
        self.gb1 = sb("gb1", [P, 1])
        self.gb2 = sb("gb2", [64, 1])
        self.gb3 = sb("gb3", [P, 1])
        self.ar = sb("ar", [P, 1])
        self.sar = sb("sar", [P, 3])
        self.x = sb("x0", [P, NT, D])
        self.mod = sb("mod0", [P, NMOD])
        self.ga = sb("ga0", [P, D])
        self.mod_next = sb("mod0n", [P, NMOD])
        self.norm = Norm(prog, sb, "n0", const.power)
        self.tmp = self.norm.xn[:, 0:2, :]
        self.hT = sb("hT0", [P, KC, T])
        self.q = sb("q0", [P, KC, NBLK, 2, LB])
        self.k = sb("k0", [P, KC, NBLK, NR, LB])
        self.v = sb("v0", [P, NBLK, NR, 66])
        self.mx = [sb(f"mx0{i}", [P, NR * KC]) for i in range(2)]
        self.s = [sb(f"s0{i}", [P, NR, KC, LB]) for i in range(2)]
        self.pT = [sb(f"pT0{i}", [P, NR, P]) for i in range(2)]
        self.ri = [sb(f"ri0{i}", [P, NR, KC]) for i in range(2)]
        self.o = [sb(f"o0{i}", [P, KC, NR, 2, HD0]) for i in range(2)]
        self.sum = sb("sum0", [P, KC])
        self.gf = sb("gf", [P, 4])
        self.a1 = sb("a1", [P, KC, T])
        self.aT = self.a1
        self.a2 = sb("a2", [P, T])
        self.a3 = self.a2[0:64, :]
        self.tf = self.a2
        names = ["x", "mod", "modn", "ga", "xout"]
        self.dma = {n: DmaSem(prog, f"b0_{n}") for n in names}
        self.dw = [DmaSem(prog, f"b0_w{i}") for i in range(2)]
        self.mod_ready = []
        self.mod_next_ready = lambda: []

    def load_weights(self):
        p, d = self.p, self.d
        nc, act = p.nc, p.act
        e, dw = (act.eng, self.dw[0])

        def load(dst, src):
            return dw.mark(e.dma_start(dst, src))

        load(self.wqkv[:, :, :], d["w_qkv0"].rearrange("(k p) n -> p k n", p=P))
        bq = d["L0_attn_b_qkv"].rearrange("(a k p) -> a p k", p=P, k=KC)
        with nc.allow_non_contiguous_dma(reason="bias columns"):
            load(self.bq[:, :], bq[0])
            load(self.bk[:, :], bq[1])
            load(self.bv[:, :], bq[2])
            load(self.b1[:, :], d["L0_ffn_cn_b1"].rearrange("(k p) -> p k", p=P))
            load(self.b2[:, :], d["L0_ffn_cn_b2"].rearrange("(p a) -> p a", a=1))
            load(self.b3[:, :], d["L0_ffn_cn_b3"].rearrange("(p a) -> p a", a=1))
            load(self.gb1[:, :], d["L0_ffn_gc_b1"].rearrange("(p a) -> p a", a=1))
            load(self.gb2[:, :], d["L0_ffn_gc_b2"].rearrange("(p a) -> p a", a=1))
            load(self.b4[:, :], d["L0_ffn_cn_b4"].partition_broadcast(P))
            load(self.gb3[:, :], d["L0_ffn_gc_b3"].partition_broadcast(P))
            load(self.ar[:, :], d["L0_ffn_adaptive_range"].partition_broadcast(P))
            load(self.w4c[:, :], d["L0_ffn_cn_w4"])
            load(self.g3c[:, :], d["L0_ffn_gc_w3"])
        load(self.wout[:, :, :], d["w_out0"].rearrange("(k p) n -> p k n", p=P))
        load(self.bout[:, :], d["L0_attn_b_out"].partition_broadcast(3))
        load(self.w1[:, :, :], d["L0_ffn_cn_w1"].rearrange("(k p) n -> p k n", p=P))
        load(self.w2[:, :, :], d["L0_ffn_cn_w2"].rearrange("(k p) n -> p k n", p=P))
        load(self.w3[:, :], d["L0_ffn_cn_w3"])
        load(self.g1[:, :, :], d["L0_ffn_gc_w1"].rearrange("(k p) n -> p k n", p=P))
        return load(self.g2[:, :], d["L0_ffn_gc_w2"])

    def setup(self, loaded):
        p = self.p
        dve = p.dve
        v = dve.eng
        pool = p.pool
        g = pool.eng
        m = pool.mark(g.memset(self.v[:, :, :, :], 0.0))
        m0 = pool.mark(g.memset(self.k[:, :, :, :, :], 0.0))
        for o in self.o:
            m0 = pool.mark(g.memset(o[:, :, :, :, :], 0.0))
        dve.wait(m)
        for c in range(KC):
            v.memset(self.v[64 * c:64 * c + 64, :, :, 64 + c:65 + c], 1.0)
        dve.wait(loaded, *self.const.ready)
        v.tensor_copy(self.w4[:, :], self.w4c[:, 0:1].to_broadcast([64, P]))
        v.tensor_copy(self.g3[:, :], self.g3c[:, 0:1].to_broadcast([64, P]))
        for c in range(KC):
            v.tensor_scalar(self.bqp[:, c, :], self.const.parity[:, :], self.bq[:, c:c + 1], None, ALU.mult)
        v.tensor_scalar(self.b4[:, :], self.b4[:, :], 0.5, None, ALU.mult)
        v.tensor_scalar(self.gb3[:, :], self.gb3[:, :], 0.5, None, ALU.mult)
        m = dve.mark(v.tensor_tensor(self.ar[:, :], self.ar[:, :], self.const.sign[:, :], ALU.mult))
        dve.wait(m)
        v.tensor_scalar(self.sar[:, 0:1], self.ar[:, :], 0.3, None, ALU.mult)
        bout, parts, ident = self.bout[:, :], self.bout_parts[:, :], self.const.ident
        kept = [self.s[k][0:3, 0:2, :, :].rearrange("p r c m -> p (r c m)") for k in range(2)]
        for k in range(2):
            m = dve.mark(v.tensor_copy(parts, bout))
            dve.wait(m)
            v.tensor_scalar(kept[k], parts, ident[0:3, k:k + 1], None, ALU.mult)
            m = dve.mark(v.tensor_tensor(bout, bout, parts, ALU.subtract))
            dve.wait(m)
        m = dve.mark(v.scalar_tensor_tensor(out=bout, in0=bout, scalar=ident[0:3, 2:3], in1=kept[0], op0=ALU.mult,
                                            op1=ALU.add))
        dve.wait(m)
        v.tensor_tensor(parts, bout, kept[1], ALU.add)
        v.tensor_scalar(self.sar[:, 1:2], self.ar[:, :], 0.7, None, ALU.mult)
        return [loaded, m0,
                dve.mark(v.tensor_scalar(self.sar[:, 2:3], self.const.sign[:, :], 0.1, None, ALU.mult))]

    def batch(self, b, b1, columns=None):
        p, ring, const, d = self.p, self.ring, self.const, self.d
        pe, act, dve, sp = p.pe, p.act, p.dve, p.sp
        v, a, te = dve.eng, act.eng, pe.eng
        one = bass.ds(b, 1)
        x, hT = self.x, self.hT
        x_in = self.dma["x"].mark(sp.eng.dma_start(
            x[:, :, :], d["L0_attn_x"][one, :, :].rearrange("b (t p) n -> p (b t) n", p=P)))
        yield
        yield
        xn = self.norm.tokens(x, [x_in], [])
        yield
        yield
        if columns is None:
            mod_in = self.dma["mod"].mark(sp.eng.dma_start(
                self.mod[:, :], d["mod0"][one, :, :].rearrange("b p n -> p (b n)")))
        else:
            mod_in = dve.mark(v.tensor_copy(self.mod[:, :], columns["cols"]))
        sp.wait(*self.mod_ready)
        ga_in = self.dma["ga"].mark(sp.eng.dma_start(
            self.ga[:, :], d["rows0"][one, :].rearrange("b n -> (b n)").partition_broadcast(P)))
        act.wait(mod_in)
        h = self.norm.features(ring, const.ident, xn, hT, [], self.mod, SA, CA)
        yield
        kdone, qdone, vdone = [], [], []
        for c in range(KC):
            bank = ring.take(pe)
            pe.wait(*h)
            for k in range(KC):
                mm = te.matmul(bank[:, :], self.wqkv[:, k, D + c * P:D + (c + 1) * P], hT[:, k, :], start=(k == 0),
                               stop=(k == KC - 1))
            m = pe.mark(mm)
            act.wait(m)
            for r in range(NR):
                rows = slice(32 * r, 32 * r + 32)
                m = act.mark(a.activation(self.k[rows, c, :, r, :], bank[rows, :].rearrange("p (n m) -> p n m", m=LB),
                                          ACT.Identity, bias=self.bk[rows, c:c + 1]))
            bank.free = [m]
            kdone = [m]
            bank = ring.take(pe)
            for k in range(KC):
                mm = te.matmul(bank[:, :], self.wqkv[:, k, c * P:(c + 1) * P], hT[:, k, :], start=(k == 0),
                               stop=(k == KC - 1))
            m = pe.mark(mm)
            dve.wait(m)
            for par in range(2):
                m = dve.mark(v.tensor_scalar(self.q[:, c, :, par, :], bank[:, :].rearrange("p (n l) -> p n l", l=LB),
                                             const.parity[:, par:par + 1], self.bqp[:, c, par:par + 1], ALU.mult,
                                             ALU.add))
            bank.free = [m]
            qdone = [m]
            yield
        for half in range(2):
            bank = ring.take(pe)
            for n in range(4):
                blk = 4 * half + n
                for c in range(KC):
                    for k in range(KC):
                        mm = te.matmul(bank[64 * c:64 * c + 64, n * P:(n + 1) * P], hT[:, k, blk * LB:(blk + 1) * LB],
                                       self.wqkv[:, k, 2 * D + c * P:2 * D + (c + 1) * P], start=(k == 0),
                                       stop=(k == KC - 1))
            m = pe.mark(mm)
            for c in range(KC):
                rows = slice(64 * c, 64 * c + 64)
                line, copy = (act, a.copy) if c else (dve, v.tensor_copy)
                line.wait(m)
                vdone.append(line.mark(copy(self.v[rows, 4 * half:4 * half + 4, :, 32 * c:32 * c + 32],
                                            bank[rows, :].rearrange("p (n r e) -> p n r e", n=4, r=NR))))
            bank.free = vdone[-2:]
            yield
        sdone, exped, tdone, odone, adone = {}, {}, {}, {}, {}
        ptr_free, o_free, s_free = {}, {}, {}

        def scores(n):
            bank = ring.take(pe)
            pe.wait(*kdone, *qdone)
            for c in range(KC):
                mm = te.matmul(bank[:, c * 256:(c + 1) * 256], self.q[:, c, n, :, :].rearrange("p a l -> p (a l)"),
                               self.k[:, c, n, :, :].rearrange("p r m -> p (r m)"), start=True, stop=True)
            m = pe.mark(mm)
            view = bank[:, :].rearrange("p (c r m) -> p c r m", c=KC, r=NR)
            s, mx = self.s[n % 2], self.mx[n % 2]
            dve.wait(m)
            m = dve.mark(v.tensor_reduce(mx[:, :], bank[:, :].rearrange("p (g m) -> p g m", m=LB), AX.X, ALU.max))
            dve.wait(m, s_free.get(n - 2))
            m = dve.mark(v.tensor_tensor(s[:, :, :, :].rearrange("p r c m -> p c r m"), view,
                                         mx[:, :].rearrange("p (c r) -> p c r", c=KC).unsqueeze(3)
                                         .to_broadcast([P, KC, NR, LB]), ALU.subtract))
            bank.free = [m]
            act.wait(m)
            exped[n] = act.mark(a.activation(s[:, :, :, :], s[:, :, :, :], ACT.Exp))

        def turn(n):
            bank = ring.take(pe)
            pe.wait(exped[n])
            for r in range(NR):
                mm = te.transpose(bank[:, r * P:(r + 1) * P],
                                  self.s[n % 2][:, r, :, :].rearrange("p c m -> p (c m)"), const.ident[:, :])
            m = pe.mark(mm)
            s_free[n] = m
            act.wait(m, ptr_free.get(n - 2))
            tdone[n] = act.mark(a.copy(self.pT[n % 2][:, :, :], bank[:, :].rearrange("p (r l) -> p r l", r=NR)))
            bank.free = [tdone[n]]

        def values(n):
            bank = ring.take(pe)
            pe.wait(tdone[n], *vdone)
            for r in range(NR):
                mm = te.matmul(bank[:, r * 66:(r + 1) * 66], self.pT[n % 2][:, r, :], self.v[:, n, r, :], start=True,
                               stop=True)
            m = pe.mark(mm)
            ptr_free[n] = m
            view = bank[:, 0:NR * 66].rearrange("p (r e) -> p r e", r=NR)
            ri, o = self.ri[n % 2], self.o[n % 2]
            dve.wait(m)
            m = dve.mark(v.reciprocal(ri[:, :, :], view[:, :, 64:66]))
            dve.wait(m, o_free.get(n - 2))
            for par in range(2):
                rows = slice(64 * par, 64 * par + 64)
                for c in range(KC):
                    m = dve.mark(v.tensor_tensor(
                        o[rows, c, :, par, :], view[rows, :, 32 * c + 16 * par:32 * c + 16 * par + 16],
                        ri[rows, :, c:c + 1].to_broadcast([64, NR, HD0]), ALU.mult))
            bank.free = [m]
            odone[n] = m

        def gather(n):
            bank = ring.take(pe)
            pe.wait(odone[n])
            for c in range(KC):
                mm = te.matmul(bank[:, c * LB:(c + 1) * LB],
                               self.o[n % 2][:, c, :, :, :].rearrange("p r a e -> p (r a e)"), const.fold[:, :],
                               start=True, stop=True)
            m = pe.mark(mm)
            o_free[n] = m
            act.wait(m)
            for c in range(KC):
                m = act.mark(a.activation(self.aT[:, c, n * LB:(n + 1) * LB], bank[:, c * LB:(c + 1) * LB],
                                          ACT.Identity, bias=self.bv[:, c:c + 1]))
            bank.free = [m]
            adone[n] = m

        for n in range(NBLK + 3):
            if n < NBLK:
                scores(n)
                yield
            if 0 <= n - 1 < NBLK:
                turn(n - 1)
                yield
            if 0 <= n - 2 < NBLK:
                values(n - 2)
                yield
            if 0 <= n - 3 < NBLK:
                gather(n - 3)
                yield
        xdone = []
        dve.wait(ga_in)
        for pair in range(NT // 2):
            bank = ring.take(pe)
            pe.wait(adone[NBLK - 1])
            for i in range(2):
                t = 2 * pair + i
                out = bank[:, i * D:(i + 1) * D]
                for k in range(KC):
                    te.matmul(out, self.aT[:, k, t * P:(t + 1) * P], self.wout[:, k, :], start=(k == 0), stop=False)
                mm = te.matmul(out, const.ones[:, :], self.bout_parts[:, :], start=False, stop=True)
            m = pe.mark(mm)
            dve.wait(m, *xdone)
            m = dve.mark(v.tensor_tensor(self.tmp, bank[:, :].rearrange("p (i n) -> p i n", i=2),
                                         self.ga[:, :].unsqueeze(1).to_broadcast([P, 2, D]), ALU.mult))
            bank.free = [m]
            dve.wait(m)
            xt = x[:, 2 * pair:2 * pair + 2, :]
            xdone = [dve.mark(v.tensor_tensor(xt, xt, self.tmp, ALU.add))]
            yield
        xn = self.norm.tokens(x, xdone, h)
        yield
        yield
        out = self.norm.features(ring, const.ident, xn, hT, [], self.mod, SB, CB, accum=self.sum)
        yield
        bank = ring.take(pe)
        pe.wait(*out)
        for k in range(KC):
            mm = te.matmul(bank[:, 0:1], self.g1[:, k, :], self.sum[:, k:k + 1], start=(k == 0), stop=(k == KC - 1))
        m = pe.mark(mm)
        act.wait(m)
        m = act.mark(a.activation(self.gf[:, 0:1], bank[:, 0:1], ACT.Gelu, bias=self.gb1[:, :], scale=1.0 / T))
        bank.free = [m]
        yield
        bank = ring.take(pe)
        pe.wait(m)
        m = pe.mark(te.matmul(bank[0:64, 0:1], self.g2[:, :], self.gf[:, 0:1], start=True, stop=True))
        act.wait(m)
        m = act.mark(a.activation(self.gf[0:64, 1:2], bank[0:64, 0:1], ACT.Gelu, bias=self.gb2[:, :]))
        bank.free = [m]
        yield
        bank = ring.take(pe)
        pe.wait(m)
        m = pe.mark(te.matmul(bank[:, 0:1], self.g3[:, :], self.gf[0:64, 1:2], start=True, stop=True))
        act.wait(m)
        m = act.mark(a.activation(self.gf[:, 2:3], bank[:, 0:1], ACT.Tanh, bias=self.gb3[:, :], scale=0.5))
        bank.free = [m]
        dve.wait(m)
        base = dve.mark(v.tensor_scalar(self.gf[:, 3:4], self.gf[:, 2:3], self.sar[:, 1:2], self.sar[:, 2:3], ALU.mult,
                                        ALU.add))
        yield
        sp.wait(*self.mod_next_ready())
        modn_in = self.dma["modn"].mark(sp.eng.dma_start(
            self.mod_next[:, :], d["mod1"][one, :, :].rearrange("b p n -> p (b n)")))
        csdone = []
        for cycle in range(CYCLES):
            l1 = []
            for c in range(KC):
                bank = ring.take(pe)
                pe.wait(*out)
                for k in range(KC):
                    mm = te.matmul(bank[:, :], self.w1[:, k, c * P:(c + 1) * P], hT[:, k, :], start=(k == 0),
                                   stop=(k == KC - 1))
                m = pe.mark(mm)
                act.wait(m)
                m = act.mark(a.activation(self.a1[:, c, :], bank[:, :], ACT.Gelu, bias=self.b1[:, c:c + 1]))
                bank.free = [m]
                l1.append(m)
            yield
            bank = ring.take(pe)
            pe.wait(*l1)
            for k in range(KC):
                mm = te.matmul(bank[:, :], self.w2[:, k, :], self.a1[:, k, :], start=(k == 0), stop=(k == KC - 1))
            m = pe.mark(mm)
            act.wait(m)
            m = act.mark(a.activation(self.a2[:, :], bank[:, :], ACT.Gelu, bias=self.b2[:, :]))
            bank.free = [m]
            yield
            bank = ring.take(pe)
            pe.wait(m)
            m = pe.mark(te.matmul(bank[0:64, :], self.w3[:, :], self.a2[:, :], start=True, stop=True))
            act.wait(m)
            m = act.mark(a.activation(self.a3[:, :], bank[0:64, :], ACT.Gelu, bias=self.b3[:, :]))
            bank.free = [m]
            yield
            bank = ring.take(pe)
            pe.wait(m)
            m = pe.mark(te.matmul(bank[:, :], self.w4[:, :], self.a3[:, :], start=True, stop=True))
            act.wait(m, *csdone)
            m = act.mark(a.activation(self.tf[:, :], bank[:, :], ACT.Tanh, bias=self.b4[:, :], scale=0.5))
            bank.free = [m]
            dve.wait(m, base)
            m = dve.mark(v.tensor_scalar(self.tf[:, :], self.tf[:, :], self.sar[:, 0:1], self.gf[:, 3:4], ALU.mult,
                                         ALU.add))
            dve.wait(m)
            dve.mark(v.tensor_tensor(self.a1[:, 0, :], self.tf[:, :], hT[:, 1, :], ALU.mult))
            m = dve.mark(v.tensor_tensor(self.a1[:, 1, :], self.tf[:, :], hT[:, 0, :], ALU.mult))
            csdone = [m]
            dve.wait(m)
            dve.mark(v.tensor_tensor(hT[:, 0, :], hT[:, 0, :], self.a1[:, 0, :], ALU.add))
            out = [dve.mark(v.tensor_tensor(hT[:, 1, :], hT[:, 1, :], self.a1[:, 1, :], ALU.subtract))]
            yield
            yield
        dve.wait(*out)
        for c in range(KC):
            m = dve.mark(v.tensor_scalar(hT[:, c, :], hT[:, c, :], self.mod[:, GB + c:GB + c + 1], None, ALU.mult))
        yield
        for pair in range(NT // 2):
            bank = ring.take(pe)
            pe.wait(m)
            for i in range(2):
                t = 2 * pair + i
                for c in range(KC):
                    mm = te.transpose(bank[:, i * D + c * P:i * D + (c + 1) * P], hT[:, c, t * P:(t + 1) * P],
                                      const.ident[:, :])
            md = pe.mark(mm)
            dve.wait(md)
            xt = x[:, 2 * pair:2 * pair + 2, :]
            md = dve.mark(v.tensor_tensor(xt, xt, bank[:, :].rearrange("p (i n) -> p i n", i=2), ALU.add))
            bank.free = [md]
        sp.wait(md)
        self.dma["xout"].mark(sp.eng.dma_start(d["x1"][one, :, :].rearrange("b (t p) n -> p (b t) n", p=P), x[:, :, :]))
        xn = self.norm.tokens(x, [md], [])
        yield
        yield
        act.wait(modn_in)
        self.norm.features(ring, const.ident, xn, b1.hT, [b1.last_projection], self.mod_next, SA, CA)
        yield



class Block1:
    def __init__(self, prog, sb, const, ring, d):
        self.p, self.const, self.ring, self.d = prog, const, ring, d
        self.wout = sb("wout1", [P, NHP, D])
        self.wgate = sb("wgate", [P, KC, E])
        self.x = sb("x1s", [P, NT, D])
        self.mod = sb("mod1", [P, NMOD])
        self.ga = sb("ga1", [P, D])
        self.norm = Norm(prog, sb, "n1", const.power)
        self.tmp = self.norm.xn[:, 0:2, :]
        self.oT = sb("oT1", [P, NHP, T])
        self.hTt = sb("hT1t", [P, KC, T])
        self.pr = sb("pr1", [P, NT, E])
        self.pm = sb("pm1", [P, NT, 3])
        self.prT = sb("prT1", [E, T])
        self.rows = sb("rows", [B * E, T])
        self.left = sb("left", [B * E, T])
        self.top = sb("top8", [B * E, 8])
        self.pos = sb("pos", [P, NT, B * E])
        self.attention_at = sb.at
        self.wqkv = sb("wqkv1", [P, KC, 6 * CH1])
        self.hT = sb("hT1", [P, KC, T])
        self.vc = sb("vc1", [P, NT, CH1])
        self.setup_at = sb.at
        self.f = [[sb(f"f1{i}{j}", [P, T]) for j in range(5)] for i in range(2)]
        w = P * NT * (NT + 1) // 2
        self.look = [sb(f"look{i}", [P, w]) for i in range(2)]
        self.term = [sb(f"term{i}", [P, w]) for i in range(2)]
        self.th = [sb(f"th1{i}", [P, T]) for i in range(2)]
        self.s = [sb(f"s1{i}", [P, T]) for i in range(3)]
        self.pT = [sb(f"pT1{i}", [P, T]) for i in range(2)]
        self.mx = [sb(f"mx1{i}", [P, 2]) for i in range(4)]
        self.o = [sb(f"o1{i}", [P, NT, P]) for i in range(2)]
        self.sums = [sb(f"sums{i}", [P, 2 * NT]) for i in range(2)]
        self.last_projection = self.output_projection = None
        self.dma = {n: DmaSem(prog, f"b1_{n}")
                    for n in ["x", "mod", "ga", "w", "xout", "xn", "pr", "prT", "rows", "pos"]}

    def setup(self, weights_read):
        e, d, dw = self.p.sp.eng, self.d, self.dma["w"]
        self.p.sp.wait(*weights_read)
        dw.mark(e.dma_start(self.wqkv[:, :, :], d["w_qkv1"].rearrange("(k p) n -> p k n", p=P)))
        dw.mark(e.dma_start(self.wout[:, :, :], d["w_out1"].rearrange("(k p) n -> p k n", p=P)))
        dw.mark(e.dma_start(self.wgate[:, :, :], d["w_gate"].rearrange("(k p) n -> p k n", p=P)))

    def attention(self, b):
        p, ring, const = self.p, self.ring, self.const
        pe, act, dve, pool = p.pe, p.act, p.dve, p.pool
        v, a, te = dve.eng, act.eng, pe.eng
        hT = self.hT
        self.last_projection = None
        vcdone = []
        for t in range(NT):
            bank = ring.take(pe)
            for k in range(KC):
                mm = te.matmul(bank[:, :], hT[:, k, t * P:(t + 1) * P], self.wqkv[:, k, 5 * CH1:6 * CH1],
                               start=(k == 0), stop=(k == KC - 1))
            m = pe.mark(mm)
            act.wait(m)
            m = act.mark(a.copy(self.vc[:, t, :], bank[:, :]))
            bank.free = [m]
            vcdone = [m]
            yield "V"
        SCALES = [HD1 ** -0.5, 1.0, 1.0, HD1 ** -0.5, 2.0]
        fdone, lookdone, lt_free = {}, {}, {}
        projections_free = {}

        def project(hp, j):
            bank = ring.take(pe)
            for k in range(KC):
                mm = te.matmul(bank[:, :], self.wqkv[:, k, j * CH1 + hp * P:j * CH1 + (hp + 1) * P], hT[:, k, :],
                               start=(k == 0), stop=(k == KC - 1))
            m = pe_done = pe.mark(mm)
            act.wait(m, projections_free.get(hp - 2))
            m = act.mark(a.mul(self.f[hp % 2][j][:, :], bank[:, :], SCALES[j]))
            bank.free = [m]
            fdone[hp] = m
            if (hp, j) == (NHP - 1, 4):
                self.last_projection = pe_done

        def off(j):
            return P * j * (j + 1) // 2

        def toff(j):
            return P * (j * NT - j * (j - 1) // 2)

        def lookahead(hd, j):
            rows = slice(64 * (hd % 2), 64 * (hd % 2) + 64)
            qu, ku, vu, qc, _ = self.f[hd // 2 % 2]
            look, term = self.look[hd % 2], self.term[hd % 2]
            w = (j + 1) * P
            bank = ring.take(pe)
            pe.wait(fdone[hd // 2])
            te.matmul(bank[:, 0:w], ku[rows, j * P:(j + 1) * P], qu[rows, 0:w], start=True, stop=False)
            m = pe.mark(te.matmul(bank[:, j * P:w], const.identb[:, :], const.negL[:, :], start=False, stop=True))
            act.wait(m, lt_free.get(hd - 2))
            dst = look[:, off(j):off(j) + w]
            m = act.mark(a.activation(dst, bank[:, 0:w], ACT.Tanh, scale=0.5))
            bank.free = [m]
            pool.wait(m)
            pool.mark(pool.eng.tensor_scalar(dst, dst, 0.5, 0.5, ALU.mult, ALU.add))
            bank = ring.take(pe)
            w = T - j * P
            m = pe.mark(te.matmul(bank[:, 0:w], vu[rows, j * P:(j + 1) * P], qc[rows, j * P:T], start=True, stop=True))
            dve.wait(m, lt_free.get(hd - 2))
            m = dve.mark(v.tensor_copy(term[:, toff(j):toff(j) + w], bank[:, 0:w]))
            bank.free = [m]
            pool.wait(m)
            diagonal = term[:, toff(j):toff(j) + P]
            lookdone[hd, j] = pool.mark(pool.eng.affine_select(
                out=diagonal, in_=diagonal, compare_op=ALU.is_ge, fill=0.0, base=0, pattern=[[1, P]],
                channel_multiplier=-1))

        expdone, pTdone, headdone, th_free, s_free, pT_free = {}, {}, {}, {}, {}, {}

        def scores(u):
            hd, i = u // NT, u % NT
            rows = slice(64 * (hd % 2), 64 * (hd % 2) + 64)
            _, _, _, qc, kc = self.f[hd // 2 % 2]
            look, term = self.look[hd % 2], self.term[hd % 2]
            w = (i + 1) * P
            su = ring.take(pe)
            pe.wait(lookdone[hd, i])
            for j in range(i, -1, -1):
                mm = te.matmul(su[:, 0:(j + 1) * P], term[:, toff(j) + (i - j) * P:toff(j) + (i - j + 1) * P],
                               look[:, off(j):off(j) + (j + 1) * P], start=(j == i), stop=(j == 0))
            su_done = pe.mark(mm)
            if i == NT - 1:
                lt_free[hd] = su_done
            sc = ring.take(pe)
            te.matmul(sc[:, 0:w], qc[rows, i * P:(i + 1) * P], kc[rows, 0:w], start=True, stop=False)
            sc_done = pe.mark(te.matmul(sc[:, i * P:w], const.identb[:, :], const.negS[:, :], start=False, stop=True))
            if hd % 2 and i == NT - 1:
                projections_free[hd // 2] = sc_done
            th, s, mx = self.th[u % 2], self.s[u % 3], self.mx[u % 4]
            act.wait(su_done, th_free.get(u - 2))
            m = act.mark(a.activation(th[:, 0:w], su[:, 0:w], ACT.Tanh, scale=0.5))
            dve.wait(m, su_done)
            m = dve.mark(v.scalar_tensor_tensor(out=th[:, 0:w], in0=th[:, 0:w], scalar=1.0, in1=su[:, 0:w],
                                                op0=ALU.add, op1=ALU.mult))
            su.free = [m]
            dve.wait(m, sc_done, s_free.get(u - 3))
            m = dve.mark(v.tensor_tensor_reduce(s[:, 0:w], sc[:, 0:w], th[:, 0:w], 1.0, -3e38, ALU.subtract, ALU.max,
                                                mx[:, 0:1]))
            sc.free = [m]
            th_free[u] = m
            dve.wait(m)
            m = dve.mark(v.tensor_scalar(mx[:, 1:2], mx[:, 0:1], -0.5, None, ALU.mult))
            act.wait(m, headdone.get(hd - 2))
            expdone[u] = act.mark(a.activation(s[:, 0:w], s[:, 0:w], ACT.Exp, bias=mx[:, 1:2], scale=0.5,
                                               accum_out=self.sums[hd % 2][:, i:i + 1]))

        def turn(u):
            i = u % NT
            w = (i + 1) * P
            bank = ring.take(pe)
            pe.wait(expdone[u])
            for k in range(i + 1):
                mm = te.transpose(bank[:, k * P:(k + 1) * P], self.s[u % 3][:, k * P:(k + 1) * P], const.ident[:, :])
            m = pe.mark(mm)
            s_free[u] = m
            dve.wait(m, pT_free.get(u - 2), expdone[u])
            pTdone[u] = dve.mark(v.tensor_copy(self.pT[u % 2][:, 0:w], bank[:, 0:w]))
            bank.free = [pTdone[u]]

        def attend(u):
            hd, i = u // NT, u % NT
            bank = self.out_bank
            pe.wait(pTdone[u], *vcdone)
            if i == 0:
                pe.wait(headdone.get(hd - 1))
            for k in range(i + 1):
                mm = te.matmul(bank[:, i * HD1:(i + 1) * HD1], self.pT[u % 2][:, k * P:(k + 1) * P],
                               self.vc[:, k, hd * HD1:(hd + 1) * HD1], start=(k == 0), stop=(k == i))
            m = pT_free[u] = pe.mark(mm)
            if i < NT - 1:
                return
            sums, o = self.sums[hd % 2], self.o[hd // 2 % 2]
            dve.wait(expdone[u])
            rm = dve.mark(v.reciprocal(sums[:, NT:2 * NT], sums[:, 0:NT]))
            dve.wait(m, rm, o_free.get(hd // 2 - 2))
            headdone[hd] = dve.mark(v.tensor_tensor(
                o[:, :, hd % 2 * HD1:(hd % 2 + 1) * HD1], bank[:, 0:NT * HD1].rearrange("p (t e) -> p t e", t=NT),
                sums[:, NT:2 * NT].unsqueeze(2).to_broadcast([P, NT, HD1]), ALU.mult))

        oTdone, o_free = [], {}

        def turn_out(hp, last):
            bank = ring.take(pe)
            pe.wait(last)
            for t in range(NT):
                mm = te.transpose(bank[:, t * P:(t + 1) * P], self.o[hp % 2][:, t, :], const.ident[:, :])
            m = pe.mark(mm)
            o_free[hp] = m
            act.wait(m, self.output_projection)
            oTdone.append(act.mark(a.copy(self.oT[:, hp, :], bank[:, :])))
            bank.free = [oTdone[-1]]

        for j in range(5):
            project(0, j)
            yield "P"
        for j in range(NT):
            lookahead(0, j)
            yield "L"
        nu = H1 * NT
        for u in range(nu + 3):
            hd, i = u // NT, u % NT
            if u < nu:
                scores(u)
                yield "S"
            if u < nu and hd % 2 == 0 and hd // 2 + 1 < NHP:
                for j in [[0, 1], [2], [3], [4]][i]:
                    project(hd // 2 + 1, j)
                    yield "P"
            if 0 <= u - 2 < nu:
                turn(u - 2)
                yield "T"
            if hd + 1 < H1:
                lookahead(hd + 1, i)
                yield "L"
            if u % (2 * NT) == 3 and u > 2 * NT:
                turn_out(u // (2 * NT) - 1, headdone[u // NT - 1])
            if 0 <= u - 3 < nu:
                attend(u - 3)
                yield "A"
        turn_out(NHP - 1, headdone[H1 - 1])

    def tail(self, b, ring):
        p, const, d = self.p, self.const, self.d
        pe, act, dve, sp = p.pe, p.act, p.dve, p.sp
        v, a, te = dve.eng, act.eng, pe.eng
        one = bass.ds(b, 1)
        x, hT = self.x, self.hTt
        x_in = self.dma["x"].mark(sp.eng.dma_start(
            x[:, :, :], d["x1"][one, :, :].rearrange("b (t p) n -> p (b t) n", p=P)))
        mod_in = self.dma["mod"].mark(sp.eng.dma_start(
            self.mod[:, :], d["mod1"][one, :, :].rearrange("b p n -> p (b n)")))
        ga_in = self.dma["ga"].mark(sp.eng.dma_start(
            self.ga[:, :], d["rows1"][one, 0:D].rearrange("b n -> (b n)").partition_broadcast(P)))
        yield
        xdone = []
        dve.wait(ga_in, x_in)
        for pair in range(NT // 2):
            bank = ring.take(pe)
            for i in range(2):
                t = 2 * pair + i
                for k in range(NHP):
                    mm = te.matmul(bank[:, i * D:(i + 1) * D], self.oT[:, k, t * P:(t + 1) * P], self.wout[:, k, :],
                                   start=(k == 0), stop=(k == NHP - 1))
            m = pe.mark(mm)
            self.output_projection = m
            dve.wait(m, *xdone)
            m = dve.mark(v.tensor_tensor(self.tmp, bank[:, :].rearrange("p (i n) -> p i n", i=2),
                                         self.ga[:, :].unsqueeze(1).to_broadcast([P, 2, D]), ALU.mult))
            bank.free = [m]
            dve.wait(m)
            xt = x[:, 2 * pair:2 * pair + 2, :]
            xdone = [dve.mark(v.tensor_tensor(xt, xt, self.tmp, ALU.add))]
            yield
        sp.wait(*xdone)
        self.dma["xout"].mark(sp.eng.dma_start(d["x2"][one, :, :].rearrange("b (t p) n -> p (b t) n", p=P), x[:, :, :]))
        xn = self.norm.tokens(x, xdone, [])
        sp.wait(*xn)
        self.dma["xn"].mark(sp.eng.dma_start(d["xn"][one, :, :].rearrange("b (t p) n -> p (b t) n", p=P),
                                             self.norm.xn[:, :, :]))
        yield
        yield
        act.wait(mod_in)
        h = self.norm.features(ring, const.ident, xn, hT, [], self.mod, SB, CB)
        yield
        bank = ring.take(pe)
        pe.wait(*h)
        for t in range(NT):
            for k in range(KC):
                mm = te.matmul(bank[:, t * E:(t + 1) * E], hT[:, k, t * P:(t + 1) * P], self.wgate[:, k, :],
                               start=(k == 0), stop=(k == KC - 1))
        m = pe.mark(mm)
        pr, pm = self.pr, self.pm
        view = bank[:, 0:NT * E].rearrange("p (t e) -> p t e", e=E)
        dve.wait(m)
        m = dve.mark(v.tensor_reduce(pm[:, :, 0], view, AX.X, ALU.max))
        dve.wait(m)
        m = dve.mark(v.tensor_tensor(pr[:, :, :], view, pm[:, :, 0:1].to_broadcast([P, NT, E]), ALU.subtract))
        bank.free = [m]
        act.wait(m)
        m = act.mark(a.activation(pr[:, :, :], pr[:, :, :], ACT.Exp))
        yield
        dve.wait(m)
        m = dve.mark(v.tensor_reduce(pm[:, :, 1], pr[:, :, :], AX.X, ALU.add))
        dve.wait(m)
        m = dve.mark(v.reciprocal(pm[:, :, 2], pm[:, :, 1]))
        dve.wait(m)
        m = dve.mark(v.tensor_tensor(pr[:, :, :], pr[:, :, :], pm[:, :, 2:3].to_broadcast([P, NT, E]), ALU.mult))
        sp.wait(m)
        self.dma["pr"].mark(sp.eng.dma_start(d["pr"][one, :, :].rearrange("b p n -> p (b n)"),
                                             pr[:, :, :].rearrange("p t e -> p (t e)")))
        bank = ring.take(pe)
        pe.wait(m)
        for t in range(NT):
            mm = te.transpose(bank[0:E, t * P:(t + 1) * P], pr[:, t, :], const.ident[:, :])
        m = pe.mark(mm)
        dve.wait(m)
        m = dve.mark(v.tensor_copy(self.prT[:, :], bank[0:E, :]))
        bank.free = [m]
        sp.wait(m)
        self.prT_out = self.dma["prT"].mark(sp.eng.dma_start(d["prT"][one, :, :].rearrange("b e t -> (b e) t"),
                                                             self.prT[:, :]))
        yield

    def choose(self, b0, nb, ring, stored=None):
        p, const, d = self.p, self.const, self.d
        pe, dve, sp = p.pe, p.dve, p.sp
        v, te = dve.eng, pe.eng
        n = nb * E
        rows, left = self.rows[0:n, :], self.left[0:n, :]
        if stored:
            sp.wait(stored())
        m = self.dma["rows"].mark(sp.eng.dma_start(rows, d["prT"][b0:b0 + nb, :, :].rearrange("b e t -> (b e) t")))
        yield
        src = rows
        for i in range(CAP // 8):
            dve.wait(m)
            m = dve.mark(v.max(self.top[0:n, :], src))
            dve.wait(m)
            m = dve.mark(v.match_replace(left, self.top[0:n, :], src, -1.0))
            src = left
            yield
        dve.wait(m)
        m = dve.mark(v.tensor_scalar(left, left, 0.0, None, ALU.is_lt))
        dve.wait(m)
        m = dve.mark(v.tensor_tensor_scan(rows, left, left, 0.0, ALU.add, ALU.max))
        dve.wait(m)
        m = dve.mark(v.tensor_tensor(rows, rows, left, ALU.mult))
        dve.wait(m)
        m = dve.mark(v.tensor_scalar(rows, rows, -1.0, None, ALU.add))
        yield
        bank = ring.take(pe)
        pe.wait(m)
        for t in range(NT):
            mm = te.transpose(bank[:, t * n:(t + 1) * n], self.rows[0:n, t * P:(t + 1) * P], const.ident[0:n, 0:n])
        m = pe.mark(mm)
        dve.wait(m)
        m = dve.mark(v.tensor_copy(self.pos[:, :, 0:n], bank[:, 0:NT * n].rearrange("p (t n) -> p t n", t=NT)))
        bank.free = [m]
        sp.wait(m)
        for b in range(nb):
            self.dma["pos"].mark(sp.eng.dma_start(d["pos"][b0 + b, :, :].rearrange("p (t e) -> p t e", e=E),
                                                  self.pos[:, :, b * E:(b + 1) * E]))
        yield



class Experts:
    def __init__(self, prog, const, banks, d, early, late):
        self.p, self.const, self.d = prog, const, d
        self.accs = [banks[0:2], banks[2:4]]
        self.ring = Ring(banks[4:])
        self.w1, self.w2 = [], []
        self.n_early = (early.end - early.at) // (4 * (KC * F + FC * D))
        for e in range(E):
            sb = early if e < self.n_early else late
            self.w1.append(sb(f"ew1{e}", [P, KC, F]))
            self.w2.append(sb(f"ew2{e}", [P, FC, D]))
        self.wsem = [prog.nc.alloc_semaphore(f"expert{e}_in") for e in range(E)]
        sb = late
        self.data = [{
            "mod": place(f"mode{i}", [P, NMOD]),
            "gb": early(f"gbe{i}", [P, D]),
            "pr": place(f"prb{i}", [P, NT, E]),
            "pos": place(f"posb{i}", [P, NT, E]),
            "tokens": place(f"tokens{i}", [P, 3, NT, D], BF16),
            "probs": place(f"probs{i}", [P, 3, NT, E], BF16),
        } for i, place in enumerate((early, late))]
        self.stage = early("stage", [P, NT, D])
        self.x = sb("xe", [P, NT, D])
        self.pick = [sb(f"pick{i}", [P, NT, P], BF16) for i in range(2)]
        self.gate = [sb(f"gate{i}", [P, 1]) for i in range(2)]
        self.spread = [sb(f"spread{i}", [P, T], BF16) for i in range(2)]
        self.h2parts = [sb(f"h2p{i}", [P, 3, D], BF16) for i in range(2)]
        self.xin = [sb(f"xin{i}", [P, KC, P]) for i in range(2)]
        self.h1 = [sb(f"h1{i}", [P, FC, P]) for i in range(2)]
        self.h2 = [place(f"h2{i}", [P, D]) for i, place in enumerate((early, late))]
        self.dma = [{n: DmaSem(prog, f"e{i}_{n}") for n in ["x", "xn", "mod", "gb", "pr", "pos", "out"]}
                    for i in range(2)]

    def load_weights(self, experts):
        for e in experts:
            for w, name in ((self.w1[e], "L1_ffn_w1"), (self.w2[e], "L1_ffn_w2")):
                self.p.sp.eng.dma_start(w[:, :, :], self.d[name][e].rearrange("(k p) n -> p k n", p=P)
                                        ).then_inc(self.wsem[e], 16)

    def load(self, i, b, names):
        d, t, eng, one = self.d, self.data[i], self.p.sp.eng, bass.ds(b, 1)
        places = {
            "pos": (t["pos"][:, :, :].rearrange("p t e -> p (t e)"),
                    d["pos"][one, :, :].rearrange("b p n -> p (b n)")),
            "xn": (self.stage[:, :, :], d["xn"][one, :, :].rearrange("b (t p) n -> p (b t) n", p=P)),
            "pr": (t["pr"][:, :, :].rearrange("p t e -> p (t e)"), d["pr"][one, :, :].rearrange("b p n -> p (b n)")),
            "mod": (t["mod"][:, :], d["mod1"][one, :, :].rearrange("b p n -> p (b n)")),
            "x": (self.x[:, :, :], d["x2"][one, :, :].rearrange("b (t p) n -> p (b t) n", p=P)),
            "gb": (t["gb"][:, :], d["rows1"][one, D:2 * D].rearrange("b n -> (b n)").partition_broadcast(P)),
        }
        return {n: self.dma[i][n].mark(eng.dma_start(*places[n])) for n in names}

    def split(self, i, marks, *free):
        t, dve = self.data[i], self.p.dve
        v = dve.eng
        dve.wait(marks["xn"], marks["pr"], *free)
        for parts, rest in ((t["tokens"], self.stage), (t["probs"], t["pr"])):
            for k in range(2):
                m = dve.mark(v.tensor_copy(parts[:, k, :, :], rest[:, :, :]))
                dve.wait(m)
                out = parts[:, 2, :, :] if k else rest[:, :, :]
                m = dve.mark(v.tensor_tensor(out, rest[:, :, :], parts[:, k, :, :], ALU.subtract))
                dve.wait(m)
        return m

    def first_tokens(self):
        marks = self.load(0, 0, ["xn", "pr", "mod"])
        for _ in range(4):
            yield
        self.split(0, marks)
        yield

    def two_batches(self, b0, first=False, last=False):
        p, const, d = self.p, self.const, self.d
        pe, act, dve, sp, pool = p.pe, p.act, p.dve, p.sp, p.pool
        v, a, te, g = dve.eng, act.eng, pe.eng, pool.eng
        accs, ring = self.accs, self.ring
        loaded = [{}, {}]
        split_done = [None, None]
        gathered, picked, turned, xindone, gatedone, spreaddone = {}, {}, {}, {}, {}, {}
        h1done, h2done, partsdone, ffn1, ffn2, scattered = {}, {}, {}, {}, {}, {}

        loaded[0] = self.load(0, b0, ["pos"] if first else [])
        loaded[1] = self.load(1, b0 + 1, EARLY)
        loaded[0].update(self.load(0, b0, ["x", "gb"]))
        loaded[1].update(self.load(1, b0 + 1, ["gb"]))

        def pick(u):
            i, e = u // E, u % E
            dve.wait(loaded[i].get("pos"), turned.get(u - 2))
            for t in range(NT):
                picked[u] = dve.mark(v.tensor_scalar(self.pick[u % 2][:, t, :], const.iota[:, :],
                                                     self.data[i]["pos"][:, t, e:e + 1], None, ALU.is_equal))

        def gather(u):
            i, e = u // E, u % E
            t_ = self.data[i]
            bank = ring.take(pe)
            pe.wait(picked[u], split_done[i])
            for c in range(KC):
                for t in range(NT):
                    for k in range(3):
                        te.matmul(bank[:, c * P:(c + 1) * P], t_["tokens"][:, k, t, c * P:(c + 1) * P],
                                  self.pick[u % 2][:, t, :], start=(t == 0 and k == 0), stop=(t == NT - 1 and k == 2))
            for t in range(NT):
                mm = te.matmul(bank[:, D:D + 3], self.pick[u % 2][:, t, :], t_["probs"][:, :, t, e], start=(t == 0),
                               stop=(t == NT - 1))
            m = gathered[u] = pe.mark(mm)
            dve.wait(m, loaded[i].get("mod"), ffn1.get(u - 2))
            for c in range(KC):
                m = dve.mark(v.tensor_scalar(self.xin[u % 2][:, c, :], bank[:, c * P:(c + 1) * P],
                                             t_["mod"][:, CB + c:CB + c + 1], t_["mod"][:, SB + c:SB + c + 1],
                                             ALU.mult, ALU.add))
            xindone[u] = m
            dve.wait(h2done.get(u - 2))
            gatedone[u] = dve.mark(v.tensor_reduce(self.gate[u % 2][:, :], bank[:, D:D + 3], AX.X, ALU.add))
            bank.free = [gatedone[u]]

        def turn(u):
            bank = ring.take(pe)
            pe.wait(picked[u])
            for t in range(NT):
                mm = te.matmul(bank[:, t * P:(t + 1) * P], self.pick[u % 2][:, t, :], const.identb[:, :], start=True,
                               stop=True)
            m = turned[u] = pe.mark(mm)
            dve.wait(m, scattered.get(u - 2))
            spreaddone[u] = dve.mark(v.tensor_copy(self.spread[u % 2][:, :], bank[:, :]))
            bank.free = [spreaddone[u]]

        def hidden(u):
            e = u % E
            if u < E:
                te.wait_ge(self.wsem[e], 32)
            for half in range(2):
                bank = ring.take(pe)
                pe.wait(xindone[u])
                for i in range(FC // 2):
                    f = half * (FC // 2) + i
                    for k in range(KC):
                        mm = te.matmul(bank[:, i * P:(i + 1) * P], self.w1[e][:, k, f * P:(f + 1) * P],
                                       self.xin[u % 2][:, k, :], start=(k == 0), stop=(k == KC - 1))
                m = ffn1[u] = pe.mark(mm)
                act.wait(m, ffn2.get(u - 2))
                h1done[u, half] = act.mark(a.activation(
                    self.h1[u % 2][:, half * (FC // 2):(half + 1) * (FC // 2), :],
                    bank[:, :].rearrange("p (f s) -> p f s", s=P), ACT.Gelu))
                bank.free = [h1done[u, half]]

        def output(u):
            bank = ring.take(pe)
            for f in range(FC):
                pe.wait(h1done[u, f // (FC // 2)])
                mm = te.matmul(bank[:, 0:D], self.h1[u % 2][:, f, :], self.w2[u % E][:, f, :], start=(f == 0),
                               stop=(f == FC - 1))
            m = ffn2[u] = pe.mark(mm)
            act.wait(m, gatedone[u], partsdone.get(u - 2))
            h2done[u] = act.mark(a.activation(self.h2[u % 2][:, :], bank[:, 0:D], ACT.Copy,
                                              scale=self.gate[u % 2][:, 0:1]))
            bank.free = [h2done[u]]
            h2, parts = self.h2[u % 2], self.h2parts[u % 2]
            line = dve if u == 2 * E - 1 else pool
            line.wait(h2done[u], scattered.get(u - 2))
            for k in range(2):
                m = line.mark(line.eng.tensor_copy(parts[:, k, :], h2[:, :]))
                line.wait(m)
                m = line.mark(line.eng.tensor_tensor(parts[:, 2, :] if k else h2[:, :], h2[:, :], parts[:, k, :],
                                                     ALU.subtract))
                line.wait(m)
            partsdone[u] = m

        def scatter(u):
            i, e = u // E, u % E
            acc = accs[i]
            pe.wait(partsdone[u], spreaddone[u])
            for t in range(NT):
                for k in range(3):
                    mm = te.matmul(acc[t // 2][:, t % 2 * D:(t % 2 + 1) * D], self.spread[u % 2][:, t * P:(t + 1) * P],
                                   self.h2parts[u % 2][:, k, :], start=(e == 0 and t % 2 == 0 and k == 0),
                                   stop=(e == E - 1 and t % 2 == 1 and k == 2), skip_group_check=True)
            scattered[u] = pe.mark(mm)
            if e < E - 1:
                return
            marks, x, temp = loaded[i], self.x, self.stage
            dve.wait(scattered[u], marks["gb"], marks["x"], *split_done)
            gb = self.data[i]["gb"][:, :].unsqueeze(1).to_broadcast([P, 2, D])
            for j in range(2):
                m = dve.mark(v.tensor_tensor(temp[:, 2 * j:2 * j + 2, :],
                                             acc[j][:, :].rearrange("p (i n) -> p i n", i=2), gb, ALU.mult))
            dve.wait(m)
            m = dve.mark(v.tensor_tensor(x[:, :, :], x[:, :, :], temp[:, :, :], ALU.add))
            sp.wait(m)
            out = self.dma[i]["out"].mark(sp.eng.dma_start(
                d["out"][bass.ds(b0 + i, 1), :, :].rearrange("b (t p) n -> p (b t) n", p=P), x[:, :, :]))
            if i == 0:
                if not last:
                    ahead.update(self.load(0, b0 + 2, EARLY))
                sp.wait(out)
                loaded[1].update(self.load(1, b0 + 1, ["x"]))

        ahead = {}
        n = 2 * E
        pick(0)
        yield "M"
        if first:
            self.load_weights(range(self.n_early, E))
        gather(0)
        turn(0)
        pick(1)
        yield "M"
        for u in range(n):
            hidden(u)
            yield "M"
            if u == 2:
                split_done[1] = self.split(1, loaded[1])
            if u == E + 2 and ahead:
                split_done[0] = self.split(0, ahead, gathered[E - 1])
            if u + 1 < n:
                gather(u + 1)
            yield "M"
            if u > 0:
                scatter(u - 1)
            if u + 1 < n:
                turn(u + 1)
            if u + 2 < n:
                pick(u + 2)
            yield "M"
            output(u)
            yield "M"
        scatter(n - 1)



def program(nc, d):
    prog = Program(nc)
    for name, shape in [("mod0", [B, P, NMOD]), ("mod1", [B, P, NMOD]), ("rows0", [B, D]), ("rows1", [B, 2 * D]),
                        ("x1", [B, T, D]), ("x2", [B, T, D]), ("xn", [B, T, D]), ("pr", [B, P, NT * E]),
                        ("prT", [B, E, T]),
                        ("pos", [B, P, NT * E])]:
        d[name] = nc.dram_tensor(name + "_scratch", shape, F32, kind="Internal").ap()

    banks = [Bank(nc, f"bank{i}") for i in range(8)]
    end = nc.sbuf_usable_end
    low = Arena(nc, nc.sbuf_base, end)
    const = Constants(prog, low)
    shared = low.at
    b1 = Block1(prog, low, const, Ring(banks[3:8]), d)
    b1.out_bank = banks[2]
    middle = low.at
    b0 = Block0(prog, low, const, Ring(banks[0:3]), d)
    setup_sb = Arena(nc, b1.setup_at, middle)
    half = b1.wqkv[:, :, 0:6 * D], b1.wqkv[:, :, 6 * D:12 * D]
    ring = Ring(banks[3:8])
    mod0, mod1 = {}, {}
    modulation0 = modulation(prog, ring, setup_sb, 0, half[0], d["cT0"], d["L0_wmod"], d["mod0"], d["rows0"], [GA],
                             mod0)
    modulation1 = modulation(prog, ring, setup_sb, 1, half[1], d["cT1"], d["L1_wmod"], d["mod1"], d["rows1"],
                             [GA, GB], mod1)
    first = b0.batch(0, b1, mod0)
    for line in prog.lines:
        line.wait(*const.ready)
    next(modulation0)
    next(first)
    next(modulation1)
    next(modulation0)
    loaded = b0.load_weights()
    next(first)
    next(first)
    for _ in modulation0:
        pass
    b0.mod_ready, b0.mod_next_ready = mod0["out"], lambda: mod1["out"]
    ready = b0.setup(loaded)
    for line in prog.lines:
        line.wait(*ready)

    def second():
        yield from modulation1
        b1.setup([mod0["read"], mod1["read"]])

    second_part = second()
    for n, _ in enumerate(first):
        if n >= 3:
            next(second_part, None)
    prog.meet()
    b0.ring = Ring(banks[0:2])
    interleave(b1.attention(0), NATT, (b0.batch(1, b1), N0, SPREAD0, BESIDE0))
    prog.meet()
    with nc.Fori(1, B - 1) as i:
        interleave(b1.attention(i), NATT, (b0.batch(i + 1, b1), N0, SPREAD0, BESIDE0),
                   (b1.tail(i - 1, b1.ring), NTAIL, SPREAD_TAIL, BESIDE_TAIL))
        prog.meet()
    ex = Experts(prog, const, banks, d, Arena(nc, middle, end), Arena(nc, b1.attention_at, middle))
    tail = b1.tail(B - 2, b1.ring)
    next(tail)
    first_tokens = ex.first_tokens()
    next(first_tokens)
    ex.load_weights(range(ex.n_early))
    interleave(b1.attention(B - 1), NATT, (tail, NTAIL - 1, SPREAD_TAIL, BESIDE_TAIL),
               (first_tokens, 4, SPREAD_FIRST, BESIDE_TAIL),
               (b1.choose(0, B - 2, b1.ring), NCHOOSE, SPREAD_CHOOSE, BESIDE_TAIL))
    prog.meet()

    def last_choice():
        yield from b1.tail(B - 1, ex.ring)
        yield from b1.choose(B - 2, 2, ex.ring, lambda: b1.prT_out)

    interleave(ex.two_batches(0, True), NMOE, (last_choice(), NTAIL + NCHOOSE, SPREAD_LAST, "M"))
    prog.meet()
    with nc.Fori(1, B // 2 - 1) as i:
        for _ in ex.two_batches(2 * i):
            pass
        prog.meet()
    for _ in ex.two_batches(B - 2, last=True):
        pass
    prog.meet()
    for s in ex.wsem:
        nc.sync.wait_ge(s, 32)


_DIRECT = ["L0_attn_x", "L0_attn_b_qkv", "L0_attn_b_out", "L0_ffn_cn_w1", "L0_ffn_cn_b1", "L0_ffn_cn_w2",
           "L0_ffn_cn_b2", "L0_ffn_cn_w3", "L0_ffn_cn_b3", "L0_ffn_cn_w4", "L0_ffn_cn_b4", "L0_ffn_gc_w1",
           "L0_ffn_gc_b1", "L0_ffn_gc_w2", "L0_ffn_gc_b2", "L0_ffn_gc_w3", "L0_ffn_gc_b3", "L0_ffn_adaptive_range",
           "L0_wmod", "L1_ffn_w1", "L1_ffn_w2", "L1_wmod"]
_TURNED = {"w_qkv0": "L0_attn_W_qkv", "w_out0": "L0_attn_W_out", "w_qkv1": "L1_attn_W_qkv", "w_out1": "L1_attn_W_out",
           "w_gate": "L1_ffn_gate_w", "cT0": "L0_c", "cT1": "L1_c"}


def kernel(**inputs):
    import numpy as np
    import concourse.bacc as bacc
    from concourse.bass_utils import run_bass_kernel_spmd

    nc = bacc.Bacc("TRN2", target_bir_lowering=False, num_devices=1)
    arrays = {n: np.ascontiguousarray(inputs[n]) for n in _DIRECT}
    arrays.update({n: np.ascontiguousarray(np.asarray(inputs[m]).T) for n, m in _TURNED.items()})
    d = {n: nc.dram_tensor(n, x.shape, F32, kind="ExternalInput").ap() for n, x in arrays.items()}
    d["out"] = nc.dram_tensor("out", (B, T, D), F32, kind="ExternalOutput").ap()
    program(nc, d)
    r = run_bass_kernel_spmd(nc, [arrays], core_ids=[0])
    return r.results[0]["out"]
```
